# Optimizing a Trainium2 kernel written in Bass

```python
import numpy as np
import jax
import jax.numpy as jnp

def _softmax(x, axis=-1):
    return jax.nn.softmax(x, axis=axis)

def _gelu(x):
    return jax.nn.gelu(x, approximate=True)

def _silu(x):
    return jax.nn.silu(x)

def _sigmoid(x):
    return jax.nn.sigmoid(x)

def _layernorm(x, axis=-1, eps=1e-05):
    m = jnp.mean(x, axis=axis, keepdims=True)
    v = jnp.var(x, axis=axis, keepdims=True)
    return (x - m) / jnp.sqrt(v + eps)

def _scatter_add(tgt, idx, src, axis=0):
    return tgt.at[idx].add(src)

def _segment_sum(src, seg, n):
    return jax.ops.segment_sum(src, seg, n)
kernel_name = 'mk_perceiver_d1_seqx_r2_679ff5'

def setup_inputs(seed: int=0):
    np.random.seed(seed)
    _w = jnp.asarray

    def _rec_inputs():
        import jax
        import jax.numpy as jnp
        _rk = jax.random.key(seed)
        x = -0.0002928 + 1 * jax.random.normal(jax.random.fold_in(_rk, 1), (16, 64, 512), jnp.float32)
        _lenS = 64 - jax.random.randint(jax.random.fold_in(_rk, 7), (16,), 0, max(1, 64 // 4) + 1, jnp.int32)
        _lenS2 = 1601 - jax.random.randint(jax.random.fold_in(_rk, 8), (16,), 0, max(1, 1601 // 4) + 1, jnp.int32)
        _ctx_1024P = jax.random.normal(jax.random.fold_in(_rk, 11), (16, 16, 512), jnp.float32)
        _ctx_1024c = jax.random.dirichlet(jax.random.fold_in(_rk, 511), 0.3 * jnp.ones((16,), jnp.float32), (16, 1601))
        _ctx_1024t = jnp.einsum('bsk,bkd->bsd', _ctx_1024c, _ctx_1024P)
        _ctx_1024t = _ctx_1024t * jax.lax.rsqrt(jnp.mean(jnp.square(_ctx_1024t)) + 1e-12) * 0.953939
        ctx_1024 = -1.39393e-06 + 0.999914 * (_ctx_1024t + 0.3 * jax.random.normal(jax.random.fold_in(_rk, 611), (16, 1601, 512), jnp.float32))
        return (x, ctx_1024)
    x, ctx_1024 = _rec_inputs()

    def _L0_xattn_setup():
        import jax, jax.numpy as jnp
        import numpy as np
        D_MODEL = 512
        N_HEAD = 16
        D_HEAD = D_MODEL // N_HEAD
        key = jax.random.key(seed)
        ks = jax.random.split(key, 6)
        B, L, M = (2, 1024, 1024)
        q = jax.random.normal(ks[0], (B, L, D_MODEL), dtype=jnp.float32)
        kv = jax.random.normal(ks[1], (B, L, D_MODEL), dtype=jnp.float32)
        mem = jax.random.normal(ks[2], (B, M, D_MODEL), dtype=jnp.float32)
        s = 1.0 / np.sqrt(D_MODEL)
        w_q = jax.random.normal(ks[3], (D_MODEL, D_MODEL), dtype=jnp.float32) * s
        w_kv = jax.random.normal(ks[4], (D_MODEL, 2 * D_HEAD), dtype=jnp.float32) * s
        w_concat = jax.random.normal(ks[5], (D_MODEL, D_MODEL), dtype=jnp.float32) * s
        return {'q': q, 'kv': kv, 'mem': mem, 'w_q': w_q, 'w_kv': w_kv, 'w_concat': w_concat}
    _L0_xattn_all = _L0_xattn_setup()
    _L0_xattn_in = {k: v for k, v in _L0_xattn_all.items() if k in ('w_q', 'w_kv', 'w_concat')}
    del _L0_xattn_all

    def _L0_attn_setup():
        import jax, jax.numpy as jnp
        import numpy as np
        B, T, D_MODEL = (2, 256, 512)
        D_INNER, D_HEAD, D_CONV = (1024, 64, 4)
        N_HEADS, D_STATE = (32, 32)
        DT_MIN, DT_MAX, K_MAX, EPS = (0.0001, 0.1, 0.5, 1e-08)

        def _forward(x, W_in, dw_weight, dw_bias, W_bc, W_out, skip, A_log, dt_bias):
            Bsz, Tlen, D = x.shape
            DI, K = dw_weight.shape
            H, N = A_log.shape
            DH = DI // H
            proj = jnp.einsum('btd,od->bto', x, W_in)
            gate = proj[..., :DI]
            value_raw = proj[..., DI:2 * DI]
            params = proj[..., 2 * DI:].reshape(Bsz, Tlen, H, 2)
            xp = jnp.pad(value_raw, ((0, 0), (K - 1, 0), (0, 0)))
            conv = dw_bias + sum((xp[:, k:k + Tlen, :] * dw_weight[:, k] for k in range(K)))
            value = jax.nn.silu(conv)
            dt = jnp.clip(jax.nn.softplus(params[..., 0] + dt_bias), DT_MIN, DT_MAX)
            kd = K_MAX * jax.nn.sigmoid(params[..., 1])
            A = jnp.exp(A_log)
            bc = jnp.einsum('bti,oi->bto', value, W_bc).reshape(Bsz, Tlen, H, 4, N)
            bc = bc / (jnp.sqrt(jnp.sum(bc * bc, axis=-1, keepdims=True)) + EPS)
            Bz, Bx, Cz, Cx = (bc[..., 0, :], bc[..., 1, :], bc[..., 2, :], bc[..., 3, :])
            u = value.reshape(Bsz, Tlen, H, DH)

            def step(carry, inp):
                z, s = carry
                u_t, dt_t, k_t, Bz_t, Bx_t, Cz_t, Cx_t = inp
                dtE = dt_t[:, :, None, None]
                S = 1.0 / (1.0 + dt_t[..., None] * k_t[..., None] + (dt_t * dt_t)[..., None] * A)
                z = S[..., None] * (z - dtE * A[None, :, :, None] * s + dtE * (Bz_t[..., None] * u_t[:, :, None, :]))
                s = s + dtE * z + dtE * (Bx_t[..., None] * u_t[:, :, None, :])
                y = jnp.einsum('bhn,bhnd->bhd', Cz_t, z) + jnp.einsum('bhn,bhnd->bhd', Cx_t, s)
                return ((z, s), y)
            tm = lambda a: jnp.moveaxis(a, 1, 0)
            init = (jnp.zeros((Bsz, H, N, DH), x.dtype), jnp.zeros((Bsz, H, N, DH), x.dtype))
            _, ys = jax.lax.scan(step, init, (tm(u), tm(dt), tm(kd), tm(Bz), tm(Bx), tm(Cz), tm(Cx)))
            y = jnp.moveaxis(ys, 0, 1).reshape(Bsz, Tlen, DI)
            y = (y + skip * value) * jax.nn.silu(gate)
            return jnp.einsum('bti,oi->bto', y, W_out)
        key = jax.random.key(seed)
        ks = jax.random.split(key, 8)
        n = lambda k, sh, s=1.0: jax.random.normal(k, sh, jnp.float32) * s
        return {'x': n(ks[0], (B, T, D_MODEL)), 'W_in': n(ks[1], (2 * D_INNER + N_HEADS * 2, D_MODEL), D_MODEL ** (-0.5)), 'dw_weight': n(ks[2], (D_INNER, D_CONV), D_CONV ** (-0.5)), 'dw_bias': n(ks[3], (D_INNER,), 0.1), 'W_bc': n(ks[4], (N_HEADS * 4 * D_STATE, D_INNER), D_INNER ** (-0.5)), 'W_out': n(ks[5], (D_MODEL, D_INNER), D_INNER ** (-0.5)), 'skip': jnp.ones((D_INNER,), jnp.float32), 'A_log': n(ks[6], (N_HEADS, D_STATE), 0.5), 'dt_bias': n(ks[7], (N_HEADS,), 0.5)}
    _L0_attn_all = _L0_attn_setup()
    _L0_attn_in = {k: v for k, v in _L0_attn_all.items() if k in ('W_in', 'dw_weight', 'dw_bias', 'W_bc', 'W_out', 'skip', 'A_log', 'dt_bias')}
    del _L0_attn_all

    def _L0_ffn_setup():
        import jax, jax.numpy as jnp
        import numpy as np
        IN_DIM, OUT_DIM, N_PROTO, RANK = (512, 512, 32, 16)
        key = jax.random.key(seed)
        ks = jax.random.split(key, 5)
        x = jax.random.normal(ks[0], (2, 2048, IN_DIM), dtype=jnp.float32)
        prototypes = jax.random.normal(ks[1], (N_PROTO, IN_DIM), dtype=jnp.float32) * 0.02
        B = jax.random.normal(ks[2], (N_PROTO, RANK, IN_DIM), dtype=jnp.float32) * 0.02
        A = jax.random.normal(ks[3], (N_PROTO, OUT_DIM, RANK), dtype=jnp.float32) * 0.02
        bias = jnp.zeros((N_PROTO, OUT_DIM), dtype=jnp.float32)
        temp = jnp.asarray(1.0, dtype=jnp.float32)
        return {'x': x, 'prototypes': prototypes, 'B': B, 'A': A, 'bias': bias, 'temp': temp}
    _L0_ffn_all = _L0_ffn_setup()
    _L0_ffn_in = {k: v for k, v in _L0_ffn_all.items() if k in ('prototypes', 'B', 'A', 'bias', 'temp')}
    del _L0_ffn_all
    return {'x': x, 'ctx_1024': ctx_1024, 'L0_xattn_w_q': _L0_xattn_in['w_q'], 'L0_xattn_w_kv': _L0_xattn_in['w_kv'], 'L0_xattn_w_concat': _L0_xattn_in['w_concat'], 'L0_attn_W_in': _L0_attn_in['W_in'], 'L0_attn_dw_weight': _L0_attn_in['dw_weight'], 'L0_attn_dw_bias': _L0_attn_in['dw_bias'], 'L0_attn_W_bc': _L0_attn_in['W_bc'], 'L0_attn_W_out': _L0_attn_in['W_out'], 'L0_attn_skip': _L0_attn_in['skip'], 'L0_attn_A_log': _L0_attn_in['A_log'], 'L0_attn_dt_bias': _L0_attn_in['dt_bias'], 'L0_ffn_prototypes': _L0_ffn_in['prototypes'], 'L0_ffn_B': _L0_ffn_in['B'], 'L0_ffn_A': _L0_ffn_in['A'], 'L0_ffn_bias': _L0_ffn_in['bias'], 'L0_ffn_temp': _L0_ffn_in['temp']}

def reference(x, ctx_1024, L0_xattn_w_q, L0_xattn_w_kv, L0_xattn_w_concat, L0_attn_W_in, L0_attn_dw_weight, L0_attn_dw_bias, L0_attn_W_bc, L0_attn_W_out, L0_attn_skip, L0_attn_A_log, L0_attn_dt_bias, L0_ffn_prototypes, L0_ffn_B, L0_ffn_A, L0_ffn_bias, L0_ffn_temp):
    import jax
    import jax.numpy as jnp

    def _L0_xattn_ref(q, kv, mem, w_q, w_kv, w_concat):
        import jax, jax.numpy as jnp
        import numpy as np
        D_MODEL = 512
        N_HEAD = 16
        D_HEAD = D_MODEL // N_HEAD
        B, L, D = q.shape
        c = jnp.concatenate([mem, kv], axis=1)
        qh = (q @ w_q).reshape(B, L, N_HEAD, D_HEAD).transpose(0, 2, 1, 3)
        kvp = c @ w_kv
        k, v = (kvp[..., :D_HEAD], kvp[..., D_HEAD:])
        attn_score = jnp.einsum('bhid,bjd->bhij', qh, k) / np.sqrt(D_HEAD)
        attn_prob = jax.nn.softmax(attn_score, axis=-1)
        out = jnp.einsum('bhij,bjd->bhid', attn_prob, v)
        out = out.transpose(0, 2, 1, 3).reshape(B, L, D)
        return out @ w_concat

    def _L0_attn_ref(x, W_in, dw_weight, dw_bias, W_bc, W_out, skip, A_log, dt_bias):
        import jax, jax.numpy as jnp
        import numpy as np
        B, T, D_MODEL = (2, 256, 512)
        D_INNER, D_HEAD, D_CONV = (1024, 64, 4)
        N_HEADS, D_STATE = (32, 32)
        DT_MIN, DT_MAX, K_MAX, EPS = (0.0001, 0.1, 0.5, 1e-08)

        def _forward(x, W_in, dw_weight, dw_bias, W_bc, W_out, skip, A_log, dt_bias):
            Bsz, Tlen, D = x.shape
            DI, K = dw_weight.shape
            H, N = A_log.shape
            DH = DI // H
            proj = jnp.einsum('btd,od->bto', x, W_in)
            gate = proj[..., :DI]
            value_raw = proj[..., DI:2 * DI]
            params = proj[..., 2 * DI:].reshape(Bsz, Tlen, H, 2)
            xp = jnp.pad(value_raw, ((0, 0), (K - 1, 0), (0, 0)))
            conv = dw_bias + sum((xp[:, k:k + Tlen, :] * dw_weight[:, k] for k in range(K)))
            value = jax.nn.silu(conv)
            dt = jnp.clip(jax.nn.softplus(params[..., 0] + dt_bias), DT_MIN, DT_MAX)
            kd = K_MAX * jax.nn.sigmoid(params[..., 1])
            A = jnp.exp(A_log)
            bc = jnp.einsum('bti,oi->bto', value, W_bc).reshape(Bsz, Tlen, H, 4, N)
            bc = bc / (jnp.sqrt(jnp.sum(bc * bc, axis=-1, keepdims=True)) + EPS)
            Bz, Bx, Cz, Cx = (bc[..., 0, :], bc[..., 1, :], bc[..., 2, :], bc[..., 3, :])
            u = value.reshape(Bsz, Tlen, H, DH)

            def step(carry, inp):
                z, s = carry
                u_t, dt_t, k_t, Bz_t, Bx_t, Cz_t, Cx_t = inp
                dtE = dt_t[:, :, None, None]
                S = 1.0 / (1.0 + dt_t[..., None] * k_t[..., None] + (dt_t * dt_t)[..., None] * A)
                z = S[..., None] * (z - dtE * A[None, :, :, None] * s + dtE * (Bz_t[..., None] * u_t[:, :, None, :]))
                s = s + dtE * z + dtE * (Bx_t[..., None] * u_t[:, :, None, :])
                y = jnp.einsum('bhn,bhnd->bhd', Cz_t, z) + jnp.einsum('bhn,bhnd->bhd', Cx_t, s)
                return ((z, s), y)
            tm = lambda a: jnp.moveaxis(a, 1, 0)
            init = (jnp.zeros((Bsz, H, N, DH), x.dtype), jnp.zeros((Bsz, H, N, DH), x.dtype))
            _, ys = jax.lax.scan(step, init, (tm(u), tm(dt), tm(kd), tm(Bz), tm(Bx), tm(Cz), tm(Cx)))
            y = jnp.moveaxis(ys, 0, 1).reshape(Bsz, Tlen, DI)
            y = (y + skip * value) * jax.nn.silu(gate)
            return jnp.einsum('bti,oi->bto', y, W_out)
        return _forward(x, W_in, dw_weight, dw_bias, W_bc, W_out, skip, A_log, dt_bias)

    def _L0_ffn_ref(x, prototypes, B, A, bias, temp):
        import jax, jax.numpy as jnp
        import numpy as np
        IN_DIM, OUT_DIM, N_PROTO, RANK = (512, 512, 32, 16)
        lead = x.shape[:-1]
        xf = x.reshape(-1, IN_DIM)
        x2 = jnp.sum(xf * xf, axis=1, keepdims=True)
        p2 = jnp.sum(prototypes * prototypes, axis=1)
        d2 = x2 + p2[None, :] - 2.0 * (xf @ prototypes.T)
        dists = jnp.sqrt(jnp.maximum(d2, 0.0))
        t = jnp.maximum(jnp.abs(temp), 0.1)
        w = jax.nn.softmax(-dists / t, axis=1)
        topw, topi = jax.lax.top_k(w, 2)
        topw = topw / jnp.sum(topw, axis=1, keepdims=True)
        out = jnp.zeros((xf.shape[0], OUT_DIM), dtype=xf.dtype)
        for tslot in range(2):
            idx = topi[:, tslot]
            wt = topw[:, tslot:tslot + 1]
            h = jnp.einsum('nri,ni->nr', B[idx], xf)
            y = jnp.einsum('nor,nr->no', A[idx], h) + bias[idx]
            out = out + wt * y
        return out.reshape(*lead, OUT_DIM)
    x = x + _L0_xattn_ref(_layernorm(x, axis=-1), ctx_1024, ctx_1024, L0_xattn_w_q, L0_xattn_w_kv, L0_xattn_w_concat)
    x = x + _L0_attn_ref(_layernorm(x, axis=-1), L0_attn_W_in, L0_attn_dw_weight, L0_attn_dw_bias, L0_attn_W_bc, L0_attn_W_out, L0_attn_skip, L0_attn_A_log, L0_attn_dt_bias)
    x = x + _L0_ffn_ref(_layernorm(x, axis=-1), L0_ffn_prototypes, L0_ffn_B, L0_ffn_A, L0_ffn_bias, L0_ffn_temp)
    return x

_drawn_inputs = setup_inputs


def setup_inputs(seed=0):
    import zlib

    import numpy as np

    out = dict(_drawn_inputs(seed))
    spreads = {'L0_attn_skip': (1.0, 0.2), 'L0_ffn_bias': (0.0, 0.1)}
    factors = {'L0_attn_dt_bias': 8.0, 'L0_ffn_B': 2.807, 'L0_ffn_A': 2.798}
    for name, (base, spread) in spreads.items():
        noise = np.random.default_rng([zlib.crc32(name.encode()), seed]).standard_normal(out[name].shape)
        drawn = base * np.exp(spread * noise) if base else spread * noise
        out[name] = jnp.asarray(drawn.astype(out[name].dtype))
    for name, factor in factors.items():
        out[name] = (out[name] * factor).astype(out[name].dtype)
    return out
```

```python
import numpy as np
import concourse.bass as bass
from concourse import mybir
from contextlib import ExitStack

F32 = mybir.dt.float32
F16 = mybir.dt.float16
U32 = mybir.dt.uint32
ALU = mybir.AluOpType
ACT = mybir.ActivationFunctionType
AX = mybir.AxisListType

P = 128
B, T, D = 16, 64, 512
TOK = B * T
NKEY = 1601
H, DH = 16, 32
DC = D // P
KT = -(-NKEY // P)
BLK = [(0, 401)] + [(401 + 400 * i, 400) for i in range(3)]
DI, SH, SN = 1024, 32, 32
VC = DI // P
NG = 8
HT = TOK // 2
HB = B // 2
NP, RK = 32, 16
XS, WS = 16.0, 256.0
UNS = 1.0 / (XS * WS)
MS = 256.0
SC = 1.0 / (XS * XS * DH ** 0.5)
EPS = 1e-5
CH = D * D // P
HCHUNKS = 2 + 2 * NG + 2 + 2
SEQ = [0, 1] + 2 * list(range(2, 2 + HCHUNKS)) + [2 + HCHUNKS, 3 + HCHUNKS]
ITEMS = 38
LOG1P = [(-1.0) ** (k + 1) / k for k in range(1, 9)]


def wait(eng, sem, n):
    if isinstance(n, int) and n <= 0:
        return
    eng.wait_ge(sem, n)


def build(nc, x_in, ctx_in, w_in, wkv_in, wp_in, proto_in, protot_in, bias_in, conv_in, dwb_in, skip_in, alog_in,
          dtb_in, temp_in, out):
    es = ExitStack()
    with es:
        def sb(name, shape, dt=F32):
            return es.enter_context(nc.sbuf_tensor(name, shape, dt))

        def sem(name):
            return es.enter_context(nc.semaphore(name))

        x = sb("x", [P, 8, D])
        ident = sb("ident", [P, P])
        ones = sb("ones", [P, P])
        head_ones = sb("head_ones", [P, P])
        causal = sb("causal", [P, T])
        wkv = sb("wkv", [P, DC, P])
        wp = sb("wp", [P, DC, 64])
        wph, wpl = sb("wph", [P, DC, 64], F16), sb("wpl", [P, DC, 64], F16)
        sel = sb("sel", [P, 8 * P])
        alog = sb("alog", [SH, SN])
        amat = sb("amat", [SH, SN])
        dtb = sb("dtb", [SH, 1])
        conv_w = sb("conv_w", [P, VC, 4])
        conv_b = sb("conv_b", [P, VC])
        skip = sb("skip", [P, VC])
        proto = sb("proto", [NP, D])
        proto_t = sb("proto_t", [P, DC, NP])
        pth, ptl = sb("pth", [P, DC, NP], F16), sb("ptl", [P, DC, NP], F16)
        ebias = sb("ebias", [NP, D])
        p2 = sb("p2", [NP, 1])
        nit = sb("nit", [P, 4])
        stats = sb("stats", [P, 8, 6])
        mv = sb("mv", [P, 8, 2])
        std = sb("std", [P, 8])
        tiny = sb("tiny", [P, 2])
        io = sb("io", [P, NP])
        rstd = sb("rstd", [P, 8])
        wst = sb("wst", [P, 2, CH // 2])
        wh, wl = sb("wh", [P, 2, CH], F16), sb("wl", [P, 2, CH], F16)

        words = 38300
        arena = sb("arena", [P, words])
        cursor = [0]

        def carve(n, dt=F32):
            a = cursor[0]
            cursor[0] += n
            assert cursor[0] <= words, cursor
            v = arena[:, a:a + n]
            return v if dt == F32 else v.bitcast(dt)

        ctx = [carve(DC * NKEY).rearrange("p (c k) -> p c k", c=DC) for _ in range(2)]
        qs = carve(B * H * T // 2, F16)
        ks = [carve(802, F16) for _ in range(2)]
        vt = carve(1602)
        vv = [carve(KT * 96).rearrange("p (k n) -> p k n", k=KT) for _ in range(2)]
        pr = [carve(2 * 512) for _ in range(2)]
        ot = carve(DC * TOK).rearrange("p (c t) -> p c t", c=DC)
        rl = carve(512)
        on = [carve(512) for _ in range(2)]
        mxp = carve(8 * 4).rearrange("p (i k) -> p i k", i=8)
        mx = carve(8)
        eye8 = carve(8 * P)[0:8, :].rearrange("p (i n) -> p i n", i=8)
        xn_a = carve(2 * D).rearrange("p (u d) -> p u d", u=2)
        cursor[0] = DC * NKEY
        xah = carve(DC * TOK // 2, F16).rearrange("p (c t) -> p c t", c=DC)
        xal = carve(DC * TOK // 2, F16).rearrange("p (c t) -> p c t", c=DC)
        cursor[0] = 0
        oth = carve(DC * TOK // 2, F16).rearrange("p (c t) -> p c t", c=DC)
        otl = carve(DC * TOK // 2, F16).rearrange("p (c t) -> p c t", c=DC)
        assert cursor[0] <= DC * NKEY
        cursor[0] = 0
        xbh = carve(DC * HT // 2, F16).rearrange("p (c t) -> p c t", c=DC)
        xbl = carve(DC * HT // 2, F16).rearrange("p (c t) -> p c t", c=DC)
        val = carve(VC * HT).rearrange("p (v t) -> p v t", v=VC)
        vh = carve(VC * HT // 2, F16).rearrange("p (v t) -> p v t", v=VC)
        vl = carve(VC * HT // 2, F16).rearrange("p (v t) -> p v t", v=VC)
        ut = carve(4 * DI).rearrange("p (b i) -> p b i", b=4)
        coef = carve(2 * 4 * HT).rearrange("p (j g n) -> p j g n", j=2, g=4)
        ndt = carve(4 * HT).rearrange("p (g n) -> p g n", g=4)
        NS = 4 * HB
        psi = carve(4 * NS * (T + 1)).rearrange("p (c s t) -> p c s t", c=4, s=NS)
        rm = carve(4 * NS).rearrange("p (j r s) -> p j r s", j=2, r=2)
        rq = carve(2 * NS).rearrange("p (r s) -> p r s", r=2)
        pd = carve(3 * HT).rearrange("p (j t) -> p j t", j=3)
        raw = carve(4 * HT).rearrange("p (j t) -> p j t", j=4)
        sq = carve(HT)
        rn = carve(4 * HT).rearrange("p (j t) -> p j t", j=4)
        cp = rn
        dd = coef.rearrange("p j g n -> p j (g n)")[:, 1, 0:2 * HT].rearrange("p (j t) -> p j t", j=2)
        kk = coef.rearrange("p j g n -> p j (g n)")[:, 1, 2 * HT:4 * HT]
        t1 = carve(2 * HT).rearrange("p (j t) -> p j t", j=2)
        t2 = carve(2 * HT).rearrange("p (j t) -> p j t", j=2)
        bt = carve(2 * HT).rearrange("p (j t) -> p j t", j=2)
        ct = t1
        xn_b = t1
        gate = psi.rearrange("p c s t -> p (c s t)")[:, 0:VC * HT].rearrange("p (v t) -> p v t", v=VC)
        cursor[0] = 0
        xn_c = carve(2 * D).rearrange("p (u d) -> p u d", u=2)
        xch = carve(DC * TOK // 2, F16).rearrange("p (c t) -> p c t", c=DC)
        xcl = carve(DC * TOK // 2, F16).rearrange("p (c t) -> p c t", c=DC)
        xsq = carve(D)
        x2 = carve(8)
        p2d = carve(NP)
        p2b = carve(NP)
        fa = carve(8 * NP).rearrange("p (t n) -> p t n", t=8)
        nd = carve(8 * NP).rearrange("p (t n) -> p t n", t=8)
        ds = carve(8 * NP).rearrange("p (t n) -> p t n", t=8)
        top = carve(8 * 8).rearrange("p (t n) -> p t n", t=8)
        topi = carve(8 * 8).rearrange("p (t n) -> p t n", t=8).bitcast(U32)
        topf = carve(8 * 8).rearrange("p (t n) -> p t n", t=8)
        dm = carve(8)
        m0 = carve(8 * NP).rearrange("p (t n) -> p t n", t=8)
        m1 = carve(8 * NP).rearrange("p (t n) -> p t n", t=8)
        ew = carve(8 * NP).rearrange("p (t n) -> p t n", t=8)
        es_sum = carve(8)
        wn = carve(8 * NP).rearrange("p (t n) -> p t n", t=8)
        hw = carve(2 * D).rearrange("p (u d) -> p u d", u=2)
        wt = carve(8 * P).rearrange("p (t n) -> p t n", t=8)
        hh = carve(2 * DC * P // 2, F16).rearrange("p (u c t) -> p u c t", u=2, c=DC)
        hl = carve(2 * DC * P // 2, F16).rearrange("p (u c t) -> p u c t", u=2, c=DC)

        ps = es.enter_context(nc.psum_tensor("ps", [P, 8, 512], F32))

        s_x, s_wkv, s_small, s_proto = sem("x_loaded"), sem("wkv_loaded"), sem("small_loaded"), sem("proto_loaded")
        s_ctx = [sem("ctx0_loaded"), sem("ctx1_loaded")]
        s_wld = [sem("weight_piece0_loaded"), sem("weight_piece1_loaded")]
        s_whi, s_wsc, s_wlo = sem("weight_hi"), sem("weight_scaled"), sem("weight_lo")
        s_pool, s_dve, s_act = sem("pool_step"), sem("dve_step"), sem("act_step")
        s_const, s_cdve, s_cact = sem("pool_constants"), sem("dve_constants"), sem("act_constants")
        ln_sems = [[sem(f"ln{k}_{n}") for n in ("var", "std", "xn", "tr", "hi", "lo")] for k in range(4)]
        s_q, s_qhi, s_qlo = sem("q_products"), sem("q_hi"), sem("q_lo")
        s_item, s_itemfree, s_khi = sem("item_ready"), sem("item_used"), sem("k_hi")
        s_mx, s_s2, s_exp, s_pv = sem("maxima"), sem("scores"), sem("probs"), sem("probs_used")
        s_rl, s_on = sem("denominators"), sem("attn_normed")
        s_ot = [sem("attn_even_placed"), sem("attn_odd_placed")]
        s_oh, s_ol, s_y, s_x1 = sem("attn_hi"), sem("attn_lo"), sem("concat_products"), sem("x1")
        s_vp, s_cv, s_silu = sem("value_products"), sem("conv_done"), sem("value_f32")
        s_vhi, s_vlo = sem("value_hi"), sem("value_lo")
        s_ut, s_utc = sem("value_transposed"), sem("ut_ready")
        s_pp, s_pe1, s_pdr = sem("param_products"), sem("param_exp"), sem("dt_k_ready")
        s_bc, s_bcc = sem("coef_broadcast"), sem("coef_ready")
        s_rec = sem("recurrence_step")
        s_bp, s_raw = sem("bc_products"), sem("bc_copied")
        s_sq, s_ss, s_lg, s_rn = sem("bc_squared"), sem("sum_of_squares"), sem("norm_log"), sem("norm_ready")
        s_det, s_dinv = sem("determinant"), sem("inverse_determinant")
        s_bt, s_k, s_kk, s_yp, s_yv = sem("bt_ct_ready"), sem("kernel_products"), sem("kernel_masked"), sem("y_products"), sem("y_ready")
        s_kh, s_ye = sem("kernels_of_two_heads"), sem("y_of_even_batches")
        s_gp, s_gs, s_gy, s_ghi, s_glo = sem("gate_products"), sem("gate_silu"), sem("gated"), sem("gated_hi"), sem("gated_lo")
        s_oq, s_op, s_xo = sem("out_first_half"), sem("out_products"), sem("x2")
        s_xx, s_pb = sem("x_squares"), sem("p2_broadcast")
        s_xp, s_d2, s_sqd, s_dif, s_e, s_wn = sem("proto_products"), sem("dist2"), sem("dist"), sem("dist_shift"), sem("weights_exp"), sem("router_ready")
        s_iota = sem("iota")
        s_wtt, s_wt = sem("router_transposed"), sem("router_t")
        s_hp, s_hw, s_ht, s_hhi, s_hlo = sem("h_products"), sem("h_weighted"), sem("h_transposed"), sem("h_hi"), sem("h_lo")
        s_fp, s_fo, s_out = sem("ffn_products"), sem("x3"), sem("out_stored")

        block = es.enter_context(nc.Block())

        def chunk_at(half, n):
            return 2 + half * HCHUNKS + n

        def chunk_used(s):
            if s < 2:
                return (s_q, s_y)[s], 8
            half, n = divmod(s - 2, HCHUNKS)
            if half == 2:
                return (s_hp, s_fp)[n], 8
            if n < 2:
                return s_vp, 8 * half + 4 * (n + 1)
            if n < 2 + 2 * NG:
                return s_bp, 4 * NG * half + 2 * (n - 1)
            if n < 4 + 2 * NG:
                return s_gp, 8 * half + 4 * (n - 1 - 2 * NG)
            return (s_oq, s_op)[n - 4 - 2 * NG], 4 * (half + 1)

        def weights_there(pe, s):
            pe.wait_ge(s_wlo, 2 * (s + 1))

        def split3(pairs):
            (ah, al), (bh, bl) = pairs
            return [(ah, bh), (ah, bl), (al, bh)]

        @block.sync
        def _(sp):
            for t in range(8):
                sp.dma_start(x[:, t, :], x_in[t]).then_inc(s_x, 16)

            def weight_piece(q):
                wait(sp, s_wlo, q - 1)
                sp.dma_start(wst[:, q % 2, :], w_in[SEQ[q // 2], :, (q % 2) * (CH // 2):(q % 2 + 1) * (CH // 2)]
                             ).then_inc(s_wld[q % 2], 16)

            weight_piece(0)
            weight_piece(1)
            sp.dma_start(wkv[:, :, :], wkv_in).then_inc(s_wkv, 16)
            sp.dma_start(ctx[0], ctx_in[0]).then_inc(s_ctx[0], 16)
            for dst, src in ((wp[:, :, :], wp_in), (alog[:, :], alog_in), (dtb[:, :], dtb_in), (conv_w[:, :, :], conv_in),
                             (conv_b[:, :], dwb_in), (skip[:, :], skip_in)):
                sp.dma_start(dst, src).then_inc(s_small, 16)
            sp.dma_start(proto[:, :], proto_in).then_inc(s_proto, 16)
            sp.dma_start(proto_t[:, :, :], protot_in).then_inc(s_proto, 16)
            sp.dma_start(ebias[:, :], bias_in).then_inc(s_proto, 16)
            sp.dma_start(nit[:, 0:1], temp_in).then_inc(s_proto, 16)
            for q in range(2, 6):
                weight_piece(q)
            sp.wait_ge(s_qlo, 8)
            wait(sp, s_q, 8)
            sp.dma_start(ctx[1], ctx_in[1]).then_inc(s_ctx[1], 16)

            def place(b, u):
                wait(sp, s_on, b + 1)
                for q in range(2):
                    src = on[u][96 * q:96 * q + 32, :].rearrange("p (m j t) -> p m j t", m=2, j=4)
                    for j in range(4):
                        sp.dma_start(ot[32 * j:32 * j + 32, 2 * q:2 * q + 2, bass.ds(b * T, T)], src[:, :, j, :]
                                     ).then_inc(s_ot[u], 16)

            def load_ctx(b, u):
                wait(sp, s_item, ITEMS * (b - 2) + 4)
                sp.dma_start(ctx[u], ctx_in[bass.ds(b, 1)].rearrange("a p c k -> p (a c) k")).then_inc(s_ctx[u], 16)

            load_ctx(2, 0)
            place(0, 0)
            load_ctx(3, 1)
            place(1, 1)
            with sp.Fori(1, B // 2 - 1) as i:
                load_ctx(2 * i + 2, 0)
                place(2 * i, 0)
                load_ctx(2 * i + 3, 1)
                place(2 * i + 1, 1)
            place(B - 2, 0)
            place(B - 1, 1)
            for q in range(6, 2 * len(SEQ)):
                weight_piece(q)
            for t in range(8):
                wait(sp, s_fo, t + 1)
                sp.dma_start(out[t], x[:, t, :]).then_inc(s_out, 16)
            sp.wait_ge(s_out, 8 * 16)

        @block.gpsimd
        def _(pool):
            n = [0]

            def link(ins):
                n[0] += 1
                ins.then_inc(s_pool, 1)
                pool.wait_ge(s_pool, n[0])

            nc.gpsimd.iota(io[:, :], pattern=[[1, NP]], base=0, channel_multiplier=0,
                           allow_small_or_imprecise_dtypes=True).then_inc(s_iota, 1)
            pool.wait_ge(s_iota, 1)
            link(nc.gpsimd.memset(ident[:, :], 0.0))
            link(nc.gpsimd.memset(causal[:, :], 1.0))
            link(nc.gpsimd.memset(eye8[:, :, :], 0.0))
            nc.gpsimd.affine_select(out=ident[:, :], in_=ident[:, :], compare_op=ALU.not_equal, fill=1.0, base=0,
                                    pattern=[[-1, P]], channel_multiplier=1).then_inc(s_const, 1)
            for e in range(2):
                pool.wait_ge(s_const, e + 1)
                v = causal[T * e:T * e + T, :]
                nc.gpsimd.affine_select(out=v, in_=v, compare_op=ALU.is_ge, fill=0.0, base=0,
                                        pattern=[[1, T]], channel_multiplier=-1).then_inc(s_const, 1)
            pool.wait_ge(s_const, 3)
            nc.gpsimd.affine_select(out=eye8[:, :, :], in_=eye8[:, :, :], compare_op=ALU.not_equal, fill=1.0 / MS,
                                    base=0, pattern=[[-1, 8], [0, P]], channel_multiplier=1).then_inc(s_const, 1)
            pool.wait_ge(s_const, 4)
            for q in range(2 * len(SEQ)):
                s, r = divmod(q, 2)
                st = wst[:, r, :]
                lo = slice(r * (CH // 2), (r + 1) * (CH // 2))
                pool.wait_ge(s_wld[r], 16 * (s + 1))
                if s >= 2:
                    pool.wait_ge(*chunk_used(s - 2))
                nc.gpsimd.tensor_scalar(wh[:, s % 2, lo], st, WS, 0.0, ALU.mult, ALU.add).then_inc(s_whi, 1)
                pool.wait_ge(s_whi, q + 1)
                nc.gpsimd.tensor_scalar(st, st, WS, 0.0, ALU.mult, ALU.add).then_inc(s_wsc, 1)
                pool.wait_ge(s_wsc, q + 1)
                nc.gpsimd.tensor_tensor(wl[:, s % 2, lo], st, wh[:, s % 2, lo], ALU.subtract).then_inc(s_wlo, 1)
                pool.wait_ge(s_wlo, q + 1)

        @block.tensor
        def _(pe):
            mm = nc.tensor.matmul

            def bank(b):
                return ps[:, b, :]

            def layer_norm(k, tiles, banks):
                var, stdd, xnr, tr, hi, lo = ln_sems[k]
                xn = (xn_a, xn_b, xn_b, xn_c)[k]
                for i in range(tiles):
                    pe.wait_ge(xnr, i + 1)
                    wait(pe, hi, i - 1)
                    wait(pe, lo, i - 1)
                    for c in range(DC):
                        last = nc.tensor.transpose(bank(banks[i % 2])[:, c * P:(c + 1) * P],
                                                   xn[:, i % 2, c * P:(c + 1) * P], ident[:, :])
                    last.then_inc(tr, 1)

            pe.wait_ge(s_const, 4)
            layer_norm(0, 8, (0, 1))
            W = wh[:, 0, :].rearrange("p (c n) -> p c n", c=DC), wl[:, 0, :].rearrange("p (c n) -> p c n", c=DC)
            weights_there(pe, 0)
            for u in range(8):
                n2, m = divmod(u, 4)
                pe.wait_ge(ln_sems[0][4], 4 * n2 + 4)
                pe.wait_ge(ln_sems[0][5], 4 * n2 + 4)
                wait(pe, s_qlo, u - 1)
                k = 0
                for a, b in ((W[0], xah), (W[0], xal), (W[1], xah)):
                    for c in range(DC):
                        last = mm(bank(2 + u % 2)[:, :], a[:, c, m * P:(m + 1) * P], b[:, c, n2 * HT:(n2 + 1) * HT],
                                  start=(k == 0), stop=(k == 3 * DC - 1))
                        k += 1
                last.then_inc(s_q, 1)

            def item_bank(b, p):
                if p < 3:
                    wait(pe, s_itemfree, ITEMS * b - (1, 0, 2)[p])
                else:
                    wait(pe, s_itemfree, ITEMS * b + p - 2)
                return bank(5 + p % 3)

            def kv(b, u, p, first):
                if p == 0:
                    pe.wait_ge(s_ctx[u], first)
                o = item_bank(b, p)
                k0, n = BLK[p]
                for c in range(DC):
                    last = mm(o[:, 0:n], wkv[:, c, :], ctx[u][:, c, k0:k0 + n], start=(c == 0), stop=(c == DC - 1))
                last.then_inc(s_item, 1)

            def v_there(b):
                item_bank(b, 4)
                wait(pe, s_khi, 4 * (b + 1))

            def v_turn(b):
                o = bank(6)
                for kt in range(KT):
                    nk = min(P, NKEY - kt * P)
                    last = nc.tensor.transpose(o[0:nk, 32 * kt:32 * kt + 32], vt[96:128, kt * P:kt * P + nk],
                                               ident[96:128, 96:128])
                last.then_inc(s_item, 1)

            def s1(b, u, i):
                for blk, (k0, n) in enumerate(BLK):
                    o = item_bank(b, 5 + 4 * i + blk)
                    if i == 0 and blk == 0:
                        wait(pe, s_itemfree, ITEMS * b + 4)
                    mm(o[:, 0:n], qs[0:96, bass.ds(b * 1024 + i * P, P)], ks[u][0:96, k0:k0 + n],
                       start=True, stop=True).then_inc(s_item, 1)

            def turn_max(b):
                o = item_bank(b, 37)
                wait(pe, s_mx, b + 1)
                nc.tensor.transpose(o[0:8, 0:P], mx, ident[:, :]).then_inc(s_item, 1)

            def prepare(b, u, kt, first):
                if kt < 4:
                    kv(b, u, kt, first)
                elif kt == 4:
                    v_turn(b)
                elif kt < 13:
                    s1(b, u, kt - 5)

            def s2(b, u, kt):
                k = KT * b + kt
                s = (KT * u + kt) % 2
                nk = min(P, NKEY - kt * P)
                wait(pe, s_exp, k - 1)
                if kt == 0:
                    wait(pe, s_itemfree, ITEMS * (b + 1))
                for q in range(2):
                    last = mm(ps[0:nk, 2 * s + q, :], ks[u][0:104, kt * P:kt * P + nk],
                              qs[0:104, bass.ds(b * 1024 + q * 512, 512)], start=True, stop=True)
                last.then_inc(s_s2, 1)

            def pv(b, u, kt):
                k = KT * b + kt
                s = (KT * u + kt) % 2
                nk = min(P, NKEY - kt * P)
                wait(pe, s_exp, k + 1)
                if kt == 0:
                    wait(pe, s_on, b)
                for q in range(2):
                    last = mm(ps[64 * q:64 * q + 64, 4, :], vv[u][0:nk, kt, 32 * q:32 * q + 64],
                              pr[s][0:nk, 512 * q:512 * q + 512], start=(kt == 0), stop=(kt == KT - 1))
                last.then_inc(s_pv, 1)

            def batch(b, u, nxt):
                s2(b, u, 0)
                for kt in range(KT):
                    if nxt is not None and kt == 4:
                        v_there(b + 1)
                    if kt + 1 < KT:
                        s2(b, u, kt + 1)
                    if nxt is not None:
                        prepare(b + 1, 1 - u, kt, nxt)
                    pv(b, u, kt)
                if nxt is not None:
                    turn_max(b + 1)

            pe.wait_ge(s_wkv, 16)
            wait(pe, s_qlo, 8)
            for kt in range(KT):
                if kt == 4:
                    v_there(0)
                prepare(0, 0, kt, 16)
            turn_max(0)
            batch(0, 0, 16)
            batch(1, 1, 32)
            with pe.Fori(1, B // 2 - 1) as i:
                batch(2 * i, 0, 16 * (i + 1))
                batch(2 * i + 1, 1, 16 * (i + 2))
            batch(B - 2, 0, 16 * (B // 2))
            batch(B - 1, 1, None)

            weights_there(pe, 1)
            Wc = wh[:, 1, :].rearrange("p (c n) -> p c n", c=DC), wl[:, 1, :].rearrange("p (c n) -> p c n", c=DC)
            for t in range(8):
                pe.wait_ge(s_oh, t // 4 + 1)
                pe.wait_ge(s_ol, t // 4 + 1)
                wait(pe, s_x1, t - 1)
                k = 0
                for a, b in ((oth, Wc[0]), (oth, Wc[1]), (otl, Wc[0])):
                    for c in range(DC):
                        last = mm(bank(t % 2), a[:, c, t * P:(t + 1) * P], b[:, c, :],
                                  start=(k == 0), stop=(k == 3 * DC - 1))
                        k += 1
                last.then_inc(s_y, 1)

            def wide(half, n, v, dst, done):
                s = chunk_at(half, n + v // 4)
                if v % 4 == 0:
                    weights_there(pe, s)
                hi = wh[:, s % 2, :].rearrange("p (c n) -> p c n", c=DC)
                lo = wl[:, s % 2, :].rearrange("p (c n) -> p c n", c=DC)
                cols = slice((v % 4) * P, (v % 4 + 1) * P)
                k = 0
                for a, b in ((hi, xbh), (hi, xbl), (lo, xbh)):
                    for c in range(DC):
                        last = mm(dst, a[:, c, cols], b[:, c, :], start=(k == 0), stop=(k == 3 * DC - 1))
                        k += 1
                last.then_inc(done, 1)

            for hf in range(2):
                if hf == 0:
                    pe.wait_ge(s_x1, 8)
                else:
                    pe.wait_ge(s_xo, 4)
                layer_norm(1 + hf, 4, (2, 3))
                pe.wait_ge(ln_sems[1 + hf][4], 4)
                pe.wait_ge(ln_sems[1 + hf][5], 4)
                pe.wait_ge(s_cact, 2)
                pe.wait_ge(s_cdve, 3)
                k = 0
                for a, b in ((wph, xbh), (wph, xbl), (wpl, xbh)):
                    for c in range(DC):
                        last = mm(ps[0:64, 4, :], a[:, c, :], b[:, c, :], start=(k == 0), stop=(k == 3 * DC - 1))
                        k += 1
                last.then_inc(s_pp, 1)
                for v in range(VC):
                    wait(pe, s_cv, 8 * hf + v - 1)
                    wide(hf, 0, v, bank(v % 2), s_vp)
                for n in range(8):
                    vq, bp = divmod(n, 4)
                    pe.wait_ge(s_silu, 8 * hf + 4 * vq + 4)
                    wait(pe, s_utc, 8 * hf + n - 1)
                    for c in range(4):
                        last = nc.tensor.transpose(bank(6 + n % 2)[:, c * P:(c + 1) * P],
                                                   val[:, 4 * vq + c, bp * P:(bp + 1) * P], ident[:, :])
                    last.then_inc(s_ut, 1)
                pe.wait_ge(s_vhi, 8 * (hf + 1))
                pe.wait_ge(s_vlo, 8 * (hf + 1))

                def bc(g, j):
                    G = NG * hf + g
                    s = chunk_at(hf, 2 + 2 * g + j // 2)
                    if j % 2 == 0:
                        weights_there(pe, s)
                    wait(pe, s_raw, 4 * (G - 1) + j + 1)
                    if j == 0 and g == 0:
                        wait(pe, s_cv, 8 * (hf + 1))
                    hi = wh[:, s % 2, :].rearrange("p (k j n) -> p k j n", k=VC, j=2)
                    lo = wl[:, s % 2, :].rearrange("p (k j n) -> p k j n", k=VC, j=2)
                    k = 0
                    for a, b in ((hi, vh), (hi, vl), (lo, vh)):
                        for c in range(VC):
                            last = mm(bank(j), a[:, c, j % 2, :], b[:, c, :], start=(k == 0), stop=(k == 3 * VC - 1))
                            k += 1
                    last.then_inc(s_bp, 1)

                def ss(g, j):
                    n = 4 * (NG * hf + g) + j
                    pe.wait_ge(s_sq, n + 1)
                    wait(pe, s_lg, n)
                    mm(bank(4), head_ones[:, :], sq, start=True, stop=True).then_inc(s_ss, 1)

                def kernels(g):
                    G = NG * hf + g
                    pe.wait_ge(s_bt, G + 1)
                    wait(pe, s_kk, G)
                    for h in range(4):
                        if h == 2:
                            pe.wait_ge(s_kh, G + 1)
                        for bp in range(4):
                            col = (h % 2) * 512 + (h // 2) * 256 + bp * T
                            for e in range(2):
                                t0 = (2 * bp + e) * T
                                for j in range(2):
                                    last = mm(ps[T * e:T * e + T, 6 + col // 512, col % 512:col % 512 + T],
                                              bt[32 * h:32 * h + 32, j, t0:t0 + T], ct[32 * h:32 * h + 32, 1 - j, t0:t0 + T],
                                              start=(j == 0), stop=(j == 1))
                        if h == 1:
                            last.then_inc(s_kh, 1)
                    last.then_inc(s_k, 1)

                def outputs(g):
                    G = NG * hf + g
                    pe.wait_ge(s_kk, G + 1)
                    wait(pe, s_yv, G)
                    for e in range(2):
                        if e:
                            pe.wait_ge(s_ye, G + 1)
                        for bp in range(4):
                            for h in range(4):
                                t0 = (2 * bp + e) * T
                                col = (h % 2) * 512 + (h // 2) * 256 + bp * T
                                last = mm(ps[32 * h:32 * h + 32, 5, t0:t0 + T],
                                          ut[T * e:T * e + T, bp, g * P + 32 * h:g * P + 32 * h + 32],
                                          kk[T * e:T * e + T, col:col + T],
                                          start=True, stop=True)
                        if e == 0:
                            last.then_inc(s_ye, 1)
                    last.then_inc(s_yp, 1)

                for gh in range(2):
                    wait(pe, s_pdr, hf + 1)
                    if gh == 0:
                        wait(pe, s_utc, 8 * (hf + 1))
                    for n in range(12):
                        g4, j = divmod(n, 3)
                        N = 12 * (2 * hf + gh) + n
                        wait(pe, s_bcc, N - 1)
                        c0 = (4 * gh + g4) * P
                        mm(bank(6 + n % 2), sel[:, c0:c0 + P], pd[:, j, :], start=True, stop=True).then_inc(s_bc, 1)
                    wait(pe, s_bcc, 12 * (2 * hf + gh + 1))
                    for g in range(4 * gh, 4 * gh + 4):
                        bc(g, 0)
                        if g > 4 * gh + 1:
                            outputs(g - 2)
                        bc(g, 1)
                        ss(g, 0)
                        bc(g, 2)
                        ss(g, 1)
                        bc(g, 3)
                        ss(g, 2)
                        ss(g, 3)
                        if g > 4 * gh:
                            kernels(g - 1)
                    outputs(4 * gh + 2)
                    kernels(4 * gh + 3)
                    outputs(4 * gh + 3)
                for v in range(VC):
                    wait(pe, s_gs, 8 * hf + v - 1)
                    wide(hf, 2 + 2 * NG, v, bank(v % 2), s_gp)
                for q in range(2):
                    s = chunk_at(hf, 4 + 2 * NG + q)
                    weights_there(pe, s)
                    hi = wh[:, s % 2, :].rearrange("p (k n) -> p k n", k=4)
                    lo = wl[:, s % 2, :].rearrange("p (k n) -> p k n", k=4)
                    pe.wait_ge(s_ghi, 8 * hf + 4 * q + 4)
                    pe.wait_ge(s_glo, 8 * hf + 4 * q + 4)
                    if q == 0:
                        wait(pe, s_gs, 8 * (hf + 1))
                    for t in range(4):
                        k = 0
                        for a, b in ((vh, hi), (vh, lo), (vl, hi)):
                            for c in range(4):
                                last = mm(bank(t), a[:, 4 * q + c, t * P:(t + 1) * P], b[:, c, :],
                                          start=(q == 0 and k == 0), stop=(q == 1 and k == 11))
                                k += 1
                        last.then_inc((s_oq, s_op)[q], 1)

            pe.wait_ge(s_xo, 8)
            layer_norm(3, 8, (4, 5))
            pe.wait_ge(s_pb, 1)
            mm(ps[:, 6, 0:NP], ones[0:NP, :], p2d[0:NP, :], start=True, stop=True).then_inc(s_pb, 1)
            pe.wait_ge(ln_sems[3][4], 8)
            pe.wait_ge(ln_sems[3][5], 8)
            for t in range(8):
                k = 0
                for a, b in ((xch, pth), (xch, ptl), (xcl, pth)):
                    for c in range(DC):
                        last = mm(ps[:, 7, t * NP:(t + 1) * NP], a[:, c, t * P:(t + 1) * P], b[:, c, :],
                                  start=(k == 0), stop=(k == 3 * DC - 1))
                        k += 1
            last.then_inc(s_xp, 1)
            sB, sA = len(SEQ) - 2, len(SEQ) - 1
            Wb = wh[:, sB % 2, :].rearrange("p (c n) -> p c n", c=DC), wl[:, sB % 2, :].rearrange("p (c n) -> p c n", c=DC)
            Wa = wh[:, sA % 2, :].rearrange("p (c n) -> p c n", c=DC), wl[:, sA % 2, :].rearrange("p (c n) -> p c n", c=DC)

            def h_tile(t):
                wait(pe, s_hw, t - 1)
                k = 0
                for a, b in ((xch, Wb[0]), (xch, Wb[1]), (xcl, Wb[0])):
                    for c in range(DC):
                        last = mm(bank(t % 2), a[:, c, t * P:(t + 1) * P], b[:, c, :], start=(k == 0), stop=(k == 3 * DC - 1))
                        k += 1
                last.then_inc(s_hp, 1)

            weights_there(pe, sB)
            h_tile(0)
            h_tile(1)
            pe.wait_ge(s_wn, 1)
            pe.wait_ge(s_pb, 3)
            for t in range(8):
                last = nc.tensor.transpose(ps[0:NP, 6, (t % 4) * P:(t % 4 + 1) * P], wn[:, t, :], ident[:, :])
                if t % 4 == 3:
                    last.then_inc(s_wtt, 1)
                    pe.wait_ge(s_wt, t // 4 + 1)
            weights_there(pe, sA)
            for t in range(8):
                pe.wait_ge(s_hw, t + 1)
                wait(pe, s_hhi, t - 1)
                wait(pe, s_hlo, t - 1)
                for c in range(DC):
                    last = nc.tensor.transpose(bank(4 + t % 2)[:, c * P:(c + 1) * P], hw[:, t % 2, c * P:(c + 1) * P], ident[:, :])
                last.then_inc(s_ht, 1)
                if t + 2 < 8:
                    h_tile(t + 2)
                wait(pe, s_fo, t - 1)
                o = bank(2 + t % 2)
                mm(o, wt[0:NP, t, :], ebias[:, :], start=True, stop=False)
                pe.wait_ge(s_hhi, t + 1)
                pe.wait_ge(s_hlo, t + 1)
                k = 0
                for a, b in ((hh, Wa[0]), (hh, Wa[1]), (hl, Wa[0])):
                    for c in range(DC):
                        last = mm(o, a[:, t % 2, c, :], b[:, c, :], start=False, stop=(k == 3 * DC - 1))
                        k += 1
                last.then_inc(s_fp, 1)

        @block.scalar
        def _(act):
            n = [0]
            f = nc.scalar.activation

            def link(ins):
                n[0] += 1
                ins.then_inc(s_act, 1)
                act.wait_ge(s_act, n[0])

            def layer_norm(k, tiles, banks, hi_t):
                var, stdd, xnr, tr, hi, lo = ln_sems[k]
                act.wait_ge(var, 1)
                f(std[:, 0:tiles], rstd[:, 0:tiles], ACT.Sqrt).then_inc(stdd, 1)
                for i in range(tiles):
                    act.wait_ge(tr, i + 1)
                    src = ps[:, banks[i % 2], :].rearrange("p (c t) -> p c t", c=DC)
                    if k == 3:
                        wait(act, s_xx, i)
                        f(xsq, xn_c[:, i % 2, :], ACT.Square, accum_out=x2[:, i:i + 1]).then_inc(s_xx, 1)
                    f(hi_t[:, :, i * P:(i + 1) * P], src, ACT.Copy, scale=XS).then_inc(hi, 1)

            layer_norm(0, 8, (0, 1), xah)
            nc.scalar.preload_act_table_set("natural_log_exp_and_others")
            act.wait_ge(s_small, 6 * 16)
            act.wait_ge(s_proto, 4 * 16)
            f(amat[:, :], alog[:, :], ACT.Exp).then_inc(s_cact, 1)
            f(wph[:, :, :], wp[:, :, :], ACT.Copy, scale=WS).then_inc(s_cact, 1)
            f(pth[:, :, :], proto_t[:, :, :], ACT.Copy, scale=WS).then_inc(s_cact, 1)
            for u in range(8):
                n2, m = divmod(u, 4)
                act.wait_ge(s_q, u + 1)
                for j in range(4):
                    dst = qs[0:32, :].rearrange("p (b h t) -> p b h t", b=B, h=H)[:, n2 * HB:(n2 + 1) * HB, 4 * m + j, :]
                    last = f(dst, ps[32 * j:32 * j + 32, 2 + u % 2, :].rearrange("p (b t) -> p b t", b=HB), ACT.Copy,
                             scale=1.0 / WS)
                last.then_inc(s_qhi, 1)

            def kv(b, u, p):
                if p == 0:
                    wait(act, s_pv, KT * (b - 1))
                k0, w = BLK[p]
                act.wait_ge(s_item, ITEMS * b + p + 1)
                f(ks[u][0:96, k0:k0 + w], ps[0:96, 5 + p % 3, 0:w], ACT.Copy, scale=XS)
                f(vt[96:128, k0:k0 + w], ps[96:128, 5 + p % 3, 0:w], ACT.Copy).then_inc(s_khi, 1)

            def probs(b, u, kt):
                k = KT * b + kt
                s = (KT * u + kt) % 2
                nk = min(P, NKEY - kt * P)
                wait(act, s_pv, k - 1)
                act.wait_ge(s_s2, k + 1)
                f(pr[s][0:nk, :].rearrange("p (q n) -> p q n", q=2), ps[0:nk, 2 * s:2 * s + 2, :], ACT.Exp,
                  scale=SC).then_inc(s_exp, 1)

            def batch(b, u, more):
                for kt in range(KT):
                    probs(b, u, kt)
                    if more and kt < 4:
                        kv(b + 1, 1 - u, kt)

            act.wait_ge(s_cdve, 4)
            for p in range(4):
                kv(0, 0, p)
            batch(0, 0, True)
            batch(1, 1, True)
            with act.Fori(1, B // 2 - 1) as i:
                batch(2 * i, 0, True)
                batch(2 * i + 1, 1, True)
            batch(B - 2, 0, True)
            batch(B - 1, 1, False)
            for u in range(2):
                act.wait_ge(s_ot[u], 8 * 16 * B // 2)
            for q in range(2):
                f(oth[:, :, q * HT:(q + 1) * HT], ot[:, :, q * HT:(q + 1) * HT], ACT.Copy, scale=XS).then_inc(s_oh, 1)

            for hf in range(2):
                layer_norm(1 + hf, 4, (2, 3), xbh)
                nc.scalar.preload_act_table_set("natural_log_exp_and_others")
                act.wait_ge(s_pp, hf + 1)
                f(cp[0:32, 0, :], ps[0:32, 4, :], ACT.Exp, bias=dtb[:, 0:1], scale=UNS).then_inc(s_pe1, 1)
                f(cp[0:32, 1, :], ps[32:64, 4, :], ACT.Exp, scale=-UNS).then_inc(s_pe1, 1)
                for v in range(VC):
                    act.wait_ge(s_cv, 8 * hf + v + 1)
                    f(val[:, v, :], raw[:, v % 2, :], ACT.Silu, bias=conv_b[:, v:v + 1], scale=UNS).then_inc(s_silu, 1)
                    act.wait_ge(s_silu, 8 * hf + v + 1)
                    f(vh[:, v, :], val[:, v, :], ACT.Copy, scale=XS).then_inc(s_vhi, 1)
                for m in range(8):
                    vq, bp = divmod(m, 4)
                    act.wait_ge(s_ut, 8 * hf + m + 1)
                    f(ut[:, bp, 512 * vq:512 * vq + 512], ps[:, 6 + m % 2, :], ACT.Copy).then_inc(s_utc, 1)
                nc.scalar.preload_act_table_set("natural_log_exp_and_others")
                for gh in range(2):
                    for m in range(12):
                        g4, j = divmod(m, 3)
                        N = 12 * (2 * hf + gh) + m
                        if m == 0:
                            wait(act, s_yv, 8 * hf + 4 * gh)
                        act.wait_ge(s_bc, N + 1)
                        dst = coef[:, j, g4, :] if j < 2 else ndt[:, g4, :]
                        f(dst, ps[:, 6 + m % 2, :], ACT.Copy).then_inc(s_bcc, 1)
                    for g in range(4 * gh, 4 * gh + 4):
                        G = NG * hf + g
                        wait(act, s_bt, G)
                        for j in range(4):
                            N = 4 * G + j
                            act.wait_ge(s_bp, N + 1)
                            wait(act, s_ss, N)
                            f(sq, ps[:, j, :], ACT.Square, scale=UNS).then_inc(s_sq, 1)
                            f(raw[:, j, :], ps[:, j, :], ACT.Copy, scale=UNS).then_inc(s_raw, 1)
                            act.wait_ge(s_ss, N + 1)
                            r = rn[:, j, :]
                            f(r, ps[:, 4, :], ACT.Ln, bias=tiny[:, 0:1]).then_inc(s_lg, 1)
                            act.wait_ge(s_lg, N + 1)
                            link(f(r, r, ACT.Exp, scale=0.5))
                            link(f(r, r, ACT.Ln, bias=tiny[:, 1:2]))
                            f(r, r, ACT.Exp, scale=-1.0).then_inc(s_rn, 1)
                        act.wait_ge(s_det, G + 1)
                        link(f(dd[:, 1, :], dd[:, 1, :], ACT.Ln))
                        link(f(dd[:, 1, :], dd[:, 1, :], ACT.Exp, scale=-1.0))
                        f(dd[:, 0, :], dd[:, 1, :], ACT.Copy, scale=-1.0).then_inc(s_dinv, 1)
                for v in range(VC):
                    act.wait_ge(s_gp, 8 * hf + v + 1)
                    wait(act, s_bt, 8 * hf + 8)
                    f(gate[:, v, :], ps[:, v % 2, :], ACT.Silu, scale=UNS).then_inc(s_gs, 1)
                for v in range(VC):
                    act.wait_ge(s_gy, 8 * hf + v + 1)
                    f(vh[:, v, :], val[:, v, :], ACT.Copy, scale=XS).then_inc(s_ghi, 1)

            layer_norm(3, 8, (4, 5), xch)
            act.wait_ge(s_xx, 8)
            f(xsq[0:NP, :], proto[:, :], ACT.Square, accum_out=p2[:, :]).then_inc(s_cact, 1)
            act.wait_ge(s_d2, 1)
            f(ds, fa, ACT.Sqrt).then_inc(s_sqd, 1)
            act.wait_ge(s_dif, 1)
            f(ew, ds, ACT.Exp, scale=nit[:, 3:4]).then_inc(s_e, 1)
            for q in range(2):
                act.wait_ge(s_wtt, q + 1)
                f(wt[0:NP, 4 * q:4 * q + 4, :], ps[0:NP, 6, :].rearrange("p (t n) -> p t n", t=4), ACT.Copy,
                  scale=XS * WS).then_inc(s_wt, 1)
            for t in range(8):
                act.wait_ge(s_ht, t + 1)
                wait(act, s_fp, t - 1)
                f(hh[:, t % 2, :, :], ps[:, 4 + t % 2, :].rearrange("p (c n) -> p c n", c=DC), ACT.Copy,
                  scale=XS).then_inc(s_hhi, 1)

        @block.vector
        def _(dve):
            n = [0]
            V = nc.vector

            def link(ins):
                n[0] += 1
                ins.then_inc(s_dve, 1)
                dve.wait_ge(s_dve, n[0])

            def layer_norm(k, tiles, banks, hi_t, lo_t, t0, ready):
                var, stdd, xnr, tr, hi, lo = ln_sems[k]
                xn = (xn_a, xn_b, xn_b, xn_c)[k]
                for i in range(tiles):
                    ready(i)
                    link(V.bn_stats(stats[:, i, :], x[:, t0 + i, :]))
                    link(V.bn_aggr(mv[:, i, :], stats[:, i, :]))
                V.tensor_scalar(rstd[:, 0:tiles], mv[:, 0:tiles, 1], EPS, None, ALU.add).then_inc(var, 1)
                dve.wait_ge(stdd, 1)
                link(V.reciprocal(rstd[:, 0:tiles], std[:, 0:tiles]))

                def normed(i):
                    wait(dve, tr, i - 1)
                    if k == 3:
                        wait(dve, s_xx, i - 1)
                    V.tensor_scalar(xn[:, i % 2, :], x[:, t0 + i, :], mv[:, i, 0:1], rstd[:, i:i + 1],
                                    ALU.subtract, ALU.mult).then_inc(xnr, 1)

                normed(0)
                for i in range(tiles):
                    if i + 1 < tiles:
                        normed(i + 1)
                    dve.wait_ge(tr, i + 1)
                    dve.wait_ge(hi, i + 1)
                    src = ps[:, banks[i % 2], :].rearrange("p (c t) -> p c t", c=DC)
                    cols = slice(i * P, (i + 1) * P)
                    V.scalar_tensor_tensor(lo_t[:, :, cols], src, XS, hi_t[:, :, cols], ALU.mult,
                                           ALU.subtract).then_inc(lo, 1)

            link(V.memset(tiny[:, 0:1], 1e-19))
            link(V.memset(tiny[:, 1:2], 1e-8))
            link(V.memset(head_ones[:, :], 0.0))
            for h in range(4):
                link(V.memset(head_ones[32 * h:32 * h + 32, 32 * h:32 * h + 32], 1.0))
            link(V.memset(ones[:, :], 1.0))
            link(V.memset(sel[:, :], 0.0))

            layer_norm(0, 8, (0, 1), xah, xal, 0, lambda i: dve.wait_ge(s_x, 16 * 8))
            dve.wait_ge(s_const, 4)
            dve.wait_ge(s_cact, 3)
            dve.wait_ge(s_proto, 4 * 16)
            diag = ident[0:32, 0:32].unsqueeze(2).to_broadcast([32, 32, 32])
            hv = "p (h n) -> p h n"
            V.tensor_tensor(sel[0:32, :].rearrange(hv, h=32), amat[:, :].unsqueeze(1).to_broadcast([32, 32, 32]), diag,
                            ALU.mult).then_inc(s_cdve, 1)
            V.tensor_copy(sel[32:64, :].rearrange(hv, h=32), diag)
            V.tensor_scalar(sel[64:96, :].rearrange(hv, h=32), diag, -1.0, None, ALU.mult).then_inc(s_cdve, 1)
            V.scalar_tensor_tensor(wpl[:, :, :], wp[:, :, :], WS, wph[:, :, :], ALU.mult, ALU.subtract).then_inc(s_cdve, 1)
            V.scalar_tensor_tensor(ptl[:, :, :], proto_t[:, :, :], WS, pth[:, :, :], ALU.mult, ALU.subtract)
            link(V.tensor_scalar(nit[:, 1:2], nit[:, 0:1], -1.0, None, ALU.mult))
            link(V.tensor_tensor(nit[:, 1:2], nit[:, 0:1], nit[:, 1:2], ALU.max))
            link(V.tensor_scalar(nit[:, 1:2], nit[:, 1:2], 0.1, None, ALU.max))
            link(V.reciprocal(nit[:, 2:3], nit[:, 1:2]))
            link(V.tensor_scalar(nit[:, 3:4], nit[:, 2:3], -1.0, None, ALU.mult))
            for u in range(2):
                V.memset(vv[u][:, :, 32:64], 1.0)
                last = V.memset(ks[u][96:104, 0:NKEY], MS)
            last.then_inc(s_cdve, 1)
            for u in range(8):
                n2, m = divmod(u, 4)
                dve.wait_ge(s_qhi, u + 1)
                view = [qs[32 * r:32 * r + 32, :].rearrange("p (b h t) -> p b h t", b=B, h=H)[:, n2 * HB:(n2 + 1) * HB]
                        for r in range(3)]
                for j in range(4):
                    h = 4 * m + j
                    V.tensor_copy(view[1][:, :, h, :], view[0][:, :, h, :])
                    last = V.scalar_tensor_tensor(view[2][:, :, h, :], ps[32 * j:32 * j + 32, 2 + u % 2, :].rearrange(
                        "p (b t) -> p b t", b=HB), 1.0 / WS, view[0][:, :, h, :], ALU.mult, ALU.subtract)
                last.then_inc(s_qlo, 1)

            def prepare(b, u):
                for p, (k0, w) in enumerate(BLK):
                    dve.wait_ge(s_khi, 4 * b + p + 1)
                    V.scalar_tensor_tensor(ks[u][32:64, k0:k0 + w], ps[32:64, 5 + p % 3, 0:w], XS, ks[u][32:64, k0:k0 + w],
                                           ALU.mult, ALU.subtract).then_inc(s_itemfree, 1)
                dve.wait_ge(s_item, ITEMS * b + 5)
                wait(dve, s_pv, KT * (b - 1))
                vp = ps[:, 6, 0:KT * 32].rearrange("p (k n) -> p k n", k=KT)
                for c0 in (0, 64):
                    V.tensor_copy(vv[u][:, 0:KT - 1, c0:c0 + 32], vp[:, 0:KT - 1, :])
                    nk = NKEY - (KT - 1) * P
                    last = V.tensor_copy(vv[u][0:nk, KT - 1, c0:c0 + 32], vp[0:nk, KT - 1, :])
                last.then_inc(s_itemfree, 1)
                for i in range(8):
                    for k, (k0, w) in enumerate(BLK):
                        p = 5 + 4 * i + k
                        dve.wait_ge(s_item, ITEMS * b + p + 1)
                        V.tensor_reduce(mxp[:, i, k:k + 1], ps[:, 5 + p % 3, 0:w], AX.X, ALU.max).then_inc(s_itemfree, 1)
                dve.wait_ge(s_itemfree, ITEMS * b + 37)
                V.tensor_reduce(mx, mxp, AX.X, ALU.max, negate=True).then_inc(s_mx, 1)
                dve.wait_ge(s_item, ITEMS * b + 38)
                V.tensor_tensor(qs[96:104, bass.ds(b * 1024, 1024)].rearrange("p (i n) -> p i n", i=8),
                                ps[0:8, 6, 0:P].unsqueeze(1).to_broadcast([8, 8, P]), eye8[:, :, :],
                                ALU.mult).then_inc(s_itemfree, 1)

            def finish(b, u, placed):
                dve.wait_ge(s_pv, KT * (b + 1))
                wait(dve, s_ot[u], placed)
                V.reciprocal(rl, ps[:, 4, :]).then_inc(s_rl, 1)
                dve.wait_ge(s_rl, b + 1)
                V.tensor_tensor(on[u][0:32, :], ps[0:32, 4, :], rl[32:64, :], ALU.mult)
                V.tensor_tensor(on[u][96:128, :], ps[96:128, 4, :], rl[64:96, :], ALU.mult).then_inc(s_on, 1)

            prepare(0, 0)
            prepare(1, 1)
            finish(0, 0, 0)
            prepare(2, 0)
            finish(1, 1, 0)
            with dve.Fori(1, B // 2 - 1) as i:
                prepare(2 * i + 1, 1)
                finish(2 * i, 0, 128 * i)
                prepare(2 * i + 2, 0)
                finish(2 * i + 1, 1, 128 * i)
            prepare(B - 1, 1)
            finish(B - 2, 0, 128 * (B // 2 - 1))
            finish(B - 1, 1, 128 * (B // 2 - 1))
            for q in range(2):
                dve.wait_ge(s_oh, q + 1)
                cols = slice(q * HT, (q + 1) * HT)
                for c in range(DC):
                    last = V.scalar_tensor_tensor(otl[:, c, cols], ot[:, c, cols], XS, oth[:, c, cols], ALU.mult,
                                                  ALU.subtract)
                last.then_inc(s_ol, 1)
            for t in range(8):
                dve.wait_ge(s_y, t + 1)
                V.scalar_tensor_tensor(x[:, t, :], ps[:, t % 2, :], UNS, x[:, t, :], ALU.mult, ALU.add).then_inc(s_x1, 1)

            for hf in range(2):
                layer_norm(1 + hf, 4, (2, 3), xbh, xbl, 4 * hf, lambda i: dve.wait_ge(s_x1, 4 * hf + i + 1))
                dve.wait_ge(s_pe1, 2 * hf + 2)
                y, e, r, kd = (cp[0:32, j, :] for j in range(4))
                if hf == 0:
                    link(V.memset(pd, 0.0))
                link(V.tensor_scalar(y, y, 0.11, None, ALU.min))
                link(V.tensor_scalar(r, y, LOG1P[-1], None, ALU.mult))
                for c in LOG1P[-2::-1]:
                    link(V.scalar_tensor_tensor(r, r, c, y, ALU.add, ALU.mult))
                link(V.tensor_scalar(pd[0:32, 0, :], r, 1e-4, 0.1, ALU.max, ALU.min))
                link(V.tensor_copy(pd[64:96, 2, :], pd[0:32, 0, :]))
                link(V.tensor_scalar(e, e, 1.0, None, ALU.add))
                link(V.reciprocal(kd, e))
                link(V.scalar_tensor_tensor(r, kd, 0.5, pd[0:32, 0, :], ALU.mult, ALU.mult))
                V.tensor_scalar(pd[32:64, 1, :], r, 1.0, None, ALU.add).then_inc(s_pdr, 1)

                def split_value(v):
                    dve.wait_ge(s_vhi, 8 * hf + v + 1)
                    V.scalar_tensor_tensor(vl[:, v, :], val[:, v, :], XS, vh[:, v, :], ALU.mult, ALU.subtract).then_inc(s_vlo, 1)

                def split_gated(v):
                    dve.wait_ge(s_ghi, 8 * hf + v + 1)
                    V.scalar_tensor_tensor(vl[:, v, :], val[:, v, :], XS, vh[:, v, :], ALU.mult, ALU.subtract).then_inc(s_glo, 1)

                for v in range(VC):
                    dve.wait_ge(s_vp, 8 * hf + v + 1)
                    wait(dve, s_silu, 8 * hf + v - 1)
                    o = raw[:, v % 2, :].rearrange("p (b t) -> p b t", b=HB)
                    src = ps[:, v % 2, :].rearrange("p (b t) -> p b t", b=HB)
                    link(V.tensor_scalar(o, src, conv_w[:, v, 3:4], None, ALU.mult))
                    for k in (2, 1, 0):
                        s = 3 - k
                        ins = V.scalar_tensor_tensor(o[:, :, s:T], src[:, :, 0:T - s], conv_w[:, v, k:k + 1], o[:, :, s:T],
                                                     ALU.mult, ALU.add)
                        if k:
                            link(ins)
                        else:
                            ins.then_inc(s_cv, 1)
                    if v:
                        split_value(v - 1)
                split_value(VC - 1)

                for gh in range(2):
                    dve.wait_ge(s_bcc, 12 * (2 * hf + gh + 1))
                    V.memset(psi[:, 0, :, 0], 0.0)
                    V.memset(psi[:, 1, :, 0], 1.0)
                    V.memset(psi[:, 2, :, 0], -1.0)
                    link(V.memset(psi[:, 3, :, 0], 0.0))
                    R0 = 4 * T * (2 * hf + gh)
                    cj = coef.rearrange("p j g (b t) -> p j (g b) t", b=HB)
                    nd4 = ndt.rearrange("p g (b t) -> p (g b) t", b=HB)

                    def step(t, r):
                        q, p = psi[:, 0:2, :, bass.ds(t, 1)], psi[:, 2:4, :, bass.ds(t, 1)]
                        q1, p1 = psi[:, 0:2, :, bass.ds(t + 1, 1)], psi[:, 2:4, :, bass.ds(t + 1, 1)]
                        c = cj[:, :, :, bass.ds(t, 1)]
                        sh = [P, 2, 2, NS]
                        pin = p.rearrange("p r s o -> p r (s o)")
                        qin = q.rearrange("p r s o -> p r (s o)")
                        cin = c.rearrange("p j s o -> p j (s o)")
                        nin = nd4[:, :, bass.ds(t, 1)].rearrange("p s o -> p (s o)")
                        V.tensor_tensor(rm, pin.unsqueeze(1).to_broadcast(sh), cin.unsqueeze(2).to_broadcast(sh),
                                        ALU.mult).then_inc(s_rec, 1)
                        V.tensor_tensor(rq, qin, nin.unsqueeze(1).to_broadcast([P, 2, NS]), ALU.mult).then_inc(s_rec, 1)
                        dve.wait_ge(s_rec, r + 1)
                        V.tensor_tensor(q1.rearrange("p r s o -> p r (s o)"), rm[:, 0], qin, ALU.add).then_inc(s_rec, 1)
                        dve.wait_ge(s_rec, r + 2)
                        V.tensor_tensor(p1.rearrange("p r s o -> p r (s o)"), rm[:, 1], rq, ALU.add).then_inc(s_rec, 1)
                        dve.wait_ge(s_rec, r + 4)

                    UN = 8
                    with dve.Fori(0, T // UN) as tb:
                        for k in range(UN):
                            step(tb * UN + k, R0 + tb * (4 * UN) + 4 * k)

                    def masked(g):
                        G = NG * hf + g
                        dve.wait_ge(s_k, G + 1)
                        wait(dve, s_yp, G)
                        V.tensor_tensor(kk.rearrange("p (n t) -> p n t", t=T),
                                        ps[:, 6:8, :].rearrange("p a (n t) -> p (a n) t", t=T),
                                        causal[:, :].unsqueeze(1).to_broadcast([P, 16, T]), ALU.mult).then_inc(s_kk, 1)

                    def outputs(g):
                        G = NG * hf + g
                        dve.wait_ge(s_yp, G + 1)
                        V.scalar_tensor_tensor(val[:, g, :], val[:, g, :], skip[:, g:g + 1], ps[:, 5, :], ALU.mult,
                                               ALU.add).then_inc(s_yv, 1)

                    def vectors(g):
                        G = NG * hf + g
                        gi = g % 4
                        sl = slice(gi * HB, (gi + 1) * HB)
                        bt4 = "p j (b t) -> p j b t"
                        q_, p_ = psi[:, 0:2, sl, 1:T + 1], psi[:, 2:4, sl, 1:T + 1]
                        q0, p0 = psi[:, 0:2, sl, 0:T], psi[:, 2:4, sl, 0:T]
                        full = [P, 2, HB, T]

                        def rows(a):
                            return a.rearrange("p (b t) -> p b t", b=HB).unsqueeze(1).to_broadcast(full)

                        def v4(a):
                            return a.rearrange(bt4, b=HB)

                        d1 = dd[:, 1, :].rearrange("p (b t) -> p b t", b=HB)
                        d0 = dd[:, 0, :].rearrange("p (b t) -> p b t", b=HB)
                        wait(dve, s_dinv, G)
                        V.tensor_tensor(d0, p_[:, 0], q_[:, 1], ALU.mult)
                        link(V.tensor_tensor(d1, p_[:, 1], q_[:, 0], ALU.mult))
                        V.tensor_tensor(d1, d1, d0, ALU.subtract).then_inc(s_det, 1)
                        dve.wait_ge(s_rn, 4 * G + 4)
                        link(V.tensor_tensor(raw, raw, rn, ALU.mult))
                        nd2 = ndt[:, gi, :].unsqueeze(1).to_broadcast([P, 2, HT])
                        link(V.tensor_tensor(t1, raw[:, 0:2, :], nd2, ALU.mult))
                        link(V.tensor_tensor(t2[:, 0, :], t1[:, 1, :], coef[:, 0, gi, :], ALU.mult))
                        link(V.tensor_tensor(t1[:, 0, :], t1[:, 0, :], t2[:, 0, :], ALU.add))
                        V.tensor_tensor(v4(bt), p0, rows(t1[:, 0, :]), ALU.mult)
                        link(V.tensor_tensor(v4(t2), q0, rows(t1[:, 1, :]), ALU.mult))
                        link(V.tensor_tensor(bt, bt, t2, ALU.add))
                        V.tensor_tensor(v4(t1), q_, rows(raw[:, 2, :]), ALU.mult)
                        link(V.tensor_tensor(v4(t2), p_, rows(raw[:, 3, :]), ALU.mult))
                        link(V.tensor_tensor(t1, t1, t2, ALU.subtract))
                        dve.wait_ge(s_dinv, G + 1)
                        V.tensor_tensor(ct, t1, dd, ALU.mult).then_inc(s_bt, 1)

                    g0 = 4 * gh
                    for g in range(g0, g0 + 4):
                        if g > g0 + 1:
                            outputs(g - 2)
                        if g > g0:
                            masked(g - 1)
                        vectors(g)
                    outputs(g0 + 2)
                    masked(g0 + 3)
                    outputs(g0 + 3)
                for v in range(VC):
                    dve.wait_ge(s_gs, 8 * hf + v + 1)
                    V.tensor_tensor(val[:, v, :], val[:, v, :], gate[:, v, :], ALU.mult).then_inc(s_gy, 1)
                    if v:
                        split_gated(v - 1)
                split_gated(VC - 1)
                for t in range(4):
                    dve.wait_ge(s_op, 4 * hf + t + 1)
                    tt = 4 * hf + t
                    V.scalar_tensor_tensor(x[:, tt, :], ps[:, t, :], UNS, x[:, tt, :], ALU.mult, ALU.add).then_inc(s_xo, 1)

            layer_norm(3, 8, (4, 5), xch, xcl, 0, lambda i: dve.wait_ge(s_xo, 8))
            dve.wait_ge(s_xx, 8)
            dve.wait_ge(s_cact, 4)
            V.tensor_scalar(p2d[0:NP, :], ident[0:NP, 0:NP], p2[:, 0:1], None, ALU.mult).then_inc(s_pb, 1)
            dve.wait_ge(s_pb, 2)
            V.tensor_copy(p2b, ps[:, 6, 0:NP]).then_inc(s_pb, 1)
            dve.wait_ge(s_pb, 3)
            sh3 = [P, 8, NP]
            link(V.tensor_tensor(fa, p2b.unsqueeze(1).to_broadcast(sh3), x2.unsqueeze(2).to_broadcast(sh3), ALU.add))
            dve.wait_ge(s_xp, 1)
            link(V.scalar_tensor_tensor(fa, ps[:, 7, 0:8 * NP].rearrange("p (t n) -> p t n", t=8), -2.0 * UNS, fa,
                                        ALU.mult, ALU.add))
            V.tensor_scalar(fa, fa, 0.0, None, ALU.max).then_inc(s_d2, 1)
            dve.wait_ge(s_d2, 1)
            link(V.tensor_scalar(nd, fa, -1.0, None, ALU.mult))
            for t in range(8):
                ins = V.max(top[:, t, :], nd[:, t, :])
            link(ins)
            for t in range(8):
                ins = V.max_index(topi[:, t, :], top[:, t, :], nd[:, t, :])
            link(ins)
            link(V.tensor_copy(topf, topi))
            dve.wait_ge(s_iota, 1)
            iob = io[:, :].unsqueeze(1).to_broadcast(sh3)
            V.tensor_tensor(m0, topf[:, :, 0:1].to_broadcast(sh3), iob, ALU.is_equal)
            link(V.tensor_tensor(m1, topf[:, :, 1:2].to_broadcast(sh3), iob, ALU.is_equal))
            link(V.tensor_tensor(m0, m0, m1, ALU.add))
            dve.wait_ge(s_sqd, 1)
            link(V.tensor_reduce(dm, ds, AX.X, ALU.min))
            V.tensor_tensor(ds, ds, dm.unsqueeze(2).to_broadcast(sh3), ALU.subtract).then_inc(s_dif, 1)
            dve.wait_ge(s_e, 1)
            link(V.tensor_tensor(ew, ew, m0, ALU.mult))
            link(V.tensor_reduce(es_sum, ew, AX.X, ALU.add))
            link(V.reciprocal(es_sum, es_sum))
            V.tensor_tensor(wn, ew, es_sum.unsqueeze(2).to_broadcast(sh3), ALU.mult).then_inc(s_wn, 1)
            dve.wait_ge(s_wn, 1)

            def weighted(t):
                dve.wait_ge(s_hp, t + 1)
                wait(dve, s_ht, t - 1)
                V.scalar_tensor_tensor(hw[:, t % 2, :].rearrange("p (n r) -> p n r", n=NP),
                                       ps[:, t % 2, :].rearrange("p (n r) -> p n r", n=NP), UNS,
                                       wn[:, t, :].unsqueeze(2).to_broadcast([P, NP, RK]), ALU.mult,
                                       ALU.mult).then_inc(s_hw, 1)

            weighted(0)
            for t in range(8):
                if t + 1 < 8:
                    weighted(t + 1)
                dve.wait_ge(s_hhi, t + 1)
                wait(dve, s_fp, t - 1)
                V.scalar_tensor_tensor(hl[:, t % 2, :, :], ps[:, 4 + t % 2, :].rearrange("p (c n) -> p c n", c=DC), XS,
                                       hh[:, t % 2, :, :], ALU.mult, ALU.subtract).then_inc(s_hlo, 1)
                dve.wait_ge(s_fp, t + 1)
                V.scalar_tensor_tensor(x[:, t, :], ps[:, 2 + t % 2, :], UNS, x[:, t, :], ALU.mult, ALU.add).then_inc(s_fo, 1)


def kernel(x, ctx_1024, L0_xattn_w_q, L0_xattn_w_kv, L0_xattn_w_concat, L0_attn_W_in, L0_attn_dw_weight, L0_attn_dw_bias,
           L0_attn_W_bc, L0_attn_W_out, L0_attn_skip, L0_attn_A_log, L0_attn_dt_bias, L0_ffn_prototypes, L0_ffn_B,
           L0_ffn_A, L0_ffn_bias, L0_ffn_temp):
    import concourse.bacc as bacc
    from concourse.bass_utils import run_bass_kernel_spmd

    a = np.asarray

    def lay(v, split, order, shape):
        return np.ascontiguousarray(a(v).reshape(split).transpose(order).reshape(shape))

    w_in = a(L0_attn_W_in)
    wkv = a(L0_xattn_w_kv).reshape(P, DC, 2, DH)
    chunk = (-1, P, CH)
    arrays = {
        "x": a(x).reshape(8, P, D),
        "ctx": lay(ctx_1024, (B, NKEY, P, DC), (0, 2, 3, 1), (B, P, DC, NKEY)),
        "w": np.concatenate([
            lay(L0_xattn_w_q, (DC, P, D), (1, 0, 2), chunk),
            lay(L0_xattn_w_concat, (DC, P, D), (1, 0, 2), chunk),
            lay(w_in[DI:2 * DI], (2, 512, DC, P), (0, 3, 2, 1), chunk),
            lay(L0_attn_W_bc, (NG, 4, 2, 2, SN, VC, P), (0, 2, 6, 5, 3, 1, 4), chunk),
            lay(w_in[0:DI], (2, 512, DC, P), (0, 3, 2, 1), chunk),
            lay(L0_attn_W_out, (D, 2, 4, P), (1, 3, 2, 0), chunk),
            lay(L0_ffn_B, (NP * RK, DC, P), (2, 1, 0), chunk),
            lay(L0_ffn_A, (NP, D, RK), (0, 2, 1), (DC, P, D)).transpose(1, 0, 2).reshape(chunk)]),
        "wkv": np.ascontiguousarray(wkv[:, :, [0, 0, 0, 1], :].reshape(P, DC, P)),
        "wp": lay(w_in[2 * DI:], (SH, 2, DC, P), (3, 2, 1, 0), (P, DC, 64)),
        "proto": a(L0_ffn_prototypes),
        "protot": lay(L0_ffn_prototypes, (NP, DC, P), (2, 1, 0), (P, DC, NP)),
        "bias": a(L0_ffn_bias),
        "conv": lay(L0_attn_dw_weight, (VC, P, 4), (1, 0, 2), (P, VC, 4)),
        "dwb": lay(L0_attn_dw_bias, (VC, P), (1, 0), (P, VC)),
        "skip": lay(L0_attn_skip, (VC, P), (1, 0), (P, VC)),
        "alog": a(L0_attn_A_log),
        "dtb": a(L0_attn_dt_bias).reshape(SH, 1),
        "temp": np.ascontiguousarray(np.broadcast_to(a(L0_ffn_temp).reshape(1, 1), (P, 1))),
    }
    nc = bacc.Bacc("TRN2", target_bir_lowering=False, num_devices=1)
    args = [nc.dram_tensor("in_" + k, v.shape, mybir.dt.from_np(v.dtype), kind="ExternalInput").ap() for k, v in arrays.items()]
    out = nc.dram_tensor("out_x", (8, P, D), F32, kind="ExternalOutput").ap()
    build(nc, *args, out)
    r = run_bass_kernel_spmd(nc, [{"in_" + k: v for k, v in arrays.items()}], core_ids=[0])
    return r.results[0]["out_x"].reshape(B, T, D)
```

```python
import numpy as np
import concourse.bass as bass
from concourse import mybir
from contextlib import ExitStack

F32 = mybir.dt.float32
F16 = mybir.dt.float16
U32 = mybir.dt.uint32
ALU = mybir.AluOpType
ACT = mybir.ActivationFunctionType
AX = mybir.AxisListType

P = 128
B, T, D = 16, 64, 512
TOK = B * T
NKEY = 1601
H, DH = 16, 32
DC = D // P
KT = -(-NKEY // P)
BLK = [(0, 401)] + [(401 + 400 * i, 400) for i in range(3)]
DI, SH, SN = 1024, 32, 32
VC = DI // P
NG = 8
HT = TOK // 2
HB = B // 2
PG = 2
NPASS = NG // PG
CS = 2
ST = T // CS
HS = HB * CS
NS = PG * HS
NP, RK = 32, 16
XS, WS = 16.0, 256.0
UNS = 1.0 / (XS * WS)
MS = 256.0
SC = 1.0 / (XS * XS * DH ** 0.5)
EPS = 1e-5
CH = D * D // P
HCHUNKS = 2 + 2 * NG + 2 + 2
SEQ = [0, 1] + 2 * list(range(2, 2 + HCHUNKS)) + [2 + HCHUNKS, 3 + HCHUNKS]
ITEMS = 36
V_STEP = 3
LOG1P = [(-1.0) ** (k + 1) / k for k in range(1, 9)]


def wait(eng, sem, n):
    if isinstance(n, int) and n <= 0:
        return
    eng.wait_ge(sem, n)


def build(nc, x_in, ctx_in, w_in, wkv_in, wp_in, proto_in, protot_in, bias_in, conv_in, dwb_in, skip_in, alog_in,
          dtb_in, temp_in, out):
    es = ExitStack()
    with es:
        def sb(name, shape, dt=F32):
            return es.enter_context(nc.sbuf_tensor(name, shape, dt))

        def sem(name):
            return es.enter_context(nc.semaphore(name))

        x = sb("x", [P, 8, D])
        ident = sb("ident", [P, P])
        ones = sb("ones", [P, P])
        head_ones = sb("head_ones", [P, P])
        causal = sb("causal", [P, T])
        wkv = sb("wkv", [P, DC, 2 * DH])
        wp = sb("wp", [P, DC, 64])
        wph, wpl = sb("wph", [P, DC, 64], F16), sb("wpl", [P, DC, 64], F16)
        sel = sb("sel", [P, 8 * P])
        alog = sb("alog", [SH, SN])
        amat = sb("amat", [SH, SN])
        dtb = sb("dtb", [SH, 1])
        conv_w = sb("conv_w", [P, VC, 4])
        conv_b = sb("conv_b", [P, VC])
        skip = sb("skip", [P, VC])
        proto_t = sb("proto_t", [P, DC, NP])
        pth, ptl = sb("pth", [P, DC, NP], F16), sb("ptl", [P, DC, NP], F16)
        p2 = sb("p2", [NP, 1])
        nit = sb("nit", [P, 4])
        stats = sb("stats", [P, 8, 6])
        mv = sb("mv", [P, 8, 2])
        std = sb("std", [P, 8])
        tiny = sb("tiny", [P, 2])
        io = sb("io", [P, NP])
        rstd = sb("rstd", [P, 8])
        wst = sb("wst", [P, 2, CH // 2])
        wh, wl = sb("wh", [P, 2, CH], F16), sb("wl", [P, 2, CH], F16)

        words = 39900
        arena = sb("arena", [P, words])
        cursor = [0]

        def carve(n, dt=F32):
            a = cursor[0]
            cursor[0] += n
            assert cursor[0] <= words, cursor
            v = arena[:, a:a + n]
            return v if dt == F32 else v.bitcast(dt)

        ctx = [carve(DC * NKEY).rearrange("p (c k) -> p c k", c=DC) for _ in range(2)]
        qs = carve(B * H * T // 2, F16)
        ks = [carve(802, F16) for _ in range(2)]
        vt = carve(1602)
        vv = [carve(KT * 96).rearrange("p (k n) -> p k n", k=KT) for _ in range(2)]
        pr = [carve(2 * 512) for _ in range(2)]
        ot = carve(DC * TOK).rearrange("p (c t) -> p c t", c=DC)
        rl = carve(512)
        on = [carve(512) for _ in range(2)]
        mxp = carve(8 * 4).rearrange("p (i k) -> p i k", i=8)
        mx = carve(8)
        eye8 = carve(8 * P)[0:8, :].rearrange("p (i n) -> p i n", i=8)
        xn_a = carve(2 * D).rearrange("p (u d) -> p u d", u=2)
        cursor[0] = DC * NKEY
        xah = carve(DC * TOK // 2, F16).rearrange("p (c t) -> p c t", c=DC)
        xal = carve(DC * TOK // 2, F16).rearrange("p (c t) -> p c t", c=DC)
        cursor[0] = 0
        oth = carve(DC * TOK // 2, F16).rearrange("p (c t) -> p c t", c=DC)
        otl = carve(DC * TOK // 2, F16).rearrange("p (c t) -> p c t", c=DC)
        assert cursor[0] <= DC * NKEY
        cursor[0] = 0
        xbh = carve(DC * HT // 2, F16).rearrange("p (c t) -> p c t", c=DC)
        xbl = carve(DC * HT // 2, F16).rearrange("p (c t) -> p c t", c=DC)
        val = carve(VC * HT).rearrange("p (v t) -> p v t", v=VC)
        vh = carve(VC * HT // 2, F16).rearrange("p (v t) -> p v t", v=VC)
        vl = carve(VC * HT // 2, F16).rearrange("p (v t) -> p v t", v=VC)
        ut = carve(4 * DI).rearrange("p (b i) -> p b i", b=4)
        coef = [carve(2 * PG * HT).rearrange("p (j g n) -> p j g n", j=2, g=PG) for _ in range(2)]
        ndt = [carve(PG * HT).rearrange("p (g n) -> p g n", g=PG) for _ in range(2)]
        psi0 = cursor[0]
        pw = 4 * NS * (ST + 1)
        psi_all = [carve(pw + 2) for _ in range(2)]
        psi = [a[:, 0:pw].rearrange("p (c s t) -> p c s t", c=4, s=NS) for a in psi_all]
        skew = [a.rearrange("p (j x) -> p j x", j=2)[:, :, 0:pw // 2].rearrange("p j (s t) -> p j s t", t=ST + 1)
                for a in psi_all]
        rm = carve(4 * NS).rearrange("p (j r s) -> p j r s", j=2, r=2)
        pd = carve(3 * HT).rearrange("p (j t) -> p j t", j=3)
        raw = carve(4 * HT).rearrange("p (j t) -> p j t", j=4)
        sq = [carve(HT) for _ in range(2)]
        rn = carve(4 * HT).rearrange("p (j t) -> p j t", j=4)
        cp = rn
        dd = [coef[u][:, 1, :, :] for u in range(2)]
        kk = carve(2 * HT)
        t1 = carve(2 * HT).rearrange("p (j t) -> p j t", j=2)
        t2 = carve(2 * HT).rearrange("p (j t) -> p j t", j=2)
        bt = carve(2 * HT).rearrange("p (j t) -> p j t", j=2)
        ct = t1
        xn_b = t1
        gate = arena[:, psi0:psi0 + VC * HT].rearrange("p (v t) -> p v t", v=VC)
        cursor[0] = 0
        xn_c = carve(2 * D).rearrange("p (u d) -> p u d", u=2)
        xch = carve(DC * TOK // 2, F16).rearrange("p (c t) -> p c t", c=DC)
        xcl = carve(DC * TOK // 2, F16).rearrange("p (c t) -> p c t", c=DC)
        proto = carve(D)[0:NP, :]
        ebias = carve(D)[0:NP, :]
        xsq = carve(D)
        x2 = carve(8)
        p2d = carve(NP)
        p2b = carve(NP)
        fa = carve(8 * NP).rearrange("p (t n) -> p t n", t=8)
        nd = carve(8 * NP).rearrange("p (t n) -> p t n", t=8)
        ds = carve(8 * NP).rearrange("p (t n) -> p t n", t=8)
        top = carve(8 * 8).rearrange("p (t n) -> p t n", t=8)
        topi = carve(8 * 8).rearrange("p (t n) -> p t n", t=8).bitcast(U32)
        topf = carve(8 * 8).rearrange("p (t n) -> p t n", t=8)
        dm = carve(8)
        m0 = carve(8 * NP).rearrange("p (t n) -> p t n", t=8)
        m1 = carve(8 * NP).rearrange("p (t n) -> p t n", t=8)
        ew = carve(8 * NP).rearrange("p (t n) -> p t n", t=8)
        es_sum = carve(8)
        wn = carve(8 * NP).rearrange("p (t n) -> p t n", t=8)
        hw = carve(2 * D).rearrange("p (u d) -> p u d", u=2)
        wt = carve(8 * P).rearrange("p (t n) -> p t n", t=8)
        hh = carve(2 * DC * P // 2, F16).rearrange("p (u c t) -> p u c t", u=2, c=DC)
        hl = carve(2 * DC * P // 2, F16).rearrange("p (u c t) -> p u c t", u=2, c=DC)

        ps = es.enter_context(nc.psum_tensor("ps", [P, 8, 512], F32))

        s_x, s_wkv, s_small, s_proto = sem("x_loaded"), sem("wkv_loaded"), sem("small_loaded"), sem("proto_loaded")
        s_late = sem("proto_rows_loaded")
        s_ctx = [sem("ctx0_loaded"), sem("ctx1_loaded")]
        s_wld = [sem("weight_piece0_loaded"), sem("weight_piece1_loaded")]
        s_whi, s_wsc, s_wlo = sem("weight_hi"), sem("weight_scaled"), sem("weight_lo")
        s_pool, s_dve, s_act = sem("pool_step"), sem("dve_step"), sem("act_step")
        s_const, s_cdve, s_cact = sem("pool_constants"), sem("dve_constants"), sem("act_constants")
        ln_sems = [[sem(f"ln{k}_{n}") for n in ("var", "std", "xn", "tr", "hi", "lo")] for k in range(4)]
        s_q, s_qhi, s_qlo = sem("q_products"), sem("q_hi"), sem("q_lo")
        s_item, s_itemfree, s_khi = sem("item_ready"), sem("item_used"), sem("k_hi")
        s_mx, s_s2, s_exp, s_pv = sem("maxima"), sem("scores"), sem("probs"), sem("probs_used")
        s_pvfree = sem("sums_copied")
        s_rl, s_on = sem("denominators"), sem("attn_normed")
        s_ot = [sem("attn_even_placed"), sem("attn_odd_placed")]
        s_oh, s_ol, s_y, s_x1 = sem("attn_hi"), sem("attn_lo"), sem("concat_products"), sem("x1")
        s_vp, s_cv, s_silu = sem("value_products"), sem("conv_done"), sem("value_f32")
        s_vhi, s_vlo = sem("value_hi"), sem("value_lo")
        s_ut, s_utc = sem("value_transposed"), sem("ut_ready")
        s_pp, s_pe1, s_pdr = sem("param_products"), sem("param_exp"), sem("dt_k_ready")
        s_bc, s_bcc = sem("coef_broadcast"), sem("coef_ready")
        s_rec = sem("recurrence_step")
        s_bp, s_raw = sem("bc_products"), sem("bc_copied")
        s_sq, s_ss, s_lg, s_rn = sem("bc_squared"), sem("sum_of_squares"), sem("norm_log"), sem("norm_ready")
        s_det, s_dinv = sem("determinant"), sem("inverse_determinant")
        s_bt, s_k, s_kk, s_yp, s_yv = sem("bt_ct_ready"), sem("kernel_products"), sem("kernel_masked"), sem("y_products"), sem("y_ready")
        s_kh, s_ye = sem("kernels_of_two_heads"), sem("y_of_even_batches")
        s_gp, s_gs, s_gy, s_ghi, s_glo = sem("gate_products"), sem("gate_silu"), sem("gated"), sem("gated_hi"), sem("gated_lo")
        s_oq, s_op, s_xo = sem("out_first_half"), sem("out_products"), sem("x2")
        s_xx, s_pb = sem("x_squares"), sem("p2_broadcast")
        s_xp, s_d2, s_sqd, s_dif, s_e, s_wn = sem("proto_products"), sem("dist2"), sem("dist"), sem("dist_shift"), sem("weights_exp"), sem("router_ready")
        s_iota = sem("iota")
        s_wtt, s_wt = sem("router_transposed"), sem("router_t")
        s_hp, s_hw, s_ht, s_hhi, s_hlo = sem("h_products"), sem("h_weighted"), sem("h_transposed"), sem("h_hi"), sem("h_lo")
        s_fp, s_fo, s_out = sem("ffn_products"), sem("x3"), sem("out_stored")

        block = es.enter_context(nc.Block())

        def chunk_at(half, n):
            return 2 + half * HCHUNKS + n

        def chunk_used(s):
            if s < 2:
                return (s_q, s_y)[s], 8
            half, n = divmod(s - 2, HCHUNKS)
            if half == 2:
                return (s_hp, s_fp)[n], 8
            if n < 2:
                return s_vp, 8 * half + 4 * (n + 1)
            if n < 2 + 2 * NG:
                return s_bp, 4 * NG * half + 2 * (n - 1)
            if n < 4 + 2 * NG:
                return s_gp, 8 * half + 4 * (n - 1 - 2 * NG)
            return (s_oq, s_op)[n - 4 - 2 * NG], 4 * (half + 1)

        def weights_there(pe, s):
            pe.wait_ge(s_wlo, 2 * (s + 1))

        def split3(pairs):
            (ah, al), (bh, bl) = pairs
            return [(ah, bh), (ah, bl), (al, bh)]

        @block.sync
        def _(sp):
            for t in range(8):
                sp.dma_start(x[:, t, :], x_in[t]).then_inc(s_x, 16)

            def weight_piece(q):
                wait(sp, s_wlo, q - 1)
                sp.dma_start(wst[:, q % 2, :], w_in[SEQ[q // 2], :, (q % 2) * (CH // 2):(q % 2 + 1) * (CH // 2)]
                             ).then_inc(s_wld[q % 2], 16)

            weight_piece(0)
            weight_piece(1)
            sp.dma_start(wkv[:, :, :], wkv_in).then_inc(s_wkv, 16)
            sp.dma_start(ctx[0], ctx_in[0]).then_inc(s_ctx[0], 16)
            for dst, src in ((wp[:, :, :], wp_in), (alog[:, :], alog_in), (dtb[:, :], dtb_in), (conv_w[:, :, :], conv_in),
                             (conv_b[:, :], dwb_in), (skip[:, :], skip_in)):
                sp.dma_start(dst, src).then_inc(s_small, 16)
            sp.dma_start(proto_t[:, :, :], protot_in).then_inc(s_proto, 16)
            sp.dma_start(nit[:, 0:1], temp_in).then_inc(s_proto, 16)
            for q in range(2, 6):
                weight_piece(q)
            sp.wait_ge(s_qlo, 8)
            wait(sp, s_q, 8)
            sp.dma_start(ctx[1], ctx_in[1]).then_inc(s_ctx[1], 16)

            def place(b, u):
                wait(sp, s_on, b + 1)
                for q in range(2):
                    src = on[u][96 * q:96 * q + 32, :].rearrange("p (m j t) -> p m j t", m=2, j=4)
                    for j in range(4):
                        sp.dma_start(ot[32 * j:32 * j + 32, 2 * q:2 * q + 2, bass.ds(b * T, T)], src[:, :, j, :]
                                     ).then_inc(s_ot[u], 16)

            def load_ctx(b, u):
                wait(sp, s_item, ITEMS * (b - 2) + 2)
                sp.dma_start(ctx[u], ctx_in[bass.ds(b, 1)].rearrange("a p c k -> p (a c) k")).then_inc(s_ctx[u], 16)

            load_ctx(2, 0)
            place(0, 0)
            load_ctx(3, 1)
            place(1, 1)
            with sp.Fori(1, B // 2 - 1) as i:
                load_ctx(2 * i + 2, 0)
                place(2 * i, 0)
                load_ctx(2 * i + 3, 1)
                place(2 * i + 1, 1)
            place(B - 2, 0)
            place(B - 1, 1)
            for q in range(6, 2 * len(SEQ)):
                weight_piece(q)
            sp.wait_ge(s_xo, 8)
            sp.dma_start(proto, proto_in).then_inc(s_late, 16)
            sp.dma_start(ebias, bias_in).then_inc(s_late, 16)
            for t in range(8):
                wait(sp, s_fo, t + 1)
                sp.dma_start(out[t], x[:, t, :]).then_inc(s_out, 16)
            sp.wait_ge(s_out, 8 * 16)

        @block.gpsimd
        def _(pool):
            n = [0]

            def link(ins):
                n[0] += 1
                ins.then_inc(s_pool, 1)
                pool.wait_ge(s_pool, n[0])

            nc.gpsimd.iota(io[:, :], pattern=[[1, NP]], base=0, channel_multiplier=0,
                           allow_small_or_imprecise_dtypes=True).then_inc(s_iota, 1)
            pool.wait_ge(s_iota, 1)
            link(nc.gpsimd.memset(ident[:, :], 0.0))
            link(nc.gpsimd.memset(causal[:, :], 1.0))
            link(nc.gpsimd.memset(eye8[:, :, :], 0.0))
            nc.gpsimd.affine_select(out=ident[:, :], in_=ident[:, :], compare_op=ALU.not_equal, fill=1.0, base=0,
                                    pattern=[[-1, P]], channel_multiplier=1).then_inc(s_const, 1)
            for e in range(2):
                pool.wait_ge(s_const, e + 1)
                v = causal[T * e:T * e + T, :]
                nc.gpsimd.affine_select(out=v, in_=v, compare_op=ALU.is_ge, fill=0.0, base=0,
                                        pattern=[[1, T]], channel_multiplier=-1).then_inc(s_const, 1)
            pool.wait_ge(s_const, 3)
            nc.gpsimd.affine_select(out=eye8[:, :, :], in_=eye8[:, :, :], compare_op=ALU.not_equal, fill=1.0 / MS,
                                    base=0, pattern=[[-1, 8], [0, P]], channel_multiplier=1).then_inc(s_const, 1)
            pool.wait_ge(s_const, 4)
            for q in range(2 * len(SEQ)):
                s, r = divmod(q, 2)
                st = wst[:, r, :]
                lo = slice(r * (CH // 2), (r + 1) * (CH // 2))
                pool.wait_ge(s_wld[r], 16 * (s + 1))
                if s >= 2:
                    pool.wait_ge(*chunk_used(s - 2))
                nc.gpsimd.tensor_scalar(wh[:, s % 2, lo], st, WS, 0.0, ALU.mult, ALU.add).then_inc(s_whi, 1)
                pool.wait_ge(s_whi, q + 1)
                nc.gpsimd.tensor_scalar(st, st, WS, 0.0, ALU.mult, ALU.add).then_inc(s_wsc, 1)
                pool.wait_ge(s_wsc, q + 1)
                nc.gpsimd.tensor_tensor(wl[:, s % 2, lo], st, wh[:, s % 2, lo], ALU.subtract).then_inc(s_wlo, 1)
                pool.wait_ge(s_wlo, q + 1)

        @block.tensor
        def _(pe):
            mm = nc.tensor.matmul

            def bank(b):
                return ps[:, b, :]

            def layer_norm(k, tiles, banks):
                var, stdd, xnr, tr, hi, lo = ln_sems[k]
                xn = (xn_a, xn_b, xn_b, xn_c)[k]
                for i in range(tiles):
                    pe.wait_ge(xnr, i + 1)
                    wait(pe, hi, i - 1)
                    wait(pe, lo, i - 1)
                    for c in range(DC):
                        last = nc.tensor.transpose(bank(banks[i % 2])[:, c * P:(c + 1) * P],
                                                   xn[:, i % 2, c * P:(c + 1) * P], ident[:, :])
                    last.then_inc(tr, 1)

            pe.wait_ge(s_const, 4)
            layer_norm(0, 8, (0, 1))
            W = wh[:, 0, :].rearrange("p (c n) -> p c n", c=DC), wl[:, 0, :].rearrange("p (c n) -> p c n", c=DC)
            weights_there(pe, 0)
            for u in range(8):
                n2, m = divmod(u, 4)
                pe.wait_ge(ln_sems[0][4], 4 * n2 + 4)
                pe.wait_ge(ln_sems[0][5], 4 * n2 + 4)
                wait(pe, s_qlo, u - 1)
                k = 0
                for a, b in ((W[0], xah), (W[0], xal), (W[1], xah)):
                    for c in range(DC):
                        last = mm(bank(2 + u % 2)[:, :], a[:, c, m * P:(m + 1) * P], b[:, c, n2 * HT:(n2 + 1) * HT],
                                  start=(k == 0), stop=(k == 3 * DC - 1))
                        k += 1
                last.then_inc(s_q, 1)

            def item_bank(b, p):
                wait(pe, s_itemfree, ITEMS * b + p - 2)
                return bank(5 + p % 3)

            def kv(b, u, p, first):
                if p == 0:
                    pe.wait_ge(s_ctx[u], first)
                o = item_bank(b, p)
                for c in range(DC):
                    for r in range(2):
                        k0, n = BLK[2 * p + r]
                        last = mm(o[64 * r:64 * r + 64, 0:n], wkv[:, c, :], ctx[u][:, c, k0:k0 + n],
                                  start=(c == 0), stop=(c == DC - 1))
                last.then_inc(s_item, 1)

            def v_there(b):
                item_bank(b, 2)
                wait(pe, s_khi, 4 * (b + 1))

            def v_turn(b):
                o = bank(7)
                for kt in range(KT):
                    nk = min(P, NKEY - kt * P)
                    last = nc.tensor.transpose(o[0:nk, 32 * kt:32 * kt + 32], vt[96:128, kt * P:kt * P + nk],
                                               ident[96:128, 96:128])
                last.then_inc(s_item, 1)

            def s1(b, u, i):
                for blk, (k0, n) in enumerate(BLK):
                    o = item_bank(b, 3 + 4 * i + blk)
                    if i == 0 and blk == 0:
                        wait(pe, s_itemfree, ITEMS * b + 2)
                    mm(o[:, 0:n], qs[0:96, bass.ds(b * 1024 + i * P, P)], ks[u][0:96, k0:k0 + n],
                       start=True, stop=True).then_inc(s_item, 1)

            def turn_max(b):
                o = item_bank(b, 35)
                wait(pe, s_mx, b + 1)
                nc.tensor.transpose(o[0:8, 0:P], mx, ident[:, :]).then_inc(s_item, 1)

            def prepare(b, u, kt, first):
                if kt < 2:
                    kv(b, u, kt, first)
                elif kt == V_STEP:
                    v_turn(b)
                elif V_STEP < kt <= V_STEP + 8:
                    s1(b, u, kt - V_STEP - 1)
                elif kt == KT - 1:
                    turn_max(b)

            def s2(b, u, kt):
                k = KT * b + kt
                s = (KT * u + kt) % 2
                nk = min(P, NKEY - kt * P)
                wait(pe, s_exp, k - 1)
                if kt == 0:
                    wait(pe, s_itemfree, ITEMS * (b + 1))
                for q in range(2):
                    last = mm(ps[0:nk, 2 * s + q, :], ks[u][0:104, kt * P:kt * P + nk],
                              qs[0:104, bass.ds(b * 1024 + q * 512, 512)], start=True, stop=True)
                last.then_inc(s_s2, 1)

            def pv(b, u, kt):
                k = KT * b + kt
                s = (KT * u + kt) % 2
                nk = min(P, NKEY - kt * P)
                wait(pe, s_exp, k + 1)
                if kt == 0:
                    wait(pe, s_pvfree, b)
                for q in range(2):
                    last = mm(ps[64 * q:64 * q + 64, 4, :], vv[u][0:nk, kt, 32 * q:32 * q + 64],
                              pr[s][0:nk, 512 * q:512 * q + 512], start=(kt == 0), stop=(kt == KT - 1))
                last.then_inc(s_pv, 1)

            def batch(b, u, nxt):
                s2(b, u, 0)
                for kt in range(KT):
                    if nxt is not None and kt == V_STEP:
                        v_there(b + 1)
                    if kt + 1 < KT:
                        s2(b, u, kt + 1)
                    if nxt is not None:
                        prepare(b + 1, 1 - u, kt, nxt)
                    pv(b, u, kt)

            pe.wait_ge(s_wkv, 16)
            wait(pe, s_qlo, 8)
            for kt in range(KT):
                if kt == V_STEP:
                    v_there(0)
                prepare(0, 0, kt, 16)
            batch(0, 0, 16)
            batch(1, 1, 32)
            with pe.Fori(1, B // 2 - 1) as i:
                batch(2 * i, 0, 16 * (i + 1))
                batch(2 * i + 1, 1, 16 * (i + 2))
            batch(B - 2, 0, 16 * (B // 2))
            batch(B - 1, 1, None)

            weights_there(pe, 1)
            Wc = wh[:, 1, :].rearrange("p (c n) -> p c n", c=DC), wl[:, 1, :].rearrange("p (c n) -> p c n", c=DC)
            for t in range(8):
                pe.wait_ge(s_oh, t // 4 + 1)
                pe.wait_ge(s_ol, t // 4 + 1)
                wait(pe, s_x1, t - 1)
                k = 0
                for a, b in ((oth, Wc[0]), (oth, Wc[1]), (otl, Wc[0])):
                    for c in range(DC):
                        last = mm(bank(t % 2), a[:, c, t * P:(t + 1) * P], b[:, c, :],
                                  start=(k == 0), stop=(k == 3 * DC - 1))
                        k += 1
                last.then_inc(s_y, 1)

            def wide(half, n, v, dst, done):
                s = chunk_at(half, n + v // 4)
                if v % 4 == 0:
                    weights_there(pe, s)
                hi = wh[:, s % 2, :].rearrange("p (c n) -> p c n", c=DC)
                lo = wl[:, s % 2, :].rearrange("p (c n) -> p c n", c=DC)
                cols = slice((v % 4) * P, (v % 4 + 1) * P)
                k = 0
                for a, b in ((hi, xbh), (hi, xbl), (lo, xbh)):
                    for c in range(DC):
                        last = mm(dst, a[:, c, cols], b[:, c, :], start=(k == 0), stop=(k == 3 * DC - 1))
                        k += 1
                last.then_inc(done, 1)

            for hf in range(2):
                if hf == 0:
                    pe.wait_ge(s_x1, 8)
                else:
                    pe.wait_ge(s_xo, 4)
                layer_norm(1 + hf, 4, (2, 3))
                pe.wait_ge(ln_sems[1 + hf][4], 4)
                pe.wait_ge(ln_sems[1 + hf][5], 4)
                pe.wait_ge(s_cact, 2)
                pe.wait_ge(s_cdve, 3)
                k = 0
                for a, b in ((wph, xbh), (wph, xbl), (wpl, xbh)):
                    for c in range(DC):
                        last = mm(ps[0:64, 4, :], a[:, c, :], b[:, c, :], start=(k == 0), stop=(k == 3 * DC - 1))
                        k += 1
                last.then_inc(s_pp, 1)
                for v in range(VC):
                    wait(pe, s_cv, 8 * hf + v - 1)
                    wide(hf, 0, v, bank(v % 2), s_vp)
                for n in range(8):
                    vq, bp = divmod(n, 4)
                    pe.wait_ge(s_silu, 8 * hf + 4 * vq + 4)
                    wait(pe, s_utc, 8 * hf + n - 1)
                    for c in range(4):
                        last = nc.tensor.transpose(bank(6 + n % 2)[:, c * P:(c + 1) * P],
                                                   val[:, 4 * vq + c, bp * P:(bp + 1) * P], ident[:, :])
                    last.then_inc(s_ut, 1)
                pe.wait_ge(s_vhi, 8 * (hf + 1))
                pe.wait_ge(s_vlo, 8 * (hf + 1))

                def bc(g, j):
                    G = NG * hf + g
                    s = chunk_at(hf, 2 + 2 * g + j // 2)
                    if j % 2 == 0:
                        weights_there(pe, s)
                    wait(pe, s_raw, 4 * (G - 1) + j + 1)
                    if j == 0 and g == 0:
                        wait(pe, s_cv, 8 * (hf + 1))
                    hi = wh[:, s % 2, :].rearrange("p (k j n) -> p k j n", k=VC, j=2)
                    lo = wl[:, s % 2, :].rearrange("p (k j n) -> p k j n", k=VC, j=2)
                    k = 0
                    for a, b in ((hi, vh), (hi, vl), (lo, vh)):
                        for c in range(VC):
                            last = mm(bank(j), a[:, c, j % 2, :], b[:, c, :], start=(k == 0), stop=(k == 3 * VC - 1))
                            k += 1
                    last.then_inc(s_bp, 1)

                def ss(g, j):
                    n = 4 * (NG * hf + g) + j
                    pe.wait_ge(s_sq, n + 1)
                    wait(pe, s_lg, n)
                    mm(bank(4), head_ones[:, :], sq[j % 2], start=True, stop=True).then_inc(s_ss, 1)

                def kernels(g):
                    G = NG * hf + g
                    pe.wait_ge(s_bt, G + 1)
                    wait(pe, s_kk, G)
                    for h in range(4):
                        if h == 2:
                            pe.wait_ge(s_kh, G + 1)
                        for bp in range(4):
                            col = (h % 2) * 512 + (h // 2) * 256 + bp * T
                            for e in range(2):
                                t0 = (2 * bp + e) * T
                                for j in range(2):
                                    last = mm(ps[T * e:T * e + T, 6 + col // 512, col % 512:col % 512 + T],
                                              bt[32 * h:32 * h + 32, j, t0:t0 + T], ct[32 * h:32 * h + 32, 1 - j, t0:t0 + T],
                                              start=(j == 0), stop=(j == 1))
                        if h == 1:
                            last.then_inc(s_kh, 1)
                    last.then_inc(s_k, 1)

                def outputs(g):
                    G = NG * hf + g
                    pe.wait_ge(s_kk, G + 1)
                    wait(pe, s_yv, G)
                    for e in range(2):
                        if e:
                            pe.wait_ge(s_ye, G + 1)
                        for bp in range(4):
                            for h in range(4):
                                t0 = (2 * bp + e) * T
                                col = (h % 2) * 512 + (h // 2) * 256 + bp * T
                                last = mm(ps[32 * h:32 * h + 32, 5, t0:t0 + T],
                                          ut[T * e:T * e + T, bp, g * P + 32 * h:g * P + 32 * h + 32],
                                          kk[T * e:T * e + T, col:col + T],
                                          start=True, stop=True)
                        if e == 0:
                            last.then_inc(s_ye, 1)
                    last.then_inc(s_yp, 1)

                def spread(p, m, o):
                    g, j = divmod(m, 3)
                    c0 = (PG * p + g) * P
                    mm(o, sel[:, c0:c0 + P], pd[:, j, :], start=True, stop=True).then_inc(s_bc, 1)

                wait(pe, s_pdr, hf + 1)
                wait(pe, s_utc, 8 * (hf + 1))
                for m in range(3 * PG):
                    wait(pe, s_bcc, 3 * PG * NPASS * hf + m - 1)
                    spread(0, m, bank(6 + m % 2))
                for g in range(NG):
                    bc(g, 0)
                    if g > 1:
                        outputs(g - 2)
                    bc(g, 1)
                    bc(g, 2)
                    p = g // PG + 1
                    if g % PG == 0 and p < NPASS:
                        wait(pe, s_kk, NG * hf + g - 1)
                        for m in range(3 * PG):
                            wait(pe, s_bcc, 3 * PG * (NPASS * hf + p) + m - 1)
                            spread(p, m, bank(6 + m % 2))
                        wait(pe, s_bcc, 3 * PG * (NPASS * hf + p + 1))
                    ss(g, 0)
                    ss(g, 1)
                    if g:
                        kernels(g - 1)
                    bc(g, 3)
                    ss(g, 2)
                    ss(g, 3)
                outputs(NG - 2)
                kernels(NG - 1)
                outputs(NG - 1)
                for v in range(VC):
                    wait(pe, s_gs, 8 * hf + v - 1)
                    wide(hf, 2 + 2 * NG, v, bank(v % 2), s_gp)
                for q in range(2):
                    s = chunk_at(hf, 4 + 2 * NG + q)
                    weights_there(pe, s)
                    hi = wh[:, s % 2, :].rearrange("p (k n) -> p k n", k=4)
                    lo = wl[:, s % 2, :].rearrange("p (k n) -> p k n", k=4)
                    pe.wait_ge(s_ghi, 8 * hf + 4 * q + 4)
                    pe.wait_ge(s_glo, 8 * hf + 4 * q + 4)
                    if q == 0:
                        wait(pe, s_gs, 8 * (hf + 1))
                    for t in range(4):
                        k = 0
                        for a, b in ((vh, hi), (vh, lo), (vl, hi)):
                            for c in range(4):
                                last = mm(bank(t), a[:, 4 * q + c, t * P:(t + 1) * P], b[:, c, :],
                                          start=(q == 0 and k == 0), stop=(q == 1 and k == 11))
                                k += 1
                        last.then_inc((s_oq, s_op)[q], 1)

            pe.wait_ge(s_xo, 8)
            layer_norm(3, 8, (4, 5))
            pe.wait_ge(s_pb, 1)
            mm(ps[:, 6, 0:NP], ones[0:NP, :], p2d[0:NP, :], start=True, stop=True).then_inc(s_pb, 1)
            pe.wait_ge(ln_sems[3][4], 8)
            pe.wait_ge(ln_sems[3][5], 8)
            for t in range(8):
                k = 0
                for a, b in ((xch, pth), (xch, ptl), (xcl, pth)):
                    for c in range(DC):
                        last = mm(ps[:, 7, t * NP:(t + 1) * NP], a[:, c, t * P:(t + 1) * P], b[:, c, :],
                                  start=(k == 0), stop=(k == 3 * DC - 1))
                        k += 1
            last.then_inc(s_xp, 1)
            sB, sA = len(SEQ) - 2, len(SEQ) - 1
            Wb = wh[:, sB % 2, :].rearrange("p (c n) -> p c n", c=DC), wl[:, sB % 2, :].rearrange("p (c n) -> p c n", c=DC)
            Wa = wh[:, sA % 2, :].rearrange("p (c n) -> p c n", c=DC), wl[:, sA % 2, :].rearrange("p (c n) -> p c n", c=DC)

            def h_tile(t):
                wait(pe, s_hw, t - 1)
                k = 0
                for a, b in ((xch, Wb[0]), (xch, Wb[1]), (xcl, Wb[0])):
                    for c in range(DC):
                        last = mm(bank(t % 2), a[:, c, t * P:(t + 1) * P], b[:, c, :], start=(k == 0), stop=(k == 3 * DC - 1))
                        k += 1
                last.then_inc(s_hp, 1)

            weights_there(pe, sB)
            h_tile(0)
            h_tile(1)
            pe.wait_ge(s_wn, 1)
            pe.wait_ge(s_pb, 3)
            for t in range(8):
                last = nc.tensor.transpose(ps[0:NP, 6, (t % 4) * P:(t % 4 + 1) * P], wn[:, t, :], ident[:, :])
                if t % 4 == 3:
                    last.then_inc(s_wtt, 1)
                    pe.wait_ge(s_wt, t // 4 + 1)
            weights_there(pe, sA)
            pe.wait_ge(s_late, 32)
            for t in range(8):
                pe.wait_ge(s_hw, t + 1)
                wait(pe, s_hhi, t - 1)
                wait(pe, s_hlo, t - 1)
                for c in range(DC):
                    last = nc.tensor.transpose(bank(4 + t % 2)[:, c * P:(c + 1) * P], hw[:, t % 2, c * P:(c + 1) * P], ident[:, :])
                last.then_inc(s_ht, 1)
                if t + 2 < 8:
                    h_tile(t + 2)
                wait(pe, s_fo, t - 1)
                o = bank(2 + t % 2)
                mm(o, wt[0:NP, t, :], ebias, start=True, stop=False)
                pe.wait_ge(s_hhi, t + 1)
                pe.wait_ge(s_hlo, t + 1)
                k = 0
                for a, b in ((hh, Wa[0]), (hh, Wa[1]), (hl, Wa[0])):
                    for c in range(DC):
                        last = mm(o, a[:, t % 2, c, :], b[:, c, :], start=False, stop=(k == 3 * DC - 1))
                        k += 1
                last.then_inc(s_fp, 1)

        @block.scalar
        def _(act):
            n = [0]
            f = nc.scalar.activation

            def link(ins):
                n[0] += 1
                ins.then_inc(s_act, 1)
                act.wait_ge(s_act, n[0])

            def layer_norm(k, tiles, banks, hi_t):
                var, stdd, xnr, tr, hi, lo = ln_sems[k]
                act.wait_ge(var, 1)
                f(std[:, 0:tiles], rstd[:, 0:tiles], ACT.Sqrt).then_inc(stdd, 1)
                for i in range(tiles):
                    act.wait_ge(tr, i + 1)
                    src = ps[:, banks[i % 2], :].rearrange("p (c t) -> p c t", c=DC)
                    if k == 3:
                        wait(act, s_xx, i)
                        f(xsq, xn_c[:, i % 2, :], ACT.Square, accum_out=x2[:, i:i + 1]).then_inc(s_xx, 1)
                    f(hi_t[:, :, i * P:(i + 1) * P], src, ACT.Copy, scale=XS).then_inc(hi, 1)

            layer_norm(0, 8, (0, 1), xah)
            nc.scalar.preload_act_table_set("natural_log_exp_and_others")
            act.wait_ge(s_small, 6 * 16)
            act.wait_ge(s_proto, 2 * 16)
            f(amat[:, :], alog[:, :], ACT.Exp).then_inc(s_cact, 1)
            f(wph[:, :, :], wp[:, :, :], ACT.Copy, scale=WS).then_inc(s_cact, 1)
            f(pth[:, :, :], proto_t[:, :, :], ACT.Copy, scale=WS).then_inc(s_cact, 1)
            for u in range(8):
                n2, m = divmod(u, 4)
                act.wait_ge(s_q, u + 1)
                for j in range(4):
                    dst = qs[0:32, :].rearrange("p (b h t) -> p b h t", b=B, h=H)[:, n2 * HB:(n2 + 1) * HB, 4 * m + j, :]
                    last = f(dst, ps[32 * j:32 * j + 32, 2 + u % 2, :].rearrange("p (b t) -> p b t", b=HB), ACT.Copy,
                             scale=1.0 / WS)
                last.then_inc(s_qhi, 1)

            def kv(b, u, p):
                if p == 0:
                    wait(act, s_pv, KT * (b - 1))
                act.wait_ge(s_item, ITEMS * b + p + 1)
                for r in range(2):
                    k0, w = BLK[2 * p + r]
                    f(ks[u][0:32, k0:k0 + w], ps[64 * r:64 * r + 32, 5 + p, 0:w], ACT.Copy, scale=XS)
                    f(vt[96:128, k0:k0 + w], ps[64 * r + 32:64 * r + 64, 5 + p, 0:w], ACT.Copy).then_inc(s_khi, 1)

            def probs(b, u, kt):
                k = KT * b + kt
                s = (KT * u + kt) % 2
                nk = min(P, NKEY - kt * P)
                wait(act, s_pv, k - 1)
                act.wait_ge(s_s2, k + 1)
                f(pr[s][0:nk, :].rearrange("p (q n) -> p q n", q=2), ps[0:nk, 2 * s:2 * s + 2, :], ACT.Exp,
                  scale=SC).then_inc(s_exp, 1)

            def batch(b, u, more):
                for kt in range(KT):
                    probs(b, u, kt)
                    if more and kt < 2:
                        kv(b + 1, 1 - u, kt)

            act.wait_ge(s_cdve, 4)
            for p in range(2):
                kv(0, 0, p)
            batch(0, 0, True)
            batch(1, 1, True)
            with act.Fori(1, B // 2 - 1) as i:
                batch(2 * i, 0, True)
                batch(2 * i + 1, 1, True)
            batch(B - 2, 0, True)
            batch(B - 1, 1, False)
            for u in range(2):
                act.wait_ge(s_ot[u], 8 * 16 * B // 2)
            for q in range(2):
                f(oth[:, :, q * HT:(q + 1) * HT], ot[:, :, q * HT:(q + 1) * HT], ACT.Copy, scale=XS).then_inc(s_oh, 1)

            for hf in range(2):
                layer_norm(1 + hf, 4, (2, 3), xbh)
                nc.scalar.preload_act_table_set("natural_log_exp_and_others")
                act.wait_ge(s_pp, hf + 1)
                f(cp[0:32, 0, :], ps[0:32, 4, :], ACT.Exp, bias=dtb[:, 0:1], scale=UNS).then_inc(s_pe1, 1)
                f(cp[0:32, 1, :], ps[32:64, 4, :], ACT.Exp, scale=-UNS).then_inc(s_pe1, 1)
                for v in range(VC):
                    act.wait_ge(s_cv, 8 * hf + v + 1)
                    f(val[:, v, :], raw[:, v % 2, :], ACT.Silu, bias=conv_b[:, v:v + 1], scale=UNS).then_inc(s_silu, 1)
                    act.wait_ge(s_silu, 8 * hf + v + 1)
                    f(vh[:, v, :], val[:, v, :], ACT.Copy, scale=XS).then_inc(s_vhi, 1)
                for m in range(8):
                    vq, bp = divmod(m, 4)
                    act.wait_ge(s_ut, 8 * hf + m + 1)
                    f(ut[:, bp, 512 * vq:512 * vq + 512], ps[:, 6 + m % 2, :], ACT.Copy).then_inc(s_utc, 1)
                nc.scalar.preload_act_table_set("natural_log_exp_and_others")
                def spread(p, m, b):
                    g, j = divmod(m, 3)
                    act.wait_ge(s_bc, 3 * PG * (NPASS * hf + p) + m + 1)
                    dst = coef[p % 2][:, j, g, :] if j < 2 else ndt[p % 2][:, g, :]
                    f(dst, ps[:, b, :], ACT.Copy).then_inc(s_bcc, 1)

                for m in range(3 * PG):
                    spread(0, m, 6 + m % 2)
                for g in range(NG):
                    G = NG * hf + g
                    p = g // PG + 1
                    wait(act, s_bt, G)

                    def norm(j):
                        N = 4 * G + j
                        r = rn[:, j, :]
                        act.wait_ge(s_ss, N + 1)
                        f(r, ps[:, 4, :], ACT.Ln, bias=tiny[:, 0:1]).then_inc(s_lg, 1)
                        act.wait_ge(s_lg, N + 1)
                        link(f(r, r, ACT.Exp, scale=0.5))
                        link(f(r, r, ACT.Ln, bias=tiny[:, 1:2]))
                        f(r, r, ACT.Exp, scale=-1.0).then_inc(s_rn, 1)

                    for j in range(4):
                        N = 4 * G + j
                        act.wait_ge(s_bp, N + 1)
                        wait(act, s_ss, N - 1)
                        f(sq[j % 2], ps[:, j, :], ACT.Square, scale=UNS).then_inc(s_sq, 1)
                        f(raw[:, j, :], ps[:, j, :], ACT.Copy, scale=UNS).then_inc(s_raw, 1)
                        if j == 1:
                            if g % PG == 0 and p < NPASS:
                                for m in range(3 * PG):
                                    spread(p, m, 6 + m % 2)
                            norm(0)
                            norm(1)
                    norm(2)
                    norm(3)
                    d = dd[(p - 1) % 2]
                    act.wait_ge(s_det, G + 1)
                    link(f(d[:, 1, :], d[:, 1, :], ACT.Ln))
                    link(f(d[:, 1, :], d[:, 1, :], ACT.Exp, scale=-1.0))
                    f(d[:, 0, :], d[:, 1, :], ACT.Copy, scale=-1.0).then_inc(s_dinv, 1)
                for v in range(VC):
                    act.wait_ge(s_gp, 8 * hf + v + 1)
                    wait(act, s_bt, 8 * hf + 8)
                    f(gate[:, v, :], ps[:, v % 2, :], ACT.Silu, scale=UNS).then_inc(s_gs, 1)
                for v in range(VC):
                    act.wait_ge(s_gy, 8 * hf + v + 1)
                    f(vh[:, v, :], val[:, v, :], ACT.Copy, scale=XS).then_inc(s_ghi, 1)

            layer_norm(3, 8, (4, 5), xch)
            act.wait_ge(s_xx, 8)
            act.wait_ge(s_late, 32)
            f(xsq[0:NP, :], proto, ACT.Square, accum_out=p2[:, :]).then_inc(s_cact, 1)
            act.wait_ge(s_d2, 1)
            f(ds, fa, ACT.Sqrt).then_inc(s_sqd, 1)
            act.wait_ge(s_dif, 1)
            f(ew, ds, ACT.Exp, scale=nit[:, 3:4]).then_inc(s_e, 1)
            for q in range(2):
                act.wait_ge(s_wtt, q + 1)
                f(wt[0:NP, 4 * q:4 * q + 4, :], ps[0:NP, 6, :].rearrange("p (t n) -> p t n", t=4), ACT.Copy,
                  scale=XS * WS).then_inc(s_wt, 1)
            for t in range(8):
                act.wait_ge(s_ht, t + 1)
                wait(act, s_fp, t - 1)
                f(hh[:, t % 2, :, :], ps[:, 4 + t % 2, :].rearrange("p (c n) -> p c n", c=DC), ACT.Copy,
                  scale=XS).then_inc(s_hhi, 1)

        @block.vector
        def _(dve):
            n = [0]
            V = nc.vector

            def link(ins):
                n[0] += 1
                ins.then_inc(s_dve, 1)
                dve.wait_ge(s_dve, n[0])

            def layer_norm(k, tiles, banks, hi_t, lo_t, t0, ready):
                var, stdd, xnr, tr, hi, lo = ln_sems[k]
                xn = (xn_a, xn_b, xn_b, xn_c)[k]
                for i in range(tiles):
                    ready(i)
                    link(V.bn_stats(stats[:, i, :], x[:, t0 + i, :]))
                    link(V.bn_aggr(mv[:, i, :], stats[:, i, :]))
                V.tensor_scalar(rstd[:, 0:tiles], mv[:, 0:tiles, 1], EPS, None, ALU.add).then_inc(var, 1)
                dve.wait_ge(stdd, 1)
                link(V.reciprocal(rstd[:, 0:tiles], std[:, 0:tiles]))

                def normed(i):
                    wait(dve, tr, i - 1)
                    if k == 3:
                        wait(dve, s_xx, i - 1)
                    V.tensor_scalar(xn[:, i % 2, :], x[:, t0 + i, :], mv[:, i, 0:1], rstd[:, i:i + 1],
                                    ALU.subtract, ALU.mult).then_inc(xnr, 1)

                normed(0)
                for i in range(tiles):
                    if i + 1 < tiles:
                        normed(i + 1)
                    dve.wait_ge(tr, i + 1)
                    dve.wait_ge(hi, i + 1)
                    src = ps[:, banks[i % 2], :].rearrange("p (c t) -> p c t", c=DC)
                    cols = slice(i * P, (i + 1) * P)
                    V.scalar_tensor_tensor(lo_t[:, :, cols], src, XS, hi_t[:, :, cols], ALU.mult,
                                           ALU.subtract).then_inc(lo, 1)

            link(V.memset(tiny[:, 0:1], 1e-19))
            link(V.memset(tiny[:, 1:2], 1e-8))
            link(V.memset(head_ones[:, :], 0.0))
            for h in range(4):
                link(V.memset(head_ones[32 * h:32 * h + 32, 32 * h:32 * h + 32], 1.0))
            link(V.memset(ones[:, :], 1.0))
            link(V.memset(sel[:, :], 0.0))

            layer_norm(0, 8, (0, 1), xah, xal, 0, lambda i: dve.wait_ge(s_x, 16 * 8))
            dve.wait_ge(s_const, 4)
            dve.wait_ge(s_cact, 3)
            dve.wait_ge(s_proto, 2 * 16)
            diag = ident[0:32, 0:32].unsqueeze(2).to_broadcast([32, 32, 32])
            hv = "p (h n) -> p h n"
            V.tensor_tensor(sel[0:32, :].rearrange(hv, h=32), amat[:, :].unsqueeze(1).to_broadcast([32, 32, 32]), diag,
                            ALU.mult).then_inc(s_cdve, 1)
            V.tensor_copy(sel[32:64, :].rearrange(hv, h=32), diag)
            V.tensor_scalar(sel[64:96, :].rearrange(hv, h=32), diag, -1.0, None, ALU.mult).then_inc(s_cdve, 1)
            V.scalar_tensor_tensor(wpl[:, :, :], wp[:, :, :], WS, wph[:, :, :], ALU.mult, ALU.subtract).then_inc(s_cdve, 1)
            V.scalar_tensor_tensor(ptl[:, :, :], proto_t[:, :, :], WS, pth[:, :, :], ALU.mult, ALU.subtract)
            link(V.tensor_scalar(nit[:, 1:2], nit[:, 0:1], -1.0, None, ALU.mult))
            link(V.tensor_tensor(nit[:, 1:2], nit[:, 0:1], nit[:, 1:2], ALU.max))
            link(V.tensor_scalar(nit[:, 1:2], nit[:, 1:2], 0.1, None, ALU.max))
            link(V.reciprocal(nit[:, 2:3], nit[:, 1:2]))
            link(V.tensor_scalar(nit[:, 3:4], nit[:, 2:3], -1.0, None, ALU.mult))
            for u in range(2):
                V.memset(vv[u][:, :, 32:64], 1.0)
                last = V.memset(ks[u][96:104, 0:NKEY], MS)
            last.then_inc(s_cdve, 1)
            for u in range(8):
                n2, m = divmod(u, 4)
                dve.wait_ge(s_qhi, u + 1)
                view = [qs[32 * r:32 * r + 32, :].rearrange("p (b h t) -> p b h t", b=B, h=H)[:, n2 * HB:(n2 + 1) * HB]
                        for r in range(3)]
                for j in range(4):
                    h = 4 * m + j
                    V.tensor_copy(view[1][:, :, h, :], view[0][:, :, h, :])
                    last = V.scalar_tensor_tensor(view[2][:, :, h, :], ps[32 * j:32 * j + 32, 2 + u % 2, :].rearrange(
                        "p (b t) -> p b t", b=HB), 1.0 / WS, view[0][:, :, h, :], ALU.mult, ALU.subtract)
                last.then_inc(s_qlo, 1)

            def prepare(b, u):
                for p, (k0, w) in enumerate(BLK):
                    r = p % 2
                    dve.wait_ge(s_khi, 4 * b + p + 1)
                    last = V.scalar_tensor_tensor(ks[u][32:64, k0:k0 + w], ps[64 * r:64 * r + 32, 5 + p // 2, 0:w], XS,
                                                  ks[u][0:32, k0:k0 + w], ALU.mult, ALU.subtract)
                    last = V.tensor_copy(ks[u][64:96, k0:k0 + w], ks[u][0:32, k0:k0 + w])
                    if r:
                        last.then_inc(s_itemfree, 1)
                dve.wait_ge(s_item, ITEMS * b + 3)
                wait(dve, s_pv, KT * (b - 1))
                vp = ps[:, 7, 0:KT * 32].rearrange("p (k n) -> p k n", k=KT)
                for c0 in (0, 64):
                    V.tensor_copy(vv[u][:, 0:KT - 1, c0:c0 + 32], vp[:, 0:KT - 1, :])
                    nk = NKEY - (KT - 1) * P
                    last = V.tensor_copy(vv[u][0:nk, KT - 1, c0:c0 + 32], vp[0:nk, KT - 1, :])
                last.then_inc(s_itemfree, 1)
                for i in range(8):
                    for k, (k0, w) in enumerate(BLK):
                        p = 3 + 4 * i + k
                        dve.wait_ge(s_item, ITEMS * b + p + 1)
                        V.tensor_reduce(mxp[:, i, k:k + 1], ps[:, 5 + p % 3, 0:w], AX.X, ALU.max).then_inc(s_itemfree, 1)
                dve.wait_ge(s_itemfree, ITEMS * b + 35)
                V.tensor_reduce(mx, mxp, AX.X, ALU.max, negate=True).then_inc(s_mx, 1)
                dve.wait_ge(s_item, ITEMS * b + 36)
                V.tensor_tensor(qs[96:104, bass.ds(b * 1024, 1024)].rearrange("p (i n) -> p i n", i=8),
                                ps[0:8, 7, 0:P].unsqueeze(1).to_broadcast([8, 8, P]), eye8[:, :, :],
                                ALU.mult).then_inc(s_itemfree, 1)

            def finish(b, u, placed):
                dve.wait_ge(s_pv, KT * (b + 1))
                wait(dve, s_ot[u], placed)
                V.tensor_copy(on[u], ps[:, 4, :]).then_inc(s_pvfree, 1)
                dve.wait_ge(s_pvfree, b + 1)
                V.reciprocal(rl, on[u]).then_inc(s_rl, 1)
                dve.wait_ge(s_rl, 2 * b + 1)
                V.tensor_copy(rl[0:32, :], rl[32:64, :])
                V.tensor_copy(rl[96:128, :], rl[64:96, :]).then_inc(s_rl, 1)
                dve.wait_ge(s_rl, 2 * b + 2)
                V.tensor_tensor(on[u][0:32, :], on[u][0:32, :], rl[0:32, :], ALU.mult)
                V.tensor_tensor(on[u][96:128, :], on[u][96:128, :], rl[96:128, :], ALU.mult).then_inc(s_on, 1)

            prepare(0, 0)
            prepare(1, 1)
            finish(0, 0, 0)
            prepare(2, 0)
            finish(1, 1, 0)
            with dve.Fori(1, B // 2 - 1) as i:
                prepare(2 * i + 1, 1)
                finish(2 * i, 0, 128 * i)
                prepare(2 * i + 2, 0)
                finish(2 * i + 1, 1, 128 * i)
            prepare(B - 1, 1)
            finish(B - 2, 0, 128 * (B // 2 - 1))
            finish(B - 1, 1, 128 * (B // 2 - 1))
            for q in range(2):
                dve.wait_ge(s_oh, q + 1)
                cols = slice(q * HT, (q + 1) * HT)
                for c in range(DC):
                    last = V.scalar_tensor_tensor(otl[:, c, cols], ot[:, c, cols], XS, oth[:, c, cols], ALU.mult,
                                                  ALU.subtract)
                last.then_inc(s_ol, 1)
            for t in range(8):
                dve.wait_ge(s_y, t + 1)
                V.scalar_tensor_tensor(x[:, t, :], ps[:, t % 2, :], UNS, x[:, t, :], ALU.mult, ALU.add).then_inc(s_x1, 1)

            for hf in range(2):
                layer_norm(1 + hf, 4, (2, 3), xbh, xbl, 4 * hf, lambda i: dve.wait_ge(s_x1, 4 * hf + i + 1))
                dve.wait_ge(s_pe1, 2 * hf + 2)
                y, e, r, kd = (cp[0:32, j, :] for j in range(4))
                if hf == 0:
                    link(V.memset(pd, 0.0))
                link(V.tensor_scalar(y, y, 0.11, None, ALU.min))
                link(V.tensor_scalar(r, y, LOG1P[-1], None, ALU.mult))
                for c in LOG1P[-2::-1]:
                    link(V.scalar_tensor_tensor(r, r, c, y, ALU.add, ALU.mult))
                link(V.tensor_scalar(pd[0:32, 0, :], r, 1e-4, 0.1, ALU.max, ALU.min))
                link(V.tensor_copy(pd[64:96, 2, :], pd[0:32, 0, :]))
                link(V.tensor_scalar(e, e, 1.0, None, ALU.add))
                link(V.reciprocal(kd, e))
                link(V.scalar_tensor_tensor(r, kd, 0.5, pd[0:32, 0, :], ALU.mult, ALU.mult))
                V.tensor_scalar(pd[32:64, 1, :], r, 1.0, None, ALU.add).then_inc(s_pdr, 1)

                def split_value(v):
                    dve.wait_ge(s_vhi, 8 * hf + v + 1)
                    V.scalar_tensor_tensor(vl[:, v, :], val[:, v, :], XS, vh[:, v, :], ALU.mult, ALU.subtract).then_inc(s_vlo, 1)

                def split_gated(v):
                    dve.wait_ge(s_ghi, 8 * hf + v + 1)
                    V.scalar_tensor_tensor(vl[:, v, :], val[:, v, :], XS, vh[:, v, :], ALU.mult, ALU.subtract).then_inc(s_glo, 1)

                for v in range(VC):
                    dve.wait_ge(s_vp, 8 * hf + v + 1)
                    wait(dve, s_silu, 8 * hf + v - 1)
                    o = raw[:, v % 2, :].rearrange("p (b t) -> p b t", b=HB)
                    src = ps[:, v % 2, :].rearrange("p (b t) -> p b t", b=HB)
                    link(V.tensor_scalar(o, src, conv_w[:, v, 3:4], None, ALU.mult))
                    for k in (2, 1, 0):
                        s = 3 - k
                        ins = V.scalar_tensor_tensor(o[:, :, s:T], src[:, :, 0:T - s], conv_w[:, v, k:k + 1], o[:, :, s:T],
                                                     ALU.mult, ALU.add)
                        if k:
                            link(ins)
                        else:
                            ins.then_inc(s_cv, 1)
                    if v:
                        split_value(v - 1)
                split_value(VC - 1)

                def start(p):
                    w = psi[p % 2].rearrange("p c (s k) t -> p c s k t", k=CS)
                    last = None
                    for c, first, then in ((0, 0.0, 1.0), (1, 1.0, 0.0), (2, -1.0, 0.0), (3, 0.0, 1.0)):
                        V.memset(w[:, c, :, 0, 0], first)
                        last = V.memset(w[:, c, :, 1, 0], then)
                    link(last)
                    dve.wait_ge(s_bcc, 3 * PG * (NPASS * hf + p + 1))

                def recur(p, t0, t1):
                    w, sk = psi[p % 2], skew[p % 2]
                    R0 = 3 * ST * (NPASS * hf + p) + 3 * t0
                    cj = coef[p % 2].rearrange("p j g (b t) -> p j (g b) t", t=ST)
                    nd4 = ndt[p % 2].rearrange("p g (b t) -> p (g b) t", t=ST)
                    sh = [P, 2, 2, NS]

                    def at(a, t):
                        return a[:, :, :, bass.ds(t, 1)].rearrange("p r s o -> p r (s o)")

                    def step(t, r):
                        q, p_, c = at(w[:, 0:2], t), at(w[:, 2:4], t), at(cj, t)
                        n_ = nd4[:, :, bass.ds(t, 1)].rearrange("p s o -> p (s o)")
                        V.tensor_tensor(rm, p_.unsqueeze(1).to_broadcast(sh), c.unsqueeze(2).to_broadcast(sh),
                                        ALU.mult).then_inc(s_rec, 1)
                        V.tensor_tensor(at(w[:, 2:4], t + 1), q, n_.unsqueeze(1).to_broadcast([P, 2, NS]),
                                        ALU.mult).then_inc(s_rec, 1)
                        dve.wait_ge(s_rec, r + 2)
                        V.tensor_tensor(w[:, :, :, bass.ds(t + 1, 1)].rearrange("p (j r) s o -> p j (r s o)", j=2),
                                        rm.rearrange("p j r s -> p j (r s)"), at(sk, t), ALU.add).then_inc(s_rec, 1)
                        dve.wait_ge(s_rec, r + 3)

                    UN = 8
                    with dve.Fori(0, (t1 - t0) // UN) as tb:
                        for k in range(UN):
                            step(tb * UN + (t0 + k), R0 + tb * (3 * UN) + 3 * k)

                def join(g):
                    gi = g % PG
                    w = psi[g // PG % 2][:, :, gi * HS:(gi + 1) * HS].rearrange("p c (s k) t -> p c s k t", k=CS)
                    sh = [P, 2, HB, ST]
                    a, b = (t2[:, k, :].rearrange("p (r s t) -> p r s t", r=2, t=ST) for k in range(2))
                    for c in range(2):
                        V.tensor_tensor(a, w[:, 2 * c, :, 1, 1:].unsqueeze(1).to_broadcast(sh),
                                        w[:, 0:2, :, 0, ST:].to_broadcast(sh), ALU.mult)
                        link(V.tensor_tensor(b, w[:, 2 * c + 1, :, 1, 1:].unsqueeze(1).to_broadcast(sh),
                                             w[:, 2:4, :, 0, ST:].to_broadcast(sh), ALU.mult))
                        link(V.tensor_tensor(w[:, 2 * c:2 * c + 2, :, 1, 1:], a, b, ALU.add))
                    link(V.tensor_copy(w[:, :, :, 1, 0], w[:, :, :, 0, ST]))

                start(0)
                recur(0, 0, ST)

                def masked(g):
                    G = NG * hf + g
                    dve.wait_ge(s_k, G + 1)
                    wait(dve, s_yp, G)
                    V.tensor_tensor(kk.rearrange("p (n t) -> p n t", t=T),
                                    ps[:, 6:8, :].rearrange("p a (n t) -> p (a n) t", t=T),
                                    causal[:, :].unsqueeze(1).to_broadcast([P, 16, T]), ALU.mult).then_inc(s_kk, 1)

                def outputs(g):
                    G = NG * hf + g
                    dve.wait_ge(s_yp, G + 1)
                    V.scalar_tensor_tensor(val[:, g, :], val[:, g, :], skip[:, g:g + 1], ps[:, 5, :], ALU.mult,
                                           ALU.add).then_inc(s_yv, 1)

                def vectors(g):
                    G = NG * hf + g
                    gi = g % PG
                    w, cf, nt, d = (a[g // PG % 2] for a in (psi, coef, ndt, dd))
                    sl = slice(gi * HS, (gi + 1) * HS)
                    bt4 = "p j (b t) -> p j b t"
                    q_, p_ = w[:, 0:2, sl, 1:ST + 1], w[:, 2:4, sl, 1:ST + 1]
                    q0, p0 = w[:, 0:2, sl, 0:ST], w[:, 2:4, sl, 0:ST]
                    full = [P, 2, HS, ST]

                    def rows(a):
                        return a.rearrange("p (b t) -> p b t", b=HS).unsqueeze(1).to_broadcast(full)

                    def v4(a):
                        return a.rearrange(bt4, b=HS)

                    d1 = d[:, 1, :].rearrange("p (b t) -> p b t", b=HS)
                    d0 = d[:, 0, :].rearrange("p (b t) -> p b t", b=HS)
                    wait(dve, s_dinv, G)
                    V.tensor_tensor(d0, p_[:, 0], q_[:, 1], ALU.mult)
                    link(V.tensor_tensor(d1, p_[:, 1], q_[:, 0], ALU.mult))
                    V.tensor_tensor(d1, d1, d0, ALU.subtract).then_inc(s_det, 1)
                    dve.wait_ge(s_rn, 4 * G + 4)
                    link(V.tensor_tensor(raw, raw, rn, ALU.mult))
                    nd2 = nt[:, gi, :].unsqueeze(1).to_broadcast([P, 2, HT])
                    link(V.tensor_tensor(t1, raw[:, 0:2, :], nd2, ALU.mult))
                    link(V.tensor_tensor(t2[:, 0, :], t1[:, 1, :], cf[:, 0, gi, :], ALU.mult))
                    link(V.tensor_tensor(t1[:, 0, :], t1[:, 0, :], t2[:, 0, :], ALU.add))
                    V.tensor_tensor(v4(bt), p0, rows(t1[:, 0, :]), ALU.mult)
                    link(V.tensor_tensor(v4(t2), q0, rows(t1[:, 1, :]), ALU.mult))
                    link(V.tensor_tensor(bt, bt, t2, ALU.add))
                    V.tensor_tensor(v4(t1), q_, rows(raw[:, 2, :]), ALU.mult)
                    link(V.tensor_tensor(v4(t2), p_, rows(raw[:, 3, :]), ALU.mult))
                    link(V.tensor_tensor(t1, t1, t2, ALU.subtract))
                    dve.wait_ge(s_dinv, G + 1)
                    V.tensor_tensor(ct, t1, d, ALU.mult).then_inc(s_bt, 1)

                for g in range(NG):
                    if g > 1:
                        outputs(g - 2)
                    if g > 0:
                        masked(g - 1)
                    join(g)
                    vectors(g)
                    p, r = g // PG + 1, g % PG
                    if p < NPASS:
                        if r == 0:
                            start(p)
                        recur(p, r * (ST // PG), (r + 1) * (ST // PG))
                outputs(NG - 2)
                masked(NG - 1)
                outputs(NG - 1)
                for v in range(VC):
                    dve.wait_ge(s_gs, 8 * hf + v + 1)
                    V.tensor_tensor(val[:, v, :], val[:, v, :], gate[:, v, :], ALU.mult).then_inc(s_gy, 1)
                    if v:
                        split_gated(v - 1)
                split_gated(VC - 1)
                for t in range(4):
                    dve.wait_ge(s_op, 4 * hf + t + 1)
                    tt = 4 * hf + t
                    V.scalar_tensor_tensor(x[:, tt, :], ps[:, t, :], UNS, x[:, tt, :], ALU.mult, ALU.add).then_inc(s_xo, 1)

            layer_norm(3, 8, (4, 5), xch, xcl, 0, lambda i: dve.wait_ge(s_xo, 8))
            dve.wait_ge(s_xx, 8)
            dve.wait_ge(s_cact, 4)
            V.tensor_scalar(p2d[0:NP, :], ident[0:NP, 0:NP], p2[:, 0:1], None, ALU.mult).then_inc(s_pb, 1)
            dve.wait_ge(s_pb, 2)
            V.tensor_copy(p2b, ps[:, 6, 0:NP]).then_inc(s_pb, 1)
            dve.wait_ge(s_pb, 3)
            sh3 = [P, 8, NP]
            link(V.tensor_tensor(fa, p2b.unsqueeze(1).to_broadcast(sh3), x2.unsqueeze(2).to_broadcast(sh3), ALU.add))
            dve.wait_ge(s_xp, 1)
            link(V.scalar_tensor_tensor(fa, ps[:, 7, 0:8 * NP].rearrange("p (t n) -> p t n", t=8), -2.0 * UNS, fa,
                                        ALU.mult, ALU.add))
            V.tensor_scalar(fa, fa, 0.0, None, ALU.max).then_inc(s_d2, 1)
            dve.wait_ge(s_d2, 1)
            link(V.tensor_scalar(nd, fa, -1.0, None, ALU.mult))
            for t in range(8):
                ins = V.max(top[:, t, :], nd[:, t, :])
            link(ins)
            for t in range(8):
                ins = V.max_index(topi[:, t, :], top[:, t, :], nd[:, t, :])
            link(ins)
            link(V.tensor_copy(topf, topi))
            dve.wait_ge(s_iota, 1)
            iob = io[:, :].unsqueeze(1).to_broadcast(sh3)
            V.tensor_tensor(m0, topf[:, :, 0:1].to_broadcast(sh3), iob, ALU.is_equal)
            link(V.tensor_tensor(m1, topf[:, :, 1:2].to_broadcast(sh3), iob, ALU.is_equal))
            link(V.tensor_tensor(m0, m0, m1, ALU.add))
            dve.wait_ge(s_sqd, 1)
            link(V.tensor_reduce(dm, ds, AX.X, ALU.min))
            V.tensor_tensor(ds, ds, dm.unsqueeze(2).to_broadcast(sh3), ALU.subtract).then_inc(s_dif, 1)
            dve.wait_ge(s_e, 1)
            link(V.tensor_tensor(ew, ew, m0, ALU.mult))
            link(V.tensor_reduce(es_sum, ew, AX.X, ALU.add))
            link(V.reciprocal(es_sum, es_sum))
            V.tensor_tensor(wn, ew, es_sum.unsqueeze(2).to_broadcast(sh3), ALU.mult).then_inc(s_wn, 1)
            dve.wait_ge(s_wn, 1)

            def weighted(t):
                dve.wait_ge(s_hp, t + 1)
                wait(dve, s_ht, t - 1)
                V.scalar_tensor_tensor(hw[:, t % 2, :].rearrange("p (n r) -> p n r", n=NP),
                                       ps[:, t % 2, :].rearrange("p (n r) -> p n r", n=NP), UNS,
                                       wn[:, t, :].unsqueeze(2).to_broadcast([P, NP, RK]), ALU.mult,
                                       ALU.mult).then_inc(s_hw, 1)

            weighted(0)
            for t in range(8):
                if t + 1 < 8:
                    weighted(t + 1)
                dve.wait_ge(s_hhi, t + 1)
                wait(dve, s_fp, t - 1)
                V.scalar_tensor_tensor(hl[:, t % 2, :, :], ps[:, 4 + t % 2, :].rearrange("p (c n) -> p c n", c=DC), XS,
                                       hh[:, t % 2, :, :], ALU.mult, ALU.subtract).then_inc(s_hlo, 1)
                dve.wait_ge(s_fp, t + 1)
                V.scalar_tensor_tensor(x[:, t, :], ps[:, 2 + t % 2, :], UNS, x[:, t, :], ALU.mult, ALU.add).then_inc(s_fo, 1)


def kernel(x, ctx_1024, L0_xattn_w_q, L0_xattn_w_kv, L0_xattn_w_concat, L0_attn_W_in, L0_attn_dw_weight, L0_attn_dw_bias,
           L0_attn_W_bc, L0_attn_W_out, L0_attn_skip, L0_attn_A_log, L0_attn_dt_bias, L0_ffn_prototypes, L0_ffn_B,
           L0_ffn_A, L0_ffn_bias, L0_ffn_temp):
    import concourse.bacc as bacc
    from concourse.bass_utils import run_bass_kernel_spmd

    a = np.asarray

    def lay(v, split, order, shape):
        return np.ascontiguousarray(a(v).reshape(split).transpose(order).reshape(shape))

    w_in = a(L0_attn_W_in)
    wkv = a(L0_xattn_w_kv).reshape(P, DC, 2, DH)
    chunk = (-1, P, CH)
    arrays = {
        "x": a(x).reshape(8, P, D),
        "ctx": lay(ctx_1024, (B, NKEY, P, DC), (0, 2, 3, 1), (B, P, DC, NKEY)),
        "w": np.concatenate([
            lay(L0_xattn_w_q, (DC, P, D), (1, 0, 2), chunk),
            lay(L0_xattn_w_concat, (DC, P, D), (1, 0, 2), chunk),
            lay(w_in[DI:2 * DI], (2, 512, DC, P), (0, 3, 2, 1), chunk),
            lay(L0_attn_W_bc, (NG, 4, 2, 2, SN, VC, P), (0, 2, 6, 5, 3, 1, 4), chunk),
            lay(w_in[0:DI], (2, 512, DC, P), (0, 3, 2, 1), chunk),
            lay(L0_attn_W_out, (D, 2, 4, P), (1, 3, 2, 0), chunk),
            lay(L0_ffn_B, (NP * RK, DC, P), (2, 1, 0), chunk),
            lay(L0_ffn_A, (NP, D, RK), (0, 2, 1), (DC, P, D)).transpose(1, 0, 2).reshape(chunk)]),
        "wkv": np.ascontiguousarray(wkv.reshape(P, DC, 2 * DH)),
        "wp": lay(w_in[2 * DI:], (SH, 2, DC, P), (3, 2, 1, 0), (P, DC, 64)),
        "proto": a(L0_ffn_prototypes),
        "protot": lay(L0_ffn_prototypes, (NP, DC, P), (2, 1, 0), (P, DC, NP)),
        "bias": a(L0_ffn_bias),
        "conv": lay(L0_attn_dw_weight, (VC, P, 4), (1, 0, 2), (P, VC, 4)),
        "dwb": lay(L0_attn_dw_bias, (VC, P), (1, 0), (P, VC)),
        "skip": lay(L0_attn_skip, (VC, P), (1, 0), (P, VC)),
        "alog": a(L0_attn_A_log),
        "dtb": a(L0_attn_dt_bias).reshape(SH, 1),
        "temp": np.ascontiguousarray(np.broadcast_to(a(L0_ffn_temp).reshape(1, 1), (P, 1))),
    }
    nc = bacc.Bacc("TRN2", target_bir_lowering=False, num_devices=1)
    args = [nc.dram_tensor("in_" + k, v.shape, mybir.dt.from_np(v.dtype), kind="ExternalInput").ap() for k, v in arrays.items()]
    out = nc.dram_tensor("out_x", (8, P, D), F32, kind="ExternalOutput").ap()
    build(nc, *args, out)
    r = run_bass_kernel_spmd(nc, [{"in_" + k: v for k, v in arrays.items()}], core_ids=[0])
    return r.results[0]["out_x"].reshape(B, T, D)
```

```python
import numpy as np
import concourse.bass as bass
from concourse import mybir
from contextlib import ExitStack

F32 = mybir.dt.float32
F16 = mybir.dt.float16
U32 = mybir.dt.uint32
ALU = mybir.AluOpType
ACT = mybir.ActivationFunctionType
AX = mybir.AxisListType

P = 128
B, T, D = 16, 64, 512
TOK = B * T
NKEY = 1601
H, DH = 16, 32
DC = D // P
KT = -(-NKEY // P)
BLK = [(0, 401)] + [(401 + 400 * i, 400) for i in range(3)]
DI, SH, SN = 1024, 32, 32
VC = DI // P
NG = 8
HT = TOK // 2
HB = B // 2
PG = 2
NPASS = NG // PG
CS = 2
ST = T // CS
HS = HB * CS
NS = PG * HS
NP, RK = 32, 16
XS, WS = 16.0, 256.0
UNS = 1.0 / (XS * WS)
QB = (2, 3, 6, 7)
MS = 256.0
SC = 1.0 / (XS * XS * DH ** 0.5)
EPS = 1e-5
CH = D * D // P
HCHUNKS = 2 + 2 * NG + 2 + 2
SEQ = [0, 1] + 2 * list(range(2, 2 + HCHUNKS)) + [2 + HCHUNKS, 3 + HCHUNKS]
ITEMS = 36
V_STEP = 2
DS, AS = 4096.0, 16.0
EARLY = ST // 4
LOG1P = [(-1.0) ** (k + 1) / k for k in range(1, 9)]


def wait(eng, sem, n):
    if isinstance(n, int) and n <= 0:
        return
    eng.wait_ge(sem, n)


def build(nc, x_in, ctx_in, w_in, wkv_in, wp_in, proto_in, protot_in, bias_in, conv_in, dwb_in, skip_in, alog_in,
          dtb_in, temp_in, out):
    es = ExitStack()
    with es:
        def sb(name, shape, dt=F32):
            return es.enter_context(nc.sbuf_tensor(name, shape, dt))

        def sem(name):
            return es.enter_context(nc.semaphore(name))

        x = sb("x", [P, 8, D])
        ident = sb("ident", [P, P])
        ones = sb("ones", [P, P])
        head_ones = sb("head_ones", [P, P])
        causal = sb("causal", [P, T])
        wkv = sb("wkv", [P, DC, 2 * DH])
        wp = sb("wp", [P, DC, 64])
        wph, wpl = sb("wph", [P, DC, 64], F16), sb("wpl", [P, DC, 64], F16)
        sel_a, sel_1 = sb("sel_a", [P, 8 * P], F16), sb("sel_1", [P, 8 * P], F16)
        ah, al = sb("ah", [SH, SN], F16), sb("al", [SH, SN], F16)
        alog = sb("alog", [SH, SN])
        amat = sb("amat", [SH, SN])
        dtb = sb("dtb", [SH, 1])
        conv_w = sb("conv_w", [P, VC, 4])
        conv_b = sb("conv_b", [P, VC])
        skip = sb("skip", [P, VC])
        proto_t = sb("proto_t", [P, DC, NP])
        pth, ptl = sb("pth", [P, DC, NP], F16), sb("ptl", [P, DC, NP], F16)
        p2 = sb("p2", [NP, 1])
        nit = sb("nit", [P, 4])
        stats = sb("stats", [P, 8, 6])
        mv = sb("mv", [P, 8, 2])
        std = sb("std", [P, 8])
        tiny = sb("tiny", [P, 2])
        io = sb("io", [P, NP])
        rstd = sb("rstd", [P, 8])
        wst = sb("wst", [P, 2, CH // 2])
        wh, wl = sb("wh", [P, 2, CH], F16), sb("wl", [P, 2, CH], F16)

        words = 39900
        arena = sb("arena", [P, words])
        cursor = [0]

        def carve(n, dt=F32):
            a = cursor[0]
            cursor[0] += n
            assert cursor[0] <= words, cursor
            v = arena[:, a:a + n]
            return v if dt == F32 else v.bitcast(dt)

        ctx = [carve(DC * NKEY).rearrange("p (c k) -> p c k", c=DC) for _ in range(2)]
        qs = carve(B * H * T // 2, F16)
        ks = [carve(802, F16) for _ in range(2)]
        vt = carve(1602)
        vv = [carve(KT * DH).rearrange("p (k n) -> p k n", k=KT) for _ in range(2)]
        pr = [carve(2 * 512) for _ in range(2)]
        oth = carve(DC * TOK // 2, F16).rearrange("p (c t) -> p c t", c=DC)
        otl = carve(DC * TOK // 2, F16).rearrange("p (c t) -> p c t", c=DC)
        rl = carve(DC * T).rearrange("p (c t) -> p c t", c=DC)
        on = [carve(DC * T).rearrange("p (c t) -> p c t", c=DC) for _ in range(2)]
        mxp = carve(8 * 4).rearrange("p (i k) -> p i k", i=8)
        mx = carve(8)
        eye8 = carve(8 * P)[0:8, :].rearrange("p (i n) -> p i n", i=8)
        xn_a = carve(2 * D).rearrange("p (u d) -> p u d", u=2)
        cursor[0] = DC * NKEY
        xah = carve(DC * TOK // 2, F16).rearrange("p (c t) -> p c t", c=DC)
        xal = carve(DC * TOK // 2, F16).rearrange("p (c t) -> p c t", c=DC)
        cursor[0] = 0
        xbh = carve(DC * HT // 2, F16).rearrange("p (c t) -> p c t", c=DC)
        xbl = carve(DC * HT // 2, F16).rearrange("p (c t) -> p c t", c=DC)
        val = carve(VC * HT).rearrange("p (v t) -> p v t", v=VC)
        vh = carve(VC * HT // 2, F16).rearrange("p (v t) -> p v t", v=VC)
        vl = carve(VC * HT // 2, F16).rearrange("p (v t) -> p v t", v=VC)
        ut0 = cursor[0]
        ut = carve(4 * DI).rearrange("p (b i) -> p b i", b=4)
        coef = [carve(2 * PG * HT).rearrange("p (j g n) -> p j g n", j=2, g=PG) for _ in range(2)]
        ndt = [carve(PG * HT).rearrange("p (g n) -> p g n", g=PG) for _ in range(2)]
        pw = 4 * NS * (ST + 1)
        psi_all = [carve(pw + 2) for _ in range(2)]
        psi = [a[:, 0:pw].rearrange("p (c s t) -> p c s t", c=4, s=NS) for a in psi_all]
        skew = [a.rearrange("p (j x) -> p j x", j=2)[:, :, 0:pw // 2].rearrange("p j (s t) -> p j s t", t=ST + 1)
                for a in psi_all]
        rm = carve(4 * NS).rearrange("p (j r s) -> p j r s", j=2, r=2)
        pd = carve(HT, F16).rearrange("p (j t) -> p j t", j=2)
        raw = carve(4 * HT).rearrange("p (j t) -> p j t", j=4)
        sq = [carve(HT) for _ in range(2)]
        rn = carve(4 * HT).rearrange("p (j t) -> p j t", j=4)
        cp = rn
        dd = [coef[u][:, 1, :, :] for u in range(2)]
        kk = carve(2 * HT)
        t1 = carve(2 * HT).rearrange("p (j t) -> p j t", j=2)
        t2 = carve(2 * HT).rearrange("p (j t) -> p j t", j=2)
        bt = carve(2 * HT).rearrange("p (j t) -> p j t", j=2)
        ct = carve(2 * HT).rearrange("p (j t) -> p j t", j=2)
        xn_b = t1
        gate = psi_all[1][:, 0:VC * HT].rearrange("p (v t) -> p v t", v=VC)
        cursor[0] = 0
        xn_c = carve(2 * D).rearrange("p (u d) -> p u d", u=2)
        xch = carve(DC * TOK // 2, F16).rearrange("p (c t) -> p c t", c=DC)
        xcl = carve(DC * TOK // 2, F16).rearrange("p (c t) -> p c t", c=DC)
        assert cursor[0] <= DC * HT + VC * HT
        cursor[0] = ut0
        proto = carve(D)[0:NP, :]
        ebias = carve(D)[0:NP, :]
        xsq = carve(D)
        x2 = carve(8)
        p2d = carve(NP)
        p2b = carve(NP)
        fa = carve(8 * NP).rearrange("p (t n) -> p t n", t=8)
        nd = carve(8 * NP).rearrange("p (t n) -> p t n", t=8)
        ds = carve(8 * NP).rearrange("p (t n) -> p t n", t=8)
        top = carve(8 * 8).rearrange("p (t n) -> p t n", t=8)
        topi = carve(8 * 8).rearrange("p (t n) -> p t n", t=8).bitcast(U32)
        topf = carve(8 * 8).rearrange("p (t n) -> p t n", t=8)
        dm = carve(8)
        m0 = carve(8 * NP).rearrange("p (t n) -> p t n", t=8)
        m1 = carve(8 * NP).rearrange("p (t n) -> p t n", t=8)
        ew = carve(8 * NP).rearrange("p (t n) -> p t n", t=8)
        es_sum = carve(8)
        wn = carve(8 * NP).rearrange("p (t n) -> p t n", t=8)
        hw = carve(2 * D).rearrange("p (u d) -> p u d", u=2)
        wt = carve(8 * P).rearrange("p (t n) -> p t n", t=8)
        hh = carve(2 * DC * P // 2, F16).rearrange("p (u c t) -> p u c t", u=2, c=DC)
        hl = carve(2 * DC * P // 2, F16).rearrange("p (u c t) -> p u c t", u=2, c=DC)

        ps = es.enter_context(nc.psum_tensor("ps", [P, 8, 512], F32))

        s_x = [sem("x_first_half_loaded"), sem("x_second_half_loaded")]
        s_wkv, s_small, s_proto = sem("wkv_loaded"), sem("small_loaded"), sem("proto_loaded")
        s_late = sem("proto_rows_loaded")
        s_ctx = [sem("ctx0_loaded"), sem("ctx1_loaded")]
        s_wld = [sem("weight_piece0_loaded"), sem("weight_piece1_loaded")]
        s_whi, s_wsc, s_wlo = sem("weight_hi"), sem("weight_scaled"), sem("weight_lo")
        s_pool, s_dve, s_act = sem("pool_step"), sem("dve_step"), sem("act_step")
        s_const, s_cdve, s_cact = sem("pool_constants"), sem("dve_constants"), sem("act_constants")
        ln_sems = [[sem(f"ln{k}_{n}") for n in ("var", "std", "xn", "tr", "hi", "lo")] for k in range(6)]
        s_q, s_qhi, s_qlo = sem("q_products"), sem("q_hi"), sem("q_lo")
        s_item, s_itemfree, s_khi = sem("item_ready"), sem("item_used"), sem("k_hi")
        s_mx, s_s2, s_exp, s_pv = sem("maxima"), sem("scores"), sem("probs"), sem("probs_used")
        s_pvfree = sem("sums_read")
        s_rl = sem("reciprocals")
        s_oh, s_ol, s_y, s_x1 = sem("attn_hi"), sem("attn_lo"), sem("concat_products"), sem("x1")
        s_vp, s_cv, s_silu = sem("value_products"), sem("conv_done"), sem("value_f32")
        s_vhi, s_vlo = sem("value_hi"), sem("value_lo")
        s_ut, s_utc = sem("value_transposed"), sem("ut_ready")
        s_pp, s_pe1, s_pdr = sem("param_products"), sem("param_exp"), sem("dt_k_ready")
        s_bc, s_bcc = sem("coef_broadcast"), sem("coef_ready")
        s_rec = sem("recurrence_step")
        s_bp, s_raw = sem("bc_products"), sem("bc_copied")
        s_sq, s_ss, s_lg, s_rn = sem("bc_squared"), sem("sum_of_squares"), sem("norm_log"), sem("norm_ready")
        s_cm, s_pdz = sem("conv_last_tap"), sem("params_zeroed")
        s_normed, s_drive = sem("bc_normed"), sem("b_with_dt")
        s_det, s_dinv = sem("determinant"), sem("inverse_determinant")
        s_bt, s_k, s_kk, s_yp, s_yv = sem("b_ready"), sem("kernel_products"), sem("kernel_masked"), sem("y_products"), sem("y_ready")
        s_cp, s_ct = sem("pool_c_step"), sem("c_ready")
        s_kh, s_ye = sem("kernels_of_two_heads"), sem("y_of_even_batches")
        s_gp, s_gs, s_gy, s_ghi, s_glo = sem("gate_products"), sem("gate_silu"), sem("gated"), sem("gated_hi"), sem("gated_lo")
        s_oq, s_op, s_xo = sem("out_first_half"), sem("out_products"), sem("x2")
        s_xx, s_pb = sem("x_squares"), sem("p2_broadcast")
        s_xp, s_d2, s_sqd, s_dif, s_e, s_wn = sem("proto_products"), sem("dist2"), sem("dist"), sem("dist_shift"), sem("weights_exp"), sem("router_ready")
        s_iota = sem("iota")
        s_wtt, s_wt = sem("router_transposed"), sem("router_t")
        s_hp, s_hw, s_ht, s_hhi, s_hlo = sem("h_products"), sem("h_weighted"), sem("h_transposed"), sem("h_hi"), sem("h_lo")
        s_fp, s_fo, s_out = sem("ffn_products"), sem("x3"), sem("out_stored")

        LN = [(xn_a, (0, 1)), (xn_a, (4, 5)), (xn_b, (6, 7)), (xn_b, (6, 7)), (xn_c, (4, 5)), (xn_c, (0, 1))]

        block = es.enter_context(nc.Block())

        def chunk_at(half, n):
            return 2 + half * HCHUNKS + n

        def chunk_used(s):
            if s < 2:
                return (s_q, s_y)[s], 8
            half, n = divmod(s - 2, HCHUNKS)
            if half == 2:
                return (s_hp, s_fp)[n], 8
            if n < 2:
                return s_vp, 8 * half + 4 * (n + 1)
            if n < 2 + 2 * NG:
                return s_bp, 4 * NG * half + 2 * (n - 1)
            if n < 4 + 2 * NG:
                return s_gp, 8 * half + 4 * (n - 1 - 2 * NG)
            return (s_oq, s_op)[n - 4 - 2 * NG], 4 * (half + 1)

        def weights_there(pe, s):
            pe.wait_ge(s_wlo, 2 * (s + 1))

        def split3(pairs):
            (ah, al), (bh, bl) = pairs
            return [(ah, bh), (ah, bl), (al, bh)]

        @block.sync
        def _(sp):
            for t in range(8):
                sp.dma_start(x[:, t, :], x_in[t]).then_inc(s_x[t // 4], 16)

            def weight_piece(q):
                wait(sp, s_wlo, q - 1)
                sp.dma_start(wst[:, q % 2, :], w_in[SEQ[q // 2], :, (q % 2) * (CH // 2):(q % 2 + 1) * (CH // 2)]
                             ).then_inc(s_wld[q % 2], 16)

            weight_piece(0)
            weight_piece(1)
            sp.dma_start(wkv[:, :, :], wkv_in).then_inc(s_wkv, 16)
            sp.dma_start(ctx[0], ctx_in[0]).then_inc(s_ctx[0], 16)
            for dst, src in ((wp[:, :, :], wp_in), (alog[:, :], alog_in), (dtb[:, :], dtb_in), (conv_w[:, :, :], conv_in),
                             (conv_b[:, :], dwb_in), (skip[:, :], skip_in)):
                sp.dma_start(dst, src).then_inc(s_small, 16)
            sp.dma_start(proto_t[:, :, :], protot_in).then_inc(s_proto, 16)
            sp.dma_start(nit[:, 0:1], temp_in).then_inc(s_proto, 16)
            for q in range(2, 8):
                weight_piece(q)
            sp.wait_ge(s_qlo, 8)
            wait(sp, s_q, 8)
            sp.dma_start(ctx[1], ctx_in[1]).then_inc(s_ctx[1], 16)

            def load_ctx(b, u):
                wait(sp, s_item, ITEMS * (b - 2) + 2)
                sp.dma_start(ctx[u], ctx_in[bass.ds(b, 1)].rearrange("a p c k -> p (a c) k")).then_inc(s_ctx[u], 16)

            load_ctx(2, 0)
            load_ctx(3, 1)
            with sp.Fori(1, B // 2 - 1) as i:
                load_ctx(2 * i + 2, 0)
                load_ctx(2 * i + 3, 1)
            for q in range(8, 2 * len(SEQ)):
                weight_piece(q)
            sp.wait_ge(s_yp, 2 * NG)
            sp.dma_start(proto, proto_in).then_inc(s_late, 16)
            sp.dma_start(ebias, bias_in).then_inc(s_late, 16)
            for t in range(8):
                wait(sp, s_fo, t + 1)
                sp.dma_start(out[t], x[:, t, :]).then_inc(s_out, 16)
            sp.wait_ge(s_out, 8 * 16)

        @block.gpsimd
        def _(pool):
            n = [0]

            def link(ins):
                n[0] += 1
                ins.then_inc(s_pool, 1)
                pool.wait_ge(s_pool, n[0])

            nc.gpsimd.iota(io[:, :], pattern=[[1, NP]], base=0, channel_multiplier=0,
                           allow_small_or_imprecise_dtypes=True).then_inc(s_iota, 1)
            pool.wait_ge(s_iota, 1)
            link(nc.gpsimd.memset(ident[:, :], 0.0))
            link(nc.gpsimd.memset(causal[:, :], 1.0))
            link(nc.gpsimd.memset(eye8[:, :, :], 0.0))
            nc.gpsimd.affine_select(out=ident[:, :], in_=ident[:, :], compare_op=ALU.not_equal, fill=1.0, base=0,
                                    pattern=[[-1, P]], channel_multiplier=1).then_inc(s_const, 1)
            for e in range(2):
                pool.wait_ge(s_const, e + 1)
                v = causal[T * e:T * e + T, :]
                nc.gpsimd.affine_select(out=v, in_=v, compare_op=ALU.is_ge, fill=0.0, base=0,
                                        pattern=[[1, T]], channel_multiplier=-1).then_inc(s_const, 1)
            pool.wait_ge(s_const, 3)
            nc.gpsimd.affine_select(out=eye8[:, :, :], in_=eye8[:, :, :], compare_op=ALU.not_equal, fill=1.0 / MS,
                                    base=0, pattern=[[-1, 8], [0, P]], channel_multiplier=1).then_inc(s_const, 1)
            pool.wait_ge(s_const, 4)
            def c_vectors(half, g):
                G = NG * half + g
                w, d = (a[g // PG % 2] for a in (psi, dd))
                sl = slice((g % PG) * HS, (g % PG + 1) * HS)
                full = [P, 2, HS, ST]

                def v4(a):
                    return a.rearrange("p j (b t) -> p j b t", b=HS)

                def rows(a):
                    return a.rearrange("p (b t) -> p b t", b=HS).unsqueeze(1).to_broadcast(full)

                def step(*a):
                    nc.gpsimd.tensor_tensor(*a).then_inc(s_cp, 1)

                tmp = rn[:, 2:4, :]
                pool.wait_ge(s_normed, G + 1)
                wait(pool, s_k, G)
                step(v4(ct), w[:, 0:2, sl, 1:ST + 1], rows(raw[:, 2, :]), ALU.mult)
                pool.wait_ge(s_cp, 3 * G + 1)
                step(v4(tmp), w[:, 2:4, sl, 1:ST + 1], rows(raw[:, 3, :]), ALU.mult)
                pool.wait_ge(s_cp, 3 * G + 2)
                step(ct, ct, tmp, ALU.subtract)
                pool.wait_ge(s_cp, 3 * G + 3)
                pool.wait_ge(s_dinv, G + 1)
                nc.gpsimd.tensor_tensor(ct, ct, d, ALU.mult).then_inc(s_ct, 1)
                pool.wait_ge(s_ct, G + 1)

            for q in range(2 * len(SEQ)):
                s, r = divmod(q, 2)
                st = wst[:, r, :]
                lo = slice(r * (CH // 2), (r + 1) * (CH // 2))
                if q == 6:
                    pool.wait_ge(s_y, 8)
                    nc.gpsimd.memset(pd, 0.0).then_inc(s_pdz, 1)
                    pool.wait_ge(s_pdz, 1)
                pool.wait_ge(s_wld[r], 16 * (s + 1))
                if s >= 2:
                    pool.wait_ge(*chunk_used(s - 2))
                nc.gpsimd.tensor_scalar(wh[:, s % 2, lo], st, WS, 0.0, ALU.mult, ALU.add).then_inc(s_whi, 1)
                pool.wait_ge(s_whi, q + 1)
                nc.gpsimd.tensor_scalar(st, st, WS, 0.0, ALU.mult, ALU.add).then_inc(s_wsc, 1)
                pool.wait_ge(s_wsc, q + 1)
                nc.gpsimd.tensor_tensor(wl[:, s % 2, lo], st, wh[:, s % 2, lo], ALU.subtract).then_inc(s_wlo, 1)
                pool.wait_ge(s_wlo, q + 1)
                half, n_ = divmod(s - 2, HCHUNKS)
                if s >= 2 and half < 2 and r == 1 and n_ % 2 == 1 and 5 <= n_ <= 2 * NG + 3:
                    c_vectors(half, (n_ - 5) // 2)

        @block.tensor
        def _(pe):
            mm = nc.tensor.matmul

            def bank(b):
                return ps[:, b, :]

            def layer_norm(k):
                var, stdd, xnr, tr, hi, lo = ln_sems[k]
                xn, banks = LN[k]
                for i in range(4):
                    pe.wait_ge(xnr, i + 1)
                    wait(pe, hi, i - 1)
                    wait(pe, lo, i - 1)
                    for c in range(DC):
                        last = nc.tensor.transpose(bank(banks[i % 2])[:, c * P:(c + 1) * P],
                                                   xn[:, i % 2, c * P:(c + 1) * P], ident[:, :])
                    last.then_inc(tr, 1)

            pe.wait_ge(s_const, 4)
            layer_norm(0)
            W = wh[:, 0, :].rearrange("p (c n) -> p c n", c=DC), wl[:, 0, :].rearrange("p (c n) -> p c n", c=DC)
            weights_there(pe, 0)
            for u in range(8):
                n2, m = divmod(u, 4)
                if u == 4:
                    layer_norm(1)
                pe.wait_ge(ln_sems[n2][4], 4)
                pe.wait_ge(ln_sems[n2][5], 4)
                wait(pe, s_qlo, u - 3)
                k = 0
                for a, b in ((W[0], xah), (W[0], xal), (W[1], xah)):
                    for c in range(DC):
                        last = mm(bank(QB[m])[:, :], a[:, c, m * P:(m + 1) * P], b[:, c, n2 * HT:(n2 + 1) * HT],
                                  start=(k == 0), stop=(k == 3 * DC - 1))
                        k += 1
                last.then_inc(s_q, 1)

            def item_bank(b, p):
                wait(pe, s_itemfree, ITEMS * b + p - 2)
                return bank(5 + p % 3)

            def kv(b, u, p, first):
                if p == 0:
                    pe.wait_ge(s_ctx[u], first)
                o = item_bank(b, p)
                for c in range(DC):
                    for r in range(2):
                        k0, n = BLK[2 * p + r]
                        last = mm(o[64 * r:64 * r + 64, 0:n], wkv[:, c, :], ctx[u][:, c, k0:k0 + n],
                                  start=(c == 0), stop=(c == DC - 1))
                last.then_inc(s_item, 1)

            def v_there(b):
                item_bank(b, 2)
                wait(pe, s_khi, 4 * (b + 1))

            def v_turn(b):
                o = bank(7)
                for kt in range(KT):
                    nk = min(P, NKEY - kt * P)
                    last = nc.tensor.transpose(o[0:nk, 32 * kt:32 * kt + 32], vt[96:128, kt * P:kt * P + nk],
                                               ident[96:128, 96:128])
                last.then_inc(s_item, 1)

            def s1(b, u, i, part):
                for blk in (2 * part, 2 * part + 1):
                    k0, n = BLK[blk]
                    o = item_bank(b, 3 + 4 * i + blk)
                    if i == 0 and blk == 0:
                        wait(pe, s_itemfree, ITEMS * b + 2)
                    mm(o[:, 0:n], qs[0:96, bass.ds(b * 1024 + i * P, P)], ks[u][0:96, k0:k0 + n],
                       start=True, stop=True).then_inc(s_item, 1)

            def turn_max(b):
                o = item_bank(b, 35)
                wait(pe, s_mx, b + 1)
                nc.tensor.transpose(o[0:8, 0:P], mx, ident[:, :]).then_inc(s_item, 1)

            def prepare(b, u, kt, first, product):
                if kt < 2:
                    kv(b, u, kt, first)
                if V_STEP < kt <= V_STEP + 8:
                    s1(b, u, kt - V_STEP - 1, 0)
                product()
                if V_STEP < kt <= V_STEP + 8:
                    s1(b, u, kt - V_STEP - 1, 1)
                if kt == V_STEP + 9:
                    turn_max(b)

            def s2(b, u, kt):
                k = KT * b + kt
                s = (KT * u + kt) % 2
                nk = min(P, NKEY - kt * P)
                wait(pe, s_exp, k - 1)
                if kt == 0:
                    wait(pe, s_itemfree, ITEMS * (b + 1))
                for q in range(2):
                    last = mm(ps[0:nk, 2 * s + q, :], ks[u][0:104, kt * P:kt * P + nk],
                              qs[0:104, bass.ds(b * 1024 + q * 512, 512)], start=True, stop=True)
                last.then_inc(s_s2, 1)

            def pv(b, u, kt):
                k = KT * b + kt
                s = (KT * u + kt) % 2
                nk = min(P, NKEY - kt * P)
                wait(pe, s_exp, k + 1)
                if kt == 0:
                    wait(pe, s_pvfree, b)
                for k, a in enumerate((vv[u][0:nk, kt, :], ones[0:nk, 0:DH])):
                    for j in range(4):
                        last = mm(ps[32 * j:32 * j + 32, 4, 256 * k:256 * k + 256].rearrange("p (c t) -> p c t", c=DC), a,
                                  pr[s][0:nk, :].rearrange("p (c j t) -> p c j t", c=DC, j=4)[:, :, j, :],
                                  start=(kt == 0 and k == 0), stop=(kt == KT - 1 and k == 1))
                last.then_inc(s_pv, 1)

            def batch(b, u, nxt):
                s2(b, u, 0)
                for kt in range(KT):
                    turn = nxt is not None and kt == V_STEP + 1
                    if turn:
                        v_there(b + 1)
                    if kt + 1 < KT:
                        s2(b, u, kt + 1)
                    if turn:
                        v_turn(b + 1)
                    if nxt is not None:
                        prepare(b + 1, 1 - u, kt, nxt, lambda: pv(b, u, kt))
                    else:
                        pv(b, u, kt)

            pe.wait_ge(s_wkv, 16)
            wait(pe, s_qlo, 8)
            for kt in range(KT):
                if kt == V_STEP + 1:
                    v_there(0)
                    v_turn(0)
                prepare(0, 0, kt, 16, lambda: None)
            batch(0, 0, 16)
            batch(1, 1, 32)
            with pe.Fori(1, B // 2 - 1) as i:
                batch(2 * i, 0, 16 * (i + 1))
                batch(2 * i + 1, 1, 16 * (i + 2))
            batch(B - 2, 0, 16 * (B // 2))
            batch(B - 1, 1, None)

            weights_there(pe, 1)
            Wc = wh[:, 1, :].rearrange("p (c n) -> p c n", c=DC), wl[:, 1, :].rearrange("p (c n) -> p c n", c=DC)
            for t in range(8):
                pe.wait_ge(s_oh, 2 * t + 2)
                pe.wait_ge(s_ol, 2 * t + 2)
                wait(pe, s_x1, t - 1)
                k = 0
                for a, b in ((oth, Wc[0]), (oth, Wc[1]), (otl, Wc[0])):
                    for c in range(DC):
                        last = mm(bank(t % 2), a[:, c, t * P:(t + 1) * P], b[:, c, :],
                                  start=(k == 0), stop=(k == 3 * DC - 1))
                        k += 1
                last.then_inc(s_y, 1)

            def wide(half, n, v, dst, done):
                s = chunk_at(half, n + v // 4)
                if v % 4 == 0:
                    weights_there(pe, s)
                hi = wh[:, s % 2, :].rearrange("p (c n) -> p c n", c=DC)
                lo = wl[:, s % 2, :].rearrange("p (c n) -> p c n", c=DC)
                cols = slice((v % 4) * P, (v % 4 + 1) * P)
                k = 0
                for a, b in ((hi, xbh), (hi, xbl), (lo, xbh)):
                    for c in range(DC):
                        last = mm(dst, a[:, c, cols], b[:, c, :], start=(k == 0), stop=(k == 3 * DC - 1))
                        k += 1
                last.then_inc(done, 1)

            def params(hf):
                layer_norm(2 + hf)
                pe.wait_ge(ln_sems[2 + hf][4], 4)
                pe.wait_ge(ln_sems[2 + hf][5], 4)
                pe.wait_ge(s_cact, 2)
                pe.wait_ge(s_cdve, 4)
                k = 0
                for a, b in ((wph, xbh), (wph, xbl), (wpl, xbh)):
                    for c in range(DC):
                        last = mm(ps[0:64, 4, :], a[:, c, :], b[:, c, :], start=(k == 0), stop=(k == 3 * DC - 1))
                        k += 1
                last.then_inc(s_pp, 1)

            def spread(hf, p, m, o):
                wait(pe, s_bcc, 3 * PG * (NPASS * hf + p) + m - 1)
                g, j = divmod(m, 3)
                c0 = (PG * p + g) * P
                mm(o, (sel_a, sel_1, sel_1)[j][0:96, c0:c0 + P], pd[0:96, j % 2, :], start=True, stop=True).then_inc(s_bc, 1)

            def first_spread(hf):
                wait(pe, s_pdr, hf + 1)
                for m in range(3 * PG):
                    spread(hf, 0, m, bank(6 + m % 2))

            pe.wait_ge(s_x1, 8)
            params(0)
            for hf in range(2):
                wait(pe, s_yv, NG * hf)
                for v in range(VC):
                    wait(pe, s_cv, 8 * hf + v - 1)
                    if v == 0:
                        pe.wait_ge(s_pe1, 2 * hf + 2)
                    wide(hf, 0, v, bank(4 + v % 2), s_vp)
                if hf == 0:
                    first_spread(0)
                wait(pe, s_bcc, 3 * PG * (NPASS * hf + 1))
                for n in range(8):
                    vq, bp = divmod(n, 4)
                    pe.wait_ge(s_silu, 8 * hf + 4 * vq + 4)
                    wait(pe, s_utc, 8 * hf + n - 1)
                    for c in range(4):
                        last = nc.tensor.transpose(bank(6 + n % 2)[:, c * P:(c + 1) * P],
                                                   val[:, 4 * vq + c, bp * P:(bp + 1) * P], ident[:, :])
                    last.then_inc(s_ut, 1)
                pe.wait_ge(s_vhi, 8 * (hf + 1))
                pe.wait_ge(s_vlo, 8 * (hf + 1))

                def bc(g, j):
                    G = NG * hf + g
                    s = chunk_at(hf, 2 + 2 * g + j // 2)
                    if j % 2 == 0:
                        weights_there(pe, s)
                    wait(pe, s_raw, 4 * (G - 1) + j + 1)
                    if g == 0:
                        wait(pe, s_xo, 4 * hf)
                    hi = wh[:, s % 2, :].rearrange("p (k j n) -> p k j n", k=VC, j=2)
                    lo = wl[:, s % 2, :].rearrange("p (k j n) -> p k j n", k=VC, j=2)
                    k = 0
                    for a, b in ((hi, vh), (hi, vl), (lo, vh)):
                        for c in range(VC):
                            last = mm(bank(j), a[:, c, j % 2, :], b[:, c, :], start=(k == 0), stop=(k == 3 * VC - 1))
                            k += 1
                    last.then_inc(s_bp, 1)

                def ss(g, j):
                    n = 4 * (NG * hf + g) + j
                    pe.wait_ge(s_sq, n + 1)
                    wait(pe, s_lg, n)
                    mm(bank(4), head_ones[:, :], sq[j % 2], start=True, stop=True).then_inc(s_ss, 1)

                def kernels(g):
                    G = NG * hf + g
                    pe.wait_ge(s_bt, G + 1)
                    pe.wait_ge(s_ct, G + 1)
                    wait(pe, s_kk, G)
                    for hp in range(2):
                        if hp == 1:
                            pe.wait_ge(s_kh, G + 1)
                        for bp in range(4):
                            col = hp * 256 + bp * T
                            for j in range(2):
                                for e in range(2):
                                    t0 = (2 * bp + e) * T
                                    for h in (2 * hp, 2 * hp + 1):
                                        last = mm(ps[T * e:T * e + T, 6 + h % 2, col:col + T],
                                                  bt[32 * h:32 * h + 32, j, t0:t0 + T],
                                                  ct[32 * h:32 * h + 32, 1 - j, t0:t0 + T],
                                                  start=(j == 0), stop=(j == 1))
                        if hp == 0:
                            last.then_inc(s_kh, 1)
                    last.then_inc(s_k, 1)

                def outputs(g):
                    G = NG * hf + g
                    pe.wait_ge(s_kk, G + 1)
                    wait(pe, s_yv, G)
                    for e in range(2):
                        if e:
                            pe.wait_ge(s_ye, G + 1)
                        for bp in range(4):
                            for h in range(4):
                                t0 = (2 * bp + e) * T
                                col = (h % 2) * 512 + (h // 2) * 256 + bp * T
                                last = mm(ps[32 * h:32 * h + 32, 5, t0:t0 + T],
                                          ut[T * e:T * e + T, bp, g * P + 32 * h:g * P + 32 * h + 32],
                                          kk[T * e:T * e + T, col:col + T],
                                          start=True, stop=True)
                        if e == 0:
                            last.then_inc(s_ye, 1)
                    last.then_inc(s_yp, 1)

                for g in range(NG):
                    p = g // PG + 1

                    def spread_two(k):
                        if g % PG == 0 and p < NPASS:
                            for m in (2 * k, 2 * k + 1):
                                spread(hf, p, m, bank(6 + m % 2))

                    bc(g, 0)
                    if g > 1:
                        outputs(g - 2)
                    bc(g, 1)
                    ss(g, 0)
                    bc(g, 2)
                    ss(g, 1)
                    wait(pe, s_utc, 8 * (hf + 1))
                    wait(pe, s_kk, NG * hf + g - 1)
                    spread_two(0)
                    bc(g, 3)
                    spread_two(1)
                    ss(g, 2)
                    spread_two(2)
                    if g % PG == 0 and p < NPASS:
                        wait(pe, s_bcc, 3 * PG * (NPASS * hf + p + 1))
                    if g:
                        kernels(g - 1)
                    ss(g, 3)
                for v in range(VC):
                    if v == 1:
                        outputs(NG - 2)
                    if v == 4:
                        kernels(NG - 1)
                    if v == 6:
                        outputs(NG - 1)
                    if v < 4:
                        wait(pe, s_raw, 4 * NG * (hf + 1) - 3 + v)
                    else:
                        wait(pe, s_gs, 8 * hf + v - 3)
                    wide(hf, 2 + 2 * NG, v, bank(v % 4), s_gp)
                if hf == 0:
                    pe.wait_ge(s_kk, NG)
                    params(1)
                for q in range(2):
                    s = chunk_at(hf, 4 + 2 * NG + q)
                    weights_there(pe, s)
                    hi = wh[:, s % 2, :].rearrange("p (k n) -> p k n", k=4)
                    lo = wl[:, s % 2, :].rearrange("p (k n) -> p k n", k=4)
                    pe.wait_ge(s_ghi, 8 * hf + 4 * q + 4)
                    pe.wait_ge(s_glo, 8 * hf + 4 * q + 4)
                    if q == 0:
                        wait(pe, s_gs, 8 * (hf + 1))
                    for t in range(4):
                        if hf == 0 and q == 1 and t == 2:
                            first_spread(1)
                        if hf == 1 and q == 1 and t == 2:
                            pe.wait_ge(s_yv, 2 * NG)
                            pe.wait_ge(s_lg, 8 * NG)
                            layer_norm(4)
                        k = 0
                        for a, b in ((vh, hi), (vh, lo), (vl, hi)):
                            for c in range(4):
                                last = mm(bank(t), a[:, 4 * q + c, t * P:(t + 1) * P], b[:, c, :],
                                          start=(q == 0 and k == 0), stop=(q == 1 and k == 11))
                                k += 1
                        last.then_inc((s_oq, s_op)[q], 1)

            pe.wait_ge(s_xo, 8)
            layer_norm(5)
            pe.wait_ge(s_pb, 1)
            mm(ps[:, 6, 0:NP], ones[0:NP, :], p2d[0:NP, :], start=True, stop=True).then_inc(s_pb, 1)
            for k in (4, 5):
                pe.wait_ge(ln_sems[k][4], 4)
                pe.wait_ge(ln_sems[k][5], 4)
            for t in range(8):
                k = 0
                for a, b in ((xch, pth), (xch, ptl), (xcl, pth)):
                    for c in range(DC):
                        last = mm(ps[:, 7, t * NP:(t + 1) * NP], a[:, c, t * P:(t + 1) * P], b[:, c, :],
                                  start=(k == 0), stop=(k == 3 * DC - 1))
                        k += 1
            last.then_inc(s_xp, 1)
            sB, sA = len(SEQ) - 2, len(SEQ) - 1
            Wb = wh[:, sB % 2, :].rearrange("p (c n) -> p c n", c=DC), wl[:, sB % 2, :].rearrange("p (c n) -> p c n", c=DC)
            Wa = wh[:, sA % 2, :].rearrange("p (c n) -> p c n", c=DC), wl[:, sA % 2, :].rearrange("p (c n) -> p c n", c=DC)

            def h_tile(t):
                wait(pe, s_hw, t - 1)
                k = 0
                for a, b in ((xch, Wb[0]), (xch, Wb[1]), (xcl, Wb[0])):
                    for c in range(DC):
                        last = mm(bank(t % 2), a[:, c, t * P:(t + 1) * P], b[:, c, :], start=(k == 0), stop=(k == 3 * DC - 1))
                        k += 1
                last.then_inc(s_hp, 1)

            weights_there(pe, sB)
            h_tile(0)
            h_tile(1)
            pe.wait_ge(s_wn, 1)
            pe.wait_ge(s_pb, 3)
            for t in range(8):
                last = nc.tensor.transpose(ps[0:NP, 6, (t % 4) * P:(t % 4 + 1) * P], wn[:, t, :], ident[:, :])
                if t % 4 == 3:
                    last.then_inc(s_wtt, 1)
                    pe.wait_ge(s_wt, t // 4 + 1)
            weights_there(pe, sA)
            pe.wait_ge(s_late, 32)
            for t in range(8):
                pe.wait_ge(s_hw, t + 1)
                wait(pe, s_hhi, t - 1)
                wait(pe, s_hlo, t - 1)
                for c in range(DC):
                    last = nc.tensor.transpose(bank(4 + t % 2)[:, c * P:(c + 1) * P], hw[:, t % 2, c * P:(c + 1) * P], ident[:, :])
                last.then_inc(s_ht, 1)
                if t + 2 < 8:
                    h_tile(t + 2)
                wait(pe, s_fo, t - 1)
                o = bank(2 + t % 2)
                mm(o, wt[0:NP, t, :], ebias, start=True, stop=False)
                pe.wait_ge(s_hhi, t + 1)
                pe.wait_ge(s_hlo, t + 1)
                k = 0
                for a, b in ((hh, Wa[0]), (hh, Wa[1]), (hl, Wa[0])):
                    for c in range(DC):
                        last = mm(o, a[:, t % 2, c, :], b[:, c, :], start=False, stop=(k == 3 * DC - 1))
                        k += 1
                last.then_inc(s_fp, 1)

        @block.scalar
        def _(act):
            n = [0]
            f = nc.scalar.activation

            def link(ins):
                n[0] += 1
                ins.then_inc(s_act, 1)
                act.wait_ge(s_act, n[0])

            def layer_norm(k, hi_t, t0=0):
                var, stdd, xnr, tr, hi, lo = ln_sems[k]
                xn, banks = LN[k]
                tt = slice(4 * (k % 2), 4 * (k % 2) + 4)
                act.wait_ge(var, 1)
                f(std[:, tt], rstd[:, tt], ACT.Sqrt).then_inc(stdd, 1)
                for i in range(4):
                    act.wait_ge(tr, i + 1)
                    src = ps[:, banks[i % 2], :].rearrange("p (c t) -> p c t", c=DC)
                    if k >= 4:
                        wait(act, s_xx, t0 + i)
                        f(xsq, xn[:, i % 2, :], ACT.Square, accum_out=x2[:, t0 + i:t0 + i + 1]).then_inc(s_xx, 1)
                    f(hi_t[:, :, (t0 + i) * P:(t0 + i + 1) * P], src, ACT.Copy, scale=XS).then_inc(hi, 1)

            layer_norm(0, xah)
            layer_norm(1, xah, 4)
            nc.scalar.preload_act_table_set("natural_log_exp_and_others")
            act.wait_ge(s_small, 6 * 16)
            act.wait_ge(s_proto, 2 * 16)
            f(amat[:, :], alog[:, :], ACT.Exp).then_inc(s_cact, 1)
            f(wph[:, :, :], wp[:, :, :], ACT.Copy, scale=WS).then_inc(s_cact, 1)
            f(pth[:, :, :], proto_t[:, :, :], ACT.Copy, scale=WS).then_inc(s_cact, 1)
            for u in range(8):
                n2, m = divmod(u, 4)
                act.wait_ge(s_q, u + 1)
                for j in range(4):
                    dst = qs[0:32, :].rearrange("p (b h t) -> p b h t", b=B, h=H)[:, n2 * HB:(n2 + 1) * HB, 4 * m + j, :]
                    last = f(dst, ps[32 * j:32 * j + 32, QB[m], :].rearrange("p (b t) -> p b t", b=HB), ACT.Copy,
                             scale=1.0 / WS)
                last.then_inc(s_qhi, 1)

            def kv(b, u, p):
                if p == 0:
                    wait(act, s_pv, KT * (b - 1))
                act.wait_ge(s_item, ITEMS * b + p + 1)
                for r in range(2):
                    k0, w = BLK[2 * p + r]
                    f(ks[u][0:32, k0:k0 + w], ps[64 * r:64 * r + 32, 5 + p, 0:w], ACT.Copy, scale=XS)
                    f(vt[96:128, k0:k0 + w], ps[64 * r + 32:64 * r + 64, 5 + p, 0:w], ACT.Copy).then_inc(s_khi, 1)

            def probs(b, u, kt):
                k = KT * b + kt
                s = (KT * u + kt) % 2
                nk = min(P, NKEY - kt * P)
                wait(act, s_pv, k - 1)
                act.wait_ge(s_s2, k + 1)
                f(pr[s][0:nk, :].rearrange("p (q n) -> p q n", q=2), ps[0:nk, 2 * s:2 * s + 2, :], ACT.Exp,
                  scale=SC).then_inc(s_exp, 1)

            def attn_hi(b, u):
                wait(act, s_pvfree, b + 1)
                f(oth[:, :, bass.ds(b * T, T)], on[u], ACT.Copy, scale=XS).then_inc(s_oh, 1)

            def batch(b, u, first=False, more=True):
                for kt in range(KT):
                    probs(b, u, kt)
                    if kt == 0 and not first:
                        attn_hi(b - 1, 1 - u)
                    if more and kt < 2:
                        kv(b + 1, 1 - u, kt)

            act.wait_ge(s_cdve, 1)
            for p in range(2):
                kv(0, 0, p)
            batch(0, 0, first=True)
            batch(1, 1)
            with act.Fori(1, B // 2 - 1) as i:
                batch(2 * i, 0)
                batch(2 * i + 1, 1)
            batch(B - 2, 0)
            batch(B - 1, 1, more=False)
            attn_hi(B - 1, 1)

            def params(hf):
                wait(act, s_gp, 8 * hf)
                layer_norm(2 + hf, xbh)
                nc.scalar.preload_act_table_set("natural_log_exp_and_others")
                act.wait_ge(s_pp, hf + 1)
                f(cp[0:32, 0, :], ps[0:32, 4, :], ACT.Exp, bias=dtb[:, 0:1], scale=UNS).then_inc(s_pe1, 1)
                k = cp[0:32, 3, :]
                link(f(k, ps[32:64, 4, :], ACT.Exp, scale=-UNS))
                link(f(k, k, ACT.Ln, bias=1.0))
                f(k, k, ACT.Exp, scale=-1.0).then_inc(s_pe1, 1)

            def spread(hf, p, m):
                g, j = divmod(m, 3)
                act.wait_ge(s_bc, 3 * PG * (NPASS * hf + p) + m + 1)
                dst = coef[p % 2][:, j, g, :] if j < 2 else ndt[p % 2][:, g, :]
                f(dst, ps[:, 6 + m % 2, :], ACT.Copy, scale=(1.0 / (DS * AS), 1.0 / DS, -1.0 / DS)[j],
                  bias=(0.0, 1.0, 0.0)[j]).then_inc(s_bcc, 1)

            params(0)
            for hf in range(2):
                def last_tap(v):
                    act.wait_ge(s_vp, 8 * hf + v + 1)
                    f(raw[:, v % 2, :], ps[:, 4 + v % 2, :], ACT.Copy, scale=conv_w[:, v, 3:4]).then_inc(s_cm, 1)

                wait(act, s_bt, 8 * hf)
                last_tap(0)
                for v in range(VC):
                    if v + 1 < VC:
                        last_tap(v + 1)
                    act.wait_ge(s_cv, 8 * hf + v + 1)
                    f(val[:, v, :], raw[:, v % 2, :], ACT.Silu, bias=conv_b[:, v:v + 1], scale=UNS).then_inc(s_silu, 1)
                    act.wait_ge(s_silu, 8 * hf + v + 1)
                    f(vh[:, v, :], val[:, v, :], ACT.Copy, scale=XS).then_inc(s_vhi, 1)
                if hf == 0:
                    for m in range(3 * PG):
                        spread(0, 0, m)
                for m in range(8):
                    vq, bp = divmod(m, 4)
                    act.wait_ge(s_ut, 8 * hf + m + 1)
                    f(ut[:, bp, 512 * vq:512 * vq + 512], ps[:, 6 + m % 2, :], ACT.Copy).then_inc(s_utc, 1)
                nc.scalar.preload_act_table_set("natural_log_exp_and_others")
                for g in range(NG):
                    G = NG * hf + g
                    p = g // PG + 1

                    def spread_two(k):
                        if g % PG == 0 and p < NPASS:
                            for m in (2 * k, 2 * k + 1):
                                spread(hf, p, m)

                    def norm(j):
                        N = 4 * G + j
                        r = rn[:, j, :]
                        act.wait_ge(s_ss, N + 1)
                        wait(act, s_normed, G)
                        if j >= 2:
                            wait(act, s_ct, G)
                        f(r, ps[:, 4, :], ACT.Ln, bias=tiny[:, 0:1]).then_inc(s_lg, 1)
                        act.wait_ge(s_lg, N + 1)
                        link(f(r, r, ACT.Exp, scale=0.5))
                        link(f(r, r, ACT.Ln, bias=tiny[:, 1:2]))
                        f(r, r, ACT.Exp, scale=-1.0).then_inc(s_rn, 1)

                    for j in range(4):
                        N = 4 * G + j
                        act.wait_ge(s_bp, N + 1)
                        wait(act, s_ss, N - 1)
                        f(sq[j % 2], ps[:, j, :], ACT.Square, scale=UNS).then_inc(s_sq, 1)
                        if j < 2:
                            wait(act, s_drive, G)
                        else:
                            wait(act, s_bt, G)
                            wait(act, s_ct, G)
                        f(raw[:, j, :], ps[:, j, :], ACT.Copy, scale=UNS).then_inc(s_raw, 1)
                        if j == 3:
                            spread_two(1)
                        if j:
                            norm(j - 1)
                        if j >= 2:
                            spread_two(2 * (j - 2))
                    norm(3)
                    d = dd[(p - 1) % 2]
                    act.wait_ge(s_det, G + 1)
                    link(f(d[:, 1, :], d[:, 1, :], ACT.Ln))
                    link(f(d[:, 1, :], d[:, 1, :], ACT.Exp, scale=-1.0))
                    f(d[:, 0, :], d[:, 1, :], ACT.Copy, scale=-1.0).then_inc(s_dinv, 1)
                for v in range(VC):
                    act.wait_ge(s_gp, 8 * hf + v + 1)
                    wait(act, s_bt, 8 * hf + 8)
                    wait(act, s_ct, 8 * hf + 8)
                    f(gate[:, v, :], ps[:, v % 4, :], ACT.Silu, scale=UNS).then_inc(s_gs, 1)
                for v in range(VC):
                    if v == 4 and hf == 0:
                        params(1)
                    act.wait_ge(s_gy, 8 * hf + v + 1)
                    f(vh[:, v, :], val[:, v, :], ACT.Copy, scale=XS).then_inc(s_ghi, 1)
                if hf == 0:
                    for m in range(3 * PG):
                        spread(1, 0, m)

            layer_norm(4, xch)
            layer_norm(5, xch, 4)
            act.wait_ge(s_xx, 8)
            act.wait_ge(s_late, 32)
            f(xsq[0:NP, :], proto, ACT.Square, accum_out=p2[:, :]).then_inc(s_cact, 1)
            act.wait_ge(s_d2, 1)
            f(ds, fa, ACT.Sqrt).then_inc(s_sqd, 1)
            act.wait_ge(s_dif, 1)
            f(ew, ds, ACT.Exp, scale=nit[:, 3:4]).then_inc(s_e, 1)
            for q in range(2):
                act.wait_ge(s_wtt, q + 1)
                f(wt[0:NP, 4 * q:4 * q + 4, :], ps[0:NP, 6, :].rearrange("p (t n) -> p t n", t=4), ACT.Copy,
                  scale=XS * WS).then_inc(s_wt, 1)
            for t in range(8):
                act.wait_ge(s_ht, t + 1)
                wait(act, s_fp, t - 1)
                f(hh[:, t % 2, :, :], ps[:, 4 + t % 2, :].rearrange("p (c n) -> p c n", c=DC), ACT.Copy,
                  scale=XS).then_inc(s_hhi, 1)

        @block.vector
        def _(dve):
            n = [0]
            V = nc.vector

            def link(ins):
                n[0] += 1
                ins.then_inc(s_dve, 1)
                dve.wait_ge(s_dve, n[0])

            def moments(k, ready):
                tiles = range(4 * (k % 2), 4 * (k % 2) + 4)
                for i in tiles:
                    ready(i)
                    link(V.bn_stats(stats[:, i, :], x[:, i, :]))
                    link(V.bn_aggr(mv[:, i, :], stats[:, i, :]))
                V.tensor_scalar(rstd[:, tiles[0]:tiles[0] + 4], mv[:, tiles[0]:tiles[0] + 4, 1], EPS, None,
                                ALU.add).then_inc(ln_sems[k][0], 1)

            def normalise(k, hi_t, lo_t, t0=0):
                var, stdd, xnr, tr, hi, lo = ln_sems[k]
                xn, banks = LN[k]
                x0 = 4 * (k % 2)
                dve.wait_ge(stdd, 1)
                link(V.reciprocal(rstd[:, x0:x0 + 4], std[:, x0:x0 + 4]))

                def normed(i):
                    wait(dve, tr, i - 1)
                    if k >= 4:
                        wait(dve, s_xx, t0 + i - 1)
                    V.tensor_scalar(xn[:, i % 2, :], x[:, x0 + i, :], mv[:, x0 + i, 0:1], rstd[:, x0 + i:x0 + i + 1],
                                    ALU.subtract, ALU.mult).then_inc(xnr, 1)

                normed(0)
                for i in range(4):
                    if i + 1 < 4:
                        normed(i + 1)
                    dve.wait_ge(tr, i + 1)
                    dve.wait_ge(hi, i + 1)
                    src = ps[:, banks[i % 2], :].rearrange("p (c t) -> p c t", c=DC)
                    cols = slice((t0 + i) * P, (t0 + i + 1) * P)
                    V.scalar_tensor_tensor(lo_t[:, :, cols], src, XS, hi_t[:, :, cols], ALU.mult,
                                           ALU.subtract).then_inc(lo, 1)

            link(V.memset(tiny[:, 0:1], 1e-19))
            link(V.memset(tiny[:, 1:2], 1e-8))
            link(V.memset(head_ones[:, :], 0.0))
            for h in range(4):
                link(V.memset(head_ones[32 * h:32 * h + 32, 32 * h:32 * h + 32], 1.0))
            link(V.memset(ones[:, :], 1.0))
            link(V.memset(sel_1[:, :], 0.0))

            for k in range(2):
                moments(k, lambda i: dve.wait_ge(s_x[k], 4 * 16))
                normalise(k, xah, xal, 4 * k)
            for u in range(2):
                last = V.memset(ks[u][96:104, 0:NKEY], MS)
            last.then_inc(s_cdve, 1)
            for u in range(8):
                n2, m = divmod(u, 4)
                dve.wait_ge(s_qhi, u + 1)
                view = [qs[32 * r:32 * r + 32, :].rearrange("p (b h t) -> p b h t", b=B, h=H)[:, n2 * HB:(n2 + 1) * HB]
                        for r in range(3)]
                V.tensor_copy(view[1][:, :, 4 * m:4 * m + 4, :], view[0][:, :, 4 * m:4 * m + 4, :])
                for j in range(4):
                    h = 4 * m + j
                    last = V.scalar_tensor_tensor(view[2][:, :, h, :], ps[32 * j:32 * j + 32, QB[m], :].rearrange(
                        "p (b t) -> p b t", b=HB), 1.0 / WS, view[0][:, :, h, :], ALU.mult, ALU.subtract)
                last.then_inc(s_qlo, 1)

            def attn_lo(b, u):
                dve.wait_ge(s_oh, b + 1)
                cols = bass.ds(b * T, T)
                V.scalar_tensor_tensor(otl[:, :, cols], on[u], XS, oth[:, :, cols], ALU.mult, ALU.subtract).then_inc(s_ol, 1)

            def prepare(b, u, low=False):
                for p, (k0, w) in enumerate(BLK):
                    r = p % 2
                    dve.wait_ge(s_khi, 4 * b + p + 1)
                    last = V.scalar_tensor_tensor(ks[u][32:64, k0:k0 + w], ps[64 * r:64 * r + 32, 5 + p // 2, 0:w], XS,
                                                  ks[u][0:32, k0:k0 + w], ALU.mult, ALU.subtract)
                    last = V.tensor_copy(ks[u][64:96, k0:k0 + w], ks[u][0:32, k0:k0 + w])
                    if r:
                        last.then_inc(s_itemfree, 1)
                if low:
                    attn_lo(b - 2, u)
                dve.wait_ge(s_item, ITEMS * b + 3)
                wait(dve, s_pv, KT * (b - 1))
                vp = ps[:, 7, 0:KT * 32].rearrange("p (k n) -> p k n", k=KT)
                V.tensor_copy(vv[u][:, 0:KT - 1, :], vp[:, 0:KT - 1, :])
                nk = NKEY - (KT - 1) * P
                last = V.tensor_copy(vv[u][0:nk, KT - 1, :], vp[0:nk, KT - 1, :])
                last.then_inc(s_itemfree, 1)
                for i in range(8):
                    for k, (k0, w) in enumerate(BLK):
                        p = 3 + 4 * i + k
                        dve.wait_ge(s_item, ITEMS * b + p + 1)
                        V.tensor_reduce(mxp[:, i, k:k + 1], ps[:, 5 + p % 3, 0:w], AX.X, ALU.max).then_inc(s_itemfree, 1)
                dve.wait_ge(s_itemfree, ITEMS * b + 35)
                V.tensor_reduce(mx, mxp, AX.X, ALU.max, negate=True).then_inc(s_mx, 1)
                dve.wait_ge(s_item, ITEMS * b + 36)
                V.tensor_tensor(qs[96:104, bass.ds(b * 1024, 1024)].rearrange("p (i n) -> p i n", i=8),
                                ps[0:8, 7, 0:P].unsqueeze(1).to_broadcast([8, 8, P]), eye8[:, :, :],
                                ALU.mult).then_inc(s_itemfree, 1)

            def finish(b, u):
                dve.wait_ge(s_pv, KT * (b + 1))
                o = ps[:, 4, :].rearrange("p (k c t) -> p k c t", k=2, c=DC)
                V.reciprocal(rl, o[:, 1]).then_inc(s_rl, 1)
                dve.wait_ge(s_rl, b + 1)
                V.tensor_tensor(on[u], o[:, 0], rl, ALU.mult).then_inc(s_pvfree, 1)

            prepare(0, 0)
            dve.wait_ge(s_const, 4)
            dve.wait_ge(s_cact, 3)
            dve.wait_ge(s_proto, 2 * 16)
            diag = ident[0:32, 0:32].unsqueeze(2).to_broadcast([32, 32, 32])
            hv = "p (h n) -> p h n"
            link(V.tensor_scalar(ah[:, :], amat[:, :], AS, None, ALU.mult))
            link(V.scalar_tensor_tensor(al[:, :], amat[:, :], AS, ah[:, :], ALU.mult, ALU.subtract))
            for row, a in ((0, ah), (32, ah), (64, al)):
                last = V.tensor_tensor(sel_a[row:row + 32, :].rearrange(hv, h=32), a[:, :].unsqueeze(1).to_broadcast([32, 32, 32]),
                                       diag, ALU.mult)
            last.then_inc(s_cdve, 1)
            V.tensor_copy(sel_1[0:32, :].rearrange(hv, h=32), diag)
            V.tensor_copy(sel_1[32:64, :].rearrange(hv, h=32), diag).then_inc(s_cdve, 1)
            V.scalar_tensor_tensor(wpl[:, :, :], wp[:, :, :], WS, wph[:, :, :], ALU.mult, ALU.subtract).then_inc(s_cdve, 1)
            V.scalar_tensor_tensor(ptl[:, :, :], proto_t[:, :, :], WS, pth[:, :, :], ALU.mult, ALU.subtract)
            link(V.tensor_scalar(nit[:, 1:2], nit[:, 0:1], -1.0, None, ALU.mult))
            link(V.tensor_tensor(nit[:, 1:2], nit[:, 0:1], nit[:, 1:2], ALU.max))
            link(V.tensor_scalar(nit[:, 1:2], nit[:, 1:2], 0.1, None, ALU.max))
            link(V.reciprocal(nit[:, 2:3], nit[:, 1:2]))
            link(V.tensor_scalar(nit[:, 3:4], nit[:, 2:3], -1.0, None, ALU.mult))
            prepare(1, 1)
            finish(0, 0)
            prepare(2, 0, low=True)
            finish(1, 1)
            with dve.Fori(1, B // 2 - 1) as i:
                prepare(2 * i + 1, 1, low=True)
                finish(2 * i, 0)
                prepare(2 * i + 2, 0, low=True)
                finish(2 * i + 1, 1)
            prepare(B - 1, 1, low=True)
            finish(B - 2, 0)
            attn_lo(B - 2, 0)
            finish(B - 1, 1)
            attn_lo(B - 1, 1)
            def attn_residual(t):
                dve.wait_ge(s_y, t + 1)
                V.scalar_tensor_tensor(x[:, t, :], ps[:, t % 2, :], UNS, x[:, t, :], ALU.mult, ALU.add).then_inc(s_x1, 1)
                dve.wait_ge(s_x1, t + 1)

            moments(2, attn_residual)
            for t in range(4, 8):
                attn_residual(t)

            def params(hf):
                dve.wait_ge(s_pe1, 2 * hf + 2)
                y, r, kd = (cp[0:32, j, :] for j in (0, 2, 3))
                if hf == 0:
                    dve.wait_ge(s_pdz, 1)
                link(V.tensor_scalar(y, y, 0.11, None, ALU.min))
                link(V.tensor_scalar(r, y, LOG1P[-1], None, ALU.mult))
                for c in LOG1P[-2::-1]:
                    link(V.scalar_tensor_tensor(r, r, c, y, ALU.add, ALU.mult))
                dt, dk = cp[0:32, 1, :], r
                link(V.tensor_scalar(dt, r, 1e-4, 0.1, ALU.max, ALU.min))
                V.tensor_scalar(pd[0:32, 0, :], dt, DS, None, ALU.mult)
                link(V.scalar_tensor_tensor(dk, kd, 0.5, dt, ALU.mult, ALU.mult))
                link(V.tensor_scalar(pd[0:32, 1, :], dk, DS, None, ALU.mult))
                V.tensor_copy(pd[64:96, 0, :], pd[0:32, 0, :])
                V.scalar_tensor_tensor(pd[32:64, 0, :], dt, DS, pd[0:32, 0, :], ALU.mult, ALU.subtract)
                V.scalar_tensor_tensor(pd[32:64, 1, :], dk, DS, pd[0:32, 1, :], ALU.mult, ALU.subtract).then_inc(s_pdr, 1)

            def start(hf, p):
                w = psi[p % 2].rearrange("p c (s k) t -> p c s k t", k=CS)
                if p:
                    dve.wait_ge(s_ct, NG * hf + PG * (p - 1))
                last = None
                for c, first, then in ((0, 0.0, 1.0), (1, 1.0, 0.0), (2, -1.0, 0.0), (3, 0.0, 1.0)):
                    V.memset(w[:, c, :, 0, 0], first)
                    last = V.memset(w[:, c, :, 1, 0], then)
                link(last)
                dve.wait_ge(s_bcc, 3 * PG * (NPASS * hf + p + 1))

            def recur(hf, p, t0, t1):
                w, sk = psi[p % 2], skew[p % 2]
                R0 = 3 * ST * (NPASS * hf + p) + 3 * t0
                cj = coef[p % 2].rearrange("p j g (b t) -> p j (g b) t", t=ST)
                nd4 = ndt[p % 2].rearrange("p g (b t) -> p (g b) t", t=ST)
                sh = [P, 2, 2, NS]

                def at(a, t):
                    return a[:, :, :, bass.ds(t, 1)].rearrange("p r s o -> p r (s o)")

                def step(t, r):
                    q, p_, c = at(w[:, 0:2], t), at(w[:, 2:4], t), at(cj, t)
                    n_ = nd4[:, :, bass.ds(t, 1)].rearrange("p s o -> p (s o)")
                    V.tensor_tensor(rm, p_.unsqueeze(1).to_broadcast(sh), c.unsqueeze(2).to_broadcast(sh),
                                    ALU.mult).then_inc(s_rec, 1)
                    V.tensor_tensor(at(w[:, 2:4], t + 1), q, n_.unsqueeze(1).to_broadcast([P, 2, NS]),
                                    ALU.mult).then_inc(s_rec, 1)
                    dve.wait_ge(s_rec, r + 2)
                    V.tensor_tensor(w[:, :, :, bass.ds(t + 1, 1)].rearrange("p (j r) s o -> p j (r s o)", j=2),
                                    rm.rearrange("p j r s -> p j (r s)"), at(sk, t), ALU.add).then_inc(s_rec, 1)
                    dve.wait_ge(s_rec, r + 3)

                UN = 8
                with dve.Fori(0, (t1 - t0) // UN) as tb:
                    for k in range(UN):
                        step(tb * UN + (t0 + k), R0 + tb * (3 * UN) + 3 * k)

            normalise(2, xbh, xbl)
            for hf in range(2):
                def split_value(v):
                    dve.wait_ge(s_vhi, 8 * hf + v + 1)
                    V.scalar_tensor_tensor(vl[:, v, :], val[:, v, :], XS, vh[:, v, :], ALU.mult, ALU.subtract).then_inc(s_vlo, 1)

                def split_gated(v):
                    dve.wait_ge(s_ghi, 8 * hf + v + 1)
                    V.scalar_tensor_tensor(vl[:, v, :], val[:, v, :], XS, vh[:, v, :], ALU.mult, ALU.subtract).then_inc(s_glo, 1)

                for v in range(VC):
                    dve.wait_ge(s_cm, 8 * hf + v + 1)
                    o = raw[:, v % 2, :].rearrange("p (b t) -> p b t", b=HB)
                    src = ps[:, 4 + v % 2, :].rearrange("p (b t) -> p b t", b=HB)
                    for k in (2, 1, 0):
                        s = 3 - k
                        ins = V.scalar_tensor_tensor(o[:, :, s:T], src[:, :, 0:T - s], conv_w[:, v, k:k + 1], o[:, :, s:T],
                                                     ALU.mult, ALU.add)
                        if k:
                            link(ins)
                        else:
                            ins.then_inc(s_cv, 1)
                    if v:
                        split_value(v - 1)
                    if v == 1 and hf == 0:
                        params(0)
                split_value(VC - 1)
                if hf == 0:
                    start(0, 0)
                recur(hf, 0, hf * EARLY, ST)

                def join(g):
                    gi = g % PG
                    w = psi[g // PG % 2][:, :, gi * HS:(gi + 1) * HS].rearrange("p c (s k) t -> p c s k t", k=CS)
                    sh = [P, 2, HB, ST]
                    a, b = (t2[:, k, :].rearrange("p (r s t) -> p r s t", r=2, t=ST) for k in range(2))
                    for c in range(2):
                        V.tensor_tensor(a, w[:, 2 * c, :, 1, 1:].unsqueeze(1).to_broadcast(sh),
                                        w[:, 0:2, :, 0, ST:].to_broadcast(sh), ALU.mult)
                        link(V.tensor_tensor(b, w[:, 2 * c + 1, :, 1, 1:].unsqueeze(1).to_broadcast(sh),
                                             w[:, 2:4, :, 0, ST:].to_broadcast(sh), ALU.mult))
                        link(V.tensor_tensor(w[:, 2 * c:2 * c + 2, :, 1, 1:], a, b, ALU.add))
                    link(V.tensor_copy(w[:, :, :, 1, 0], w[:, :, :, 0, ST]))


                def masked(g):
                    G = NG * hf + g
                    dve.wait_ge(s_k, G + 1)
                    wait(dve, s_yp, G)
                    V.tensor_tensor(kk.rearrange("p (n t) -> p n t", t=T),
                                    ps[:, 6:8, :].rearrange("p a (n t) -> p (a n) t", t=T),
                                    causal[:, :].unsqueeze(1).to_broadcast([P, 16, T]), ALU.mult).then_inc(s_kk, 1)

                def outputs(g):
                    G = NG * hf + g
                    dve.wait_ge(s_yp, G + 1)
                    V.scalar_tensor_tensor(val[:, g, :], val[:, g, :], skip[:, g:g + 1], ps[:, 5, :], ALU.mult,
                                           ALU.add).then_inc(s_yv, 1)

                def determinant(g):
                    gi = g % PG
                    w, d = (a[g // PG % 2] for a in (psi, dd))
                    sl = slice(gi * HS, (gi + 1) * HS)
                    q_, p_ = w[:, 0:2, sl, 1:ST + 1], w[:, 2:4, sl, 1:ST + 1]
                    d1 = d[:, 1, :].rearrange("p (b t) -> p b t", b=HS)
                    d0 = d[:, 0, :].rearrange("p (b t) -> p b t", b=HS)
                    wait(dve, s_dinv, NG * hf + g)
                    wait(dve, s_ct, NG * hf + g)
                    V.tensor_tensor(d0, p_[:, 0], q_[:, 1], ALU.mult)
                    link(V.tensor_tensor(d1, p_[:, 1], q_[:, 0], ALU.mult))
                    V.tensor_tensor(d1, d1, d0, ALU.subtract).then_inc(s_det, 1)

                def vectors(g):
                    G = NG * hf + g
                    gi = g % PG
                    w, cf, nt, d = (a[g // PG % 2] for a in (psi, coef, ndt, dd))
                    sl = slice(gi * HS, (gi + 1) * HS)
                    bt4 = "p j (b t) -> p j b t"
                    q_, p_ = w[:, 0:2, sl, 1:ST + 1], w[:, 2:4, sl, 1:ST + 1]
                    q0, p0 = w[:, 0:2, sl, 0:ST], w[:, 2:4, sl, 0:ST]
                    full = [P, 2, HS, ST]

                    def rows(a):
                        return a.rearrange("p (b t) -> p b t", b=HS).unsqueeze(1).to_broadcast(full)

                    def v4(a):
                        return a.rearrange(bt4, b=HS)

                    dve.wait_ge(s_rn, 4 * G + 4)
                    V.tensor_tensor(raw, raw, rn, ALU.mult).then_inc(s_normed, 1)
                    dve.wait_ge(s_normed, G + 1)
                    nd2 = nt[:, gi, :].unsqueeze(1).to_broadcast([P, 2, HT])
                    V.tensor_tensor(t1, raw[:, 0:2, :], nd2, ALU.mult).then_inc(s_drive, 1)
                    dve.wait_ge(s_drive, G + 1)
                    link(V.tensor_tensor(t2[:, 0, :], t1[:, 1, :], cf[:, 0, gi, :], ALU.mult))
                    link(V.tensor_tensor(t1[:, 0, :], t1[:, 0, :], t2[:, 0, :], ALU.add))
                    V.tensor_tensor(v4(bt), p0, rows(t1[:, 0, :]), ALU.mult)
                    link(V.tensor_tensor(v4(t2), q0, rows(t1[:, 1, :]), ALU.mult))
                    V.tensor_tensor(bt, bt, t2, ALU.add).then_inc(s_bt, 1)
                    dve.wait_ge(s_bt, G + 1)

                join(0)
                determinant(0)
                for g in range(NG):
                    vectors(g)
                    p, r = g // PG + 1, g % PG
                    if p < NPASS:
                        if r == 0:
                            start(hf, p)
                        recur(hf, p, r * (ST // PG), (r + 1) * (ST // PG))
                    if g + 1 < NG:
                        join(g + 1)
                        determinant(g + 1)
                    if g > 0:
                        outputs(g - 1)
                    if hf == 0 and g == NG - 1:
                        moments(3, lambda i: dve.wait_ge(s_x1, i + 1))
                    masked(g)
                outputs(NG - 1)
                for v in range(VC):
                    if v == 4 and hf == 0:
                        split_gated(v - 1)
                        dve.wait_ge(s_gp, 8)
                        normalise(3, xbh, xbl)
                    dve.wait_ge(s_gs, 8 * hf + v + 1)
                    V.tensor_tensor(val[:, v, :], val[:, v, :], gate[:, v, :], ALU.mult).then_inc(s_gy, 1)
                    if v and not (v == 4 and hf == 0):
                        split_gated(v - 1)
                split_gated(VC - 1)
                if hf == 0:
                    params(1)
                    start(1, 0)
                    recur(1, 0, 0, EARLY)

                def residual(t):
                    dve.wait_ge(s_op, t + 1)
                    V.scalar_tensor_tensor(x[:, t, :], ps[:, t % 4, :], UNS, x[:, t, :], ALU.mult, ALU.add).then_inc(s_xo, 1)

                if hf == 0:
                    for t in range(4):
                        residual(t)
                else:
                    def residual_there(t):
                        residual(t)
                        dve.wait_ge(s_xo, t + 1)

                    moments(4, lambda i: dve.wait_ge(s_xo, i + 1))
                    normalise(4, xch, xcl)
                    moments(5, residual_there)
                    normalise(5, xch, xcl, 4)

            dve.wait_ge(s_xx, 8)
            dve.wait_ge(s_cact, 4)
            V.tensor_scalar(p2d[0:NP, :], ident[0:NP, 0:NP], p2[:, 0:1], None, ALU.mult).then_inc(s_pb, 1)
            dve.wait_ge(s_pb, 2)
            V.tensor_copy(p2b, ps[:, 6, 0:NP]).then_inc(s_pb, 1)
            dve.wait_ge(s_pb, 3)
            sh3 = [P, 8, NP]
            link(V.tensor_tensor(fa, p2b.unsqueeze(1).to_broadcast(sh3), x2.unsqueeze(2).to_broadcast(sh3), ALU.add))
            dve.wait_ge(s_xp, 1)
            link(V.scalar_tensor_tensor(fa, ps[:, 7, 0:8 * NP].rearrange("p (t n) -> p t n", t=8), -2.0 * UNS, fa,
                                        ALU.mult, ALU.add))
            V.tensor_scalar(fa, fa, 0.0, None, ALU.max).then_inc(s_d2, 1)
            dve.wait_ge(s_d2, 1)
            link(V.tensor_scalar(nd, fa, -1.0, None, ALU.mult))
            for t in range(8):
                ins = V.max(top[:, t, :], nd[:, t, :])
            link(ins)
            for t in range(8):
                ins = V.max_index(topi[:, t, :], top[:, t, :], nd[:, t, :])
            link(ins)
            link(V.tensor_copy(topf, topi))
            dve.wait_ge(s_iota, 1)
            iob = io[:, :].unsqueeze(1).to_broadcast(sh3)
            V.tensor_tensor(m0, topf[:, :, 0:1].to_broadcast(sh3), iob, ALU.is_equal)
            link(V.tensor_tensor(m1, topf[:, :, 1:2].to_broadcast(sh3), iob, ALU.is_equal))
            link(V.tensor_tensor(m0, m0, m1, ALU.add))
            dve.wait_ge(s_sqd, 1)
            link(V.tensor_reduce(dm, ds, AX.X, ALU.min))
            V.tensor_tensor(ds, ds, dm.unsqueeze(2).to_broadcast(sh3), ALU.subtract).then_inc(s_dif, 1)
            dve.wait_ge(s_e, 1)
            link(V.tensor_tensor(ew, ew, m0, ALU.mult))
            link(V.tensor_reduce(es_sum, ew, AX.X, ALU.add))
            link(V.reciprocal(es_sum, es_sum))
            V.tensor_tensor(wn, ew, es_sum.unsqueeze(2).to_broadcast(sh3), ALU.mult).then_inc(s_wn, 1)
            dve.wait_ge(s_wn, 1)

            def weighted(t):
                dve.wait_ge(s_hp, t + 1)
                wait(dve, s_ht, t - 1)
                V.scalar_tensor_tensor(hw[:, t % 2, :].rearrange("p (n r) -> p n r", n=NP),
                                       ps[:, t % 2, :].rearrange("p (n r) -> p n r", n=NP), UNS,
                                       wn[:, t, :].unsqueeze(2).to_broadcast([P, NP, RK]), ALU.mult,
                                       ALU.mult).then_inc(s_hw, 1)

            weighted(0)
            for t in range(8):
                if t + 1 < 8:
                    weighted(t + 1)
                dve.wait_ge(s_hhi, t + 1)
                wait(dve, s_fp, t - 1)
                V.scalar_tensor_tensor(hl[:, t % 2, :, :], ps[:, 4 + t % 2, :].rearrange("p (c n) -> p c n", c=DC), XS,
                                       hh[:, t % 2, :, :], ALU.mult, ALU.subtract).then_inc(s_hlo, 1)
                dve.wait_ge(s_fp, t + 1)
                V.scalar_tensor_tensor(x[:, t, :], ps[:, 2 + t % 2, :], UNS, x[:, t, :], ALU.mult, ALU.add).then_inc(s_fo, 1)


def kernel(x, ctx_1024, L0_xattn_w_q, L0_xattn_w_kv, L0_xattn_w_concat, L0_attn_W_in, L0_attn_dw_weight, L0_attn_dw_bias,
           L0_attn_W_bc, L0_attn_W_out, L0_attn_skip, L0_attn_A_log, L0_attn_dt_bias, L0_ffn_prototypes, L0_ffn_B,
           L0_ffn_A, L0_ffn_bias, L0_ffn_temp):
    import concourse.bacc as bacc
    from concourse.bass_utils import run_bass_kernel_spmd

    a = np.asarray

    def lay(v, split, order, shape):
        return np.ascontiguousarray(a(v).reshape(split).transpose(order).reshape(shape))

    w_in = a(L0_attn_W_in)
    wkv = a(L0_xattn_w_kv).reshape(P, DC, 2, DH)
    chunk = (-1, P, CH)
    arrays = {
        "x": a(x).reshape(8, P, D),
        "ctx": lay(ctx_1024, (B, NKEY, P, DC), (0, 2, 3, 1), (B, P, DC, NKEY)),
        "w": np.concatenate([
            lay(L0_xattn_w_q, (DC, P, D), (1, 0, 2), chunk),
            lay(L0_xattn_w_concat, (DC, P, D), (1, 0, 2), chunk),
            lay(w_in[DI:2 * DI], (2, 512, DC, P), (0, 3, 2, 1), chunk),
            lay(L0_attn_W_bc, (NG, 4, 2, 2, SN, VC, P), (0, 2, 6, 5, 3, 1, 4), chunk),
            lay(w_in[0:DI], (2, 512, DC, P), (0, 3, 2, 1), chunk),
            lay(L0_attn_W_out, (D, 2, 4, P), (1, 3, 2, 0), chunk),
            lay(L0_ffn_B, (NP * RK, DC, P), (2, 1, 0), chunk),
            lay(L0_ffn_A, (NP, D, RK), (0, 2, 1), (DC, P, D)).transpose(1, 0, 2).reshape(chunk)]),
        "wkv": np.ascontiguousarray(wkv.reshape(P, DC, 2 * DH)),
        "wp": lay(w_in[2 * DI:], (SH, 2, DC, P), (3, 2, 1, 0), (P, DC, 64)),
        "proto": a(L0_ffn_prototypes),
        "protot": lay(L0_ffn_prototypes, (NP, DC, P), (2, 1, 0), (P, DC, NP)),
        "bias": a(L0_ffn_bias),
        "conv": lay(L0_attn_dw_weight, (VC, P, 4), (1, 0, 2), (P, VC, 4)),
        "dwb": lay(L0_attn_dw_bias, (VC, P), (1, 0), (P, VC)),
        "skip": lay(L0_attn_skip, (VC, P), (1, 0), (P, VC)),
        "alog": a(L0_attn_A_log),
        "dtb": a(L0_attn_dt_bias).reshape(SH, 1),
        "temp": np.ascontiguousarray(np.broadcast_to(a(L0_ffn_temp).reshape(1, 1), (P, 1))),
    }
    nc = bacc.Bacc("TRN2", target_bir_lowering=False, num_devices=1)
    args = [nc.dram_tensor("in_" + k, v.shape, mybir.dt.from_np(v.dtype), kind="ExternalInput").ap() for k, v in arrays.items()]
    out = nc.dram_tensor("out_x", (8, P, D), F32, kind="ExternalOutput").ap()
    build(nc, *args, out)
    r = run_bass_kernel_spmd(nc, [{"in_" + k: v for k, v in arrays.items()}], core_ids=[0])
    return r.results[0]["out_x"].reshape(B, T, D)
```
